# Optimizing a Trainium2 kernel written in Bass

```python
import numpy as np
import jax
import jax.numpy as jnp

def _softmax(x, axis=-1):
    return jax.nn.softmax(x, axis=axis)

def _gelu(x):
    return jax.nn.gelu(x, approximate=True)

def _silu(x):
    return jax.nn.silu(x)

def _sigmoid(x):
    return jax.nn.sigmoid(x)

def _layernorm(x, axis=-1, eps=1e-05):
    m = jnp.mean(x, axis=axis, keepdims=True)
    v = jnp.var(x, axis=axis, keepdims=True)
    return (x - m) / jnp.sqrt(v + eps)

def _scatter_add(tgt, idx, src, axis=0):
    return tgt.at[idx].add(src)

def _segment_sum(src, seg, n):
    return jax.ops.segment_sum(src, seg, n)
kernel_name = 'mk_vit_tower_cls_d1_tok_img4096_r4_efc593'

def setup_inputs(seed: int=0):
    np.random.seed(seed)
    _w = jnp.asarray

    def _rec_inputs():
        import jax
        import jax.numpy as jnp
        _rk = jax.random.key(seed)
        x = -0.00348982 + 0.707501 * jax.random.normal(jax.random.fold_in(_rk, 1), (64, 128, 64, 2), jnp.float32)
        cls_tok = 0.02 * jax.random.normal(jax.random.fold_in(_rk, 5), (1, 1, 1024), jnp.float32)
        return (x, cls_tok)
    x, cls_tok = _rec_inputs()

    def _L0_tok_setup():
        import jax, jax.numpy as jnp
        import numpy as np
        H, N, S, CH, LEN = (128, 64, 128, 1, 1024)

        def _s4d_kernel(log_dt, C, B, inv_A_real, A_imag, L):
            dt = jnp.exp(log_dt)
            Cc = C[..., 0] + 1j * C[..., 1]
            Bc = B[..., 0] + 1j * B[..., 1]
            A = -jnp.exp(inv_A_real) + 1j * A_imag
            rep = H // A.shape[0]
            A = jnp.tile(A, (rep, 1))
            Bc = jnp.tile(Bc, (rep, 1))
            dtA = A * dt[:, None]
            Cc = Bc[None, :, :] * Cc
            Cc = Cc * (jnp.exp(dtA) - 1.0) / A
            ell = jnp.arange(L, dtype=jnp.float32)
            V = jnp.exp(dtA[:, :, None] * ell)
            K = 2.0 * jnp.einsum('chn,hnl->chl', Cc, V).real
            return K.astype(jnp.float32)
        key = jax.random.key(seed)
        k1, k2 = jax.random.split(key, 2)
        log_dt = jax.random.uniform(k1, (H,), minval=float(np.log(0.001)), maxval=float(np.log(0.1))).astype(jnp.float32)
        inv_A_real = jnp.full((S, N), float(np.log(0.5)), dtype=jnp.float32)
        A_imag = jnp.tile((np.pi * jnp.arange(N, dtype=jnp.float32))[None, :], (S, 1))
        B = jnp.stack([jnp.ones((S, N), jnp.float32), jnp.zeros((S, N), jnp.float32)], axis=-1)
        C = (jax.random.normal(k2, (CH, H, N, 2)) * 0.5 ** 0.5).astype(jnp.float32)
        return {'log_dt': log_dt, 'C': C, 'B': B, 'inv_A_real': inv_A_real, 'A_imag': A_imag, 'L': LEN}
    _L0_tok_all = _L0_tok_setup()
    _L0_tok_in = {k: v for k, v in _L0_tok_all.items() if k in ('log_dt', 'B', 'inv_A_real', 'A_imag')}
    del _L0_tok_all

    def _L0_attn_setup():
        import jax, jax.numpy as jnp
        import numpy as np
        HID = 1024
        DM = 128
        DIN = 2 * DM
        DST = 16
        HD = 64
        NH = DIN // HD
        DCONV = 7
        CONV_DIM = DIN + 2 * DST
        DIN_PROJ = 2 * DIN + 2 * DST + 2 * NH
        SEQ, BATCH = (512, 4)

        def _causal_conv(x, w, b):
            y = jax.lax.conv_general_dilated(jnp.transpose(x, (0, 2, 1)), w, (1,), [(DCONV - 1, 0)], feature_group_count=CONV_DIM, dimension_numbers=('NCH', 'OIH', 'NCH'))
            return jnp.transpose(y, (0, 2, 1)) + b

        def _ssm_scan(x, dt, A, B, C):
            dA = jnp.exp(dt * A)
            dBx = dt[..., None] * x

            def step(h, t):
                dA_t, dBx_t, B_t, C_t = t
                h = dA_t[:, :, None, None] * h + dBx_t[..., None] * B_t[:, None, None, :]
                y = jnp.einsum('bhpn,bn->bhp', h, C_t)
                return (h, y)
            h0 = jnp.zeros((x.shape[0], NH, HD, DST), x.dtype)
            _, ys = jax.lax.scan(step, h0, (jnp.moveaxis(dA, 1, 0), jnp.moveaxis(dBx, 1, 0), jnp.moveaxis(B, 1, 0), jnp.moveaxis(C, 1, 0)))
            return jnp.moveaxis(ys, 0, 1)

        def _hydra(u, in_w, conv_w, conv_b, dt_bias, A_log, D, fcD_w, norm_w, out_w):
            b, l, _ = u.shape
            zxbcdt = u @ in_w.T
            z = zxbcdt[..., :DIN]
            xBC = zxbcdt[..., DIN:DIN + CONV_DIM]
            dt2 = zxbcdt[..., DIN + CONV_DIM:]
            dt_fw = jax.nn.softplus(dt2[..., :NH] + dt_bias)
            dt_bw = jax.nn.softplus(jnp.flip(dt2[..., NH:], 1) + dt_bias)
            xBC = jax.nn.silu(_causal_conv(xBC, conv_w, conv_b))
            xs = xBC[..., :DIN]
            Bm = xBC[..., DIN:DIN + DST]
            Cm = xBC[..., DIN + DST:]
            A = -jnp.exp(A_log)
            x4 = xs.reshape(b, l, NH, HD)
            y_fw = _ssm_scan(x4, dt_fw, A, Bm, Cm).reshape(b, l, DIN)
            y_bw = jnp.flip(_ssm_scan(jnp.flip(x4, 1), dt_bw, A, jnp.flip(Bm, 1), jnp.flip(Cm, 1)).reshape(b, l, DIN), 1)
            zero = jnp.zeros((b, 1, DIN), u.dtype)
            y = jnp.concatenate([zero, y_fw[:, :-1]], 1) + jnp.concatenate([y_bw[:, 1:], zero], 1)
            y = y + xs * jnp.repeat(xs @ fcD_w.T + D, HD, axis=-1)
            yz = y * jax.nn.silu(z)
            y = yz * jax.lax.rsqrt(jnp.mean(jnp.square(yz), -1, keepdims=True) + 1e-05) * norm_w
            return y @ out_w.T
        key = jax.random.key(seed)
        ks = jax.random.split(key, 12)
        rn = lambda k, shape, s=0.02: jax.random.normal(k, shape, jnp.float32) * s
        dt = jnp.exp(jax.random.uniform(ks[5], (NH,), jnp.float32, np.log(0.001), np.log(0.1)))
        return dict(x=jax.random.normal(ks[0], (SEQ, BATCH, HID), jnp.float32), w_down=rn(ks[1], (DM, HID)), b_down=jnp.zeros((DM,), jnp.float32), w_up=rn(ks[2], (HID, DM)), b_up=jnp.zeros((HID,), jnp.float32), gate1=jnp.asarray(0.6, jnp.float32), hy_in_w=rn(ks[3], (DIN_PROJ, DM)), hy_conv_w=rn(ks[4], (CONV_DIM, 1, DCONV), 0.2), hy_conv_b=jnp.zeros((CONV_DIM,), jnp.float32), hy_dt_bias=jnp.log(jnp.expm1(dt)), hy_A_log=jnp.log(jax.random.uniform(ks[6], (NH,), jnp.float32, 1.0, 16.0)), hy_D=jnp.ones((NH,), jnp.float32), hy_fcD_w=rn(ks[7], (NH, DIN)), hy_norm_w=jnp.ones((DIN,), jnp.float32), hy_out_w=rn(ks[8], (DM, DIN)))
    _L0_attn_all = _L0_attn_setup()
    _L0_attn_in = {k: v for k, v in _L0_attn_all.items() if k in ('w_down', 'b_down', 'w_up', 'b_up', 'gate1', 'hy_in_w', 'hy_conv_w', 'hy_conv_b', 'hy_dt_bias', 'hy_A_log', 'hy_D', 'hy_fcD_w', 'hy_norm_w', 'hy_out_w')}
    del _L0_attn_all

    def _L0_ffn_setup():
        import jax, jax.numpy as jnp
        import numpy as np
        SCALING = 32.0 / 16.0
        key = jax.random.key(seed)
        ks = jax.random.split(key, 7)
        B, T, D, O, R, E = (4, 512, 1024, 1024, 16, 8)
        x = jax.random.normal(ks[0], (B, T, D), dtype=jnp.float32)
        base_W = jax.random.normal(ks[1], (O, D), dtype=jnp.float32) * D ** (-0.5)
        base_b = jax.random.normal(ks[2], (O,), dtype=jnp.float32) * 0.01
        router_W = jax.random.normal(ks[3], (2 * E - 1, D), dtype=jnp.float32) * D ** (-0.5)
        router_b = jax.random.normal(ks[4], (2 * E - 1,), dtype=jnp.float32) * 0.01
        A = jax.random.normal(ks[5], (E, R, D), dtype=jnp.float32) * D ** (-0.5)
        Bm = jax.random.normal(ks[6], (E, O, R), dtype=jnp.float32) * R ** (-0.5)
        assigned_idx = 0
        others = [i for i in range(E) if i != assigned_idx]
        expert_map = jnp.array([assigned_idx] * E + others, dtype=jnp.int32)
        return {'x': x, 'base_W': base_W, 'base_b': base_b, 'router_W': router_W, 'router_b': router_b, 'A': A, 'B': Bm, 'expert_map': expert_map}
    _L0_ffn_all = _L0_ffn_setup()
    _L0_ffn_in = {k: v for k, v in _L0_ffn_all.items() if k in ('base_W', 'base_b', 'router_W', 'router_b', 'A', 'B', 'expert_map')}
    del _L0_ffn_all
    return {'x': x, 'cls_tok': cls_tok, 'L0_tok_log_dt': _L0_tok_in['log_dt'], 'L0_tok_B': _L0_tok_in['B'], 'L0_tok_inv_A_real': _L0_tok_in['inv_A_real'], 'L0_tok_A_imag': _L0_tok_in['A_imag'], 'L0_attn_w_down': _L0_attn_in['w_down'], 'L0_attn_b_down': _L0_attn_in['b_down'], 'L0_attn_w_up': _L0_attn_in['w_up'], 'L0_attn_b_up': _L0_attn_in['b_up'], 'L0_attn_gate1': _L0_attn_in['gate1'], 'L0_attn_hy_in_w': _L0_attn_in['hy_in_w'], 'L0_attn_hy_conv_w': _L0_attn_in['hy_conv_w'], 'L0_attn_hy_conv_b': _L0_attn_in['hy_conv_b'], 'L0_attn_hy_dt_bias': _L0_attn_in['hy_dt_bias'], 'L0_attn_hy_A_log': _L0_attn_in['hy_A_log'], 'L0_attn_hy_D': _L0_attn_in['hy_D'], 'L0_attn_hy_fcD_w': _L0_attn_in['hy_fcD_w'], 'L0_attn_hy_norm_w': _L0_attn_in['hy_norm_w'], 'L0_attn_hy_out_w': _L0_attn_in['hy_out_w'], 'L0_ffn_base_W': _L0_ffn_in['base_W'], 'L0_ffn_base_b': _L0_ffn_in['base_b'], 'L0_ffn_router_W': _L0_ffn_in['router_W'], 'L0_ffn_router_b': _L0_ffn_in['router_b'], 'L0_ffn_A': _L0_ffn_in['A'], 'L0_ffn_B': _L0_ffn_in['B'], 'L0_ffn_expert_map': _L0_ffn_in['expert_map']}

def reference(x, cls_tok, L0_tok_log_dt, L0_tok_B, L0_tok_inv_A_real, L0_tok_A_imag, L0_attn_w_down, L0_attn_b_down, L0_attn_w_up, L0_attn_b_up, L0_attn_gate1, L0_attn_hy_in_w, L0_attn_hy_conv_w, L0_attn_hy_conv_b, L0_attn_hy_dt_bias, L0_attn_hy_A_log, L0_attn_hy_D, L0_attn_hy_fcD_w, L0_attn_hy_norm_w, L0_attn_hy_out_w, L0_ffn_base_W, L0_ffn_base_b, L0_ffn_router_W, L0_ffn_router_b, L0_ffn_A, L0_ffn_B, L0_ffn_expert_map):
    import jax
    import jax.numpy as jnp

    def _L0_tok_ref(log_dt, C, B, inv_A_real, A_imag, L):
        import jax, jax.numpy as jnp
        import numpy as np
        H, N, S, CH, LEN = (128, 64, 128, 1, 1024)

        def _s4d_kernel(log_dt, C, B, inv_A_real, A_imag, L):
            dt = jnp.exp(log_dt)
            Cc = C[..., 0] + 1j * C[..., 1]
            Bc = B[..., 0] + 1j * B[..., 1]
            A = -jnp.exp(inv_A_real) + 1j * A_imag
            rep = H // A.shape[0]
            A = jnp.tile(A, (rep, 1))
            Bc = jnp.tile(Bc, (rep, 1))
            dtA = A * dt[:, None]
            Cc = Bc[None, :, :] * Cc
            Cc = Cc * (jnp.exp(dtA) - 1.0) / A
            ell = jnp.arange(L, dtype=jnp.float32)
            V = jnp.exp(dtA[:, :, None] * ell)
            K = 2.0 * jnp.einsum('chn,hnl->chl', Cc, V).real
            return K.astype(jnp.float32)
        return _s4d_kernel(log_dt, C, B, inv_A_real, A_imag, L)

    def _L0_attn_ref(x, w_down, b_down, w_up, b_up, gate1, hy_in_w, hy_conv_w, hy_conv_b, hy_dt_bias, hy_A_log, hy_D, hy_fcD_w, hy_norm_w, hy_out_w):
        import jax, jax.numpy as jnp
        import numpy as np
        HID = 1024
        DM = 128
        DIN = 2 * DM
        DST = 16
        HD = 64
        NH = DIN // HD
        DCONV = 7
        CONV_DIM = DIN + 2 * DST
        DIN_PROJ = 2 * DIN + 2 * DST + 2 * NH
        SEQ, BATCH = (512, 4)

        def _causal_conv(x, w, b):
            y = jax.lax.conv_general_dilated(jnp.transpose(x, (0, 2, 1)), w, (1,), [(DCONV - 1, 0)], feature_group_count=CONV_DIM, dimension_numbers=('NCH', 'OIH', 'NCH'))
            return jnp.transpose(y, (0, 2, 1)) + b

        def _ssm_scan(x, dt, A, B, C):
            dA = jnp.exp(dt * A)
            dBx = dt[..., None] * x

            def step(h, t):
                dA_t, dBx_t, B_t, C_t = t
                h = dA_t[:, :, None, None] * h + dBx_t[..., None] * B_t[:, None, None, :]
                y = jnp.einsum('bhpn,bn->bhp', h, C_t)
                return (h, y)
            h0 = jnp.zeros((x.shape[0], NH, HD, DST), x.dtype)
            _, ys = jax.lax.scan(step, h0, (jnp.moveaxis(dA, 1, 0), jnp.moveaxis(dBx, 1, 0), jnp.moveaxis(B, 1, 0), jnp.moveaxis(C, 1, 0)))
            return jnp.moveaxis(ys, 0, 1)

        def _hydra(u, in_w, conv_w, conv_b, dt_bias, A_log, D, fcD_w, norm_w, out_w):
            b, l, _ = u.shape
            zxbcdt = u @ in_w.T
            z = zxbcdt[..., :DIN]
            xBC = zxbcdt[..., DIN:DIN + CONV_DIM]
            dt2 = zxbcdt[..., DIN + CONV_DIM:]
            dt_fw = jax.nn.softplus(dt2[..., :NH] + dt_bias)
            dt_bw = jax.nn.softplus(jnp.flip(dt2[..., NH:], 1) + dt_bias)
            xBC = jax.nn.silu(_causal_conv(xBC, conv_w, conv_b))
            xs = xBC[..., :DIN]
            Bm = xBC[..., DIN:DIN + DST]
            Cm = xBC[..., DIN + DST:]
            A = -jnp.exp(A_log)
            x4 = xs.reshape(b, l, NH, HD)
            y_fw = _ssm_scan(x4, dt_fw, A, Bm, Cm).reshape(b, l, DIN)
            y_bw = jnp.flip(_ssm_scan(jnp.flip(x4, 1), dt_bw, A, jnp.flip(Bm, 1), jnp.flip(Cm, 1)).reshape(b, l, DIN), 1)
            zero = jnp.zeros((b, 1, DIN), u.dtype)
            y = jnp.concatenate([zero, y_fw[:, :-1]], 1) + jnp.concatenate([y_bw[:, 1:], zero], 1)
            y = y + xs * jnp.repeat(xs @ fcD_w.T + D, HD, axis=-1)
            yz = y * jax.nn.silu(z)
            y = yz * jax.lax.rsqrt(jnp.mean(jnp.square(yz), -1, keepdims=True) + 1e-05) * norm_w
            return y @ out_w.T
        x_init = x
        h = x @ w_down.T + b_down
        h = jnp.transpose(h, (1, 0, 2))
        h = jax.nn.gelu(h, approximate=False)
        xmid = h
        hp = (hy_in_w, hy_conv_w, hy_conv_b, hy_dt_bias, hy_A_log, hy_D, hy_fcD_w, hy_norm_w, hy_out_w)
        h = _hydra(h, *hp)
        h = _hydra(h, *hp)
        alpha = jax.nn.sigmoid(gate1)
        h = alpha * xmid + (1.0 - alpha) * h
        h = xmid + h
        h = h @ w_up.T + b_up
        return x_init + jnp.transpose(h, (1, 0, 2))

    def _L0_ffn_ref(x, base_W, base_b, router_W, router_b, A, B, expert_map):
        import jax, jax.numpy as jnp
        import numpy as np
        SCALING = 32.0 / 16.0
        E = A.shape[0]
        base_out = jnp.einsum('btd,od->bto', x, base_W) + base_b
        logits = jnp.einsum('btd,nd->btn', x, router_W) + router_b
        probs = jax.nn.softmax(logits, axis=-1)
        topk_p, topk_i = jax.lax.top_k(probs, E)
        mapped = expert_map[topk_i]
        onehot = (mapped[..., None] == jnp.arange(E)).astype(x.dtype)
        w = jnp.einsum('btk,btke->bte', topk_p, onehot)
        h = jnp.einsum('btd,erd->bter', x, A)
        lora = jnp.einsum('bter,eor->bto', h * w[..., None], B) * SCALING
        return base_out + lora
    h = _L0_tok_ref(L0_tok_log_dt, x, L0_tok_B, L0_tok_inv_A_real, L0_tok_A_imag, 1024)
    h = jnp.concatenate([jnp.broadcast_to(cls_tok, (h.shape[0], 1, h.shape[2])), h], axis=1)
    h = h + _L0_attn_ref(_layernorm(h, axis=-1), L0_attn_w_down, L0_attn_b_down, L0_attn_w_up, L0_attn_b_up, L0_attn_gate1, L0_attn_hy_in_w, L0_attn_hy_conv_w, L0_attn_hy_conv_b, L0_attn_hy_dt_bias, L0_attn_hy_A_log, L0_attn_hy_D, L0_attn_hy_fcD_w, L0_attn_hy_norm_w, L0_attn_hy_out_w)
    h = h + _L0_ffn_ref(_layernorm(h, axis=-1), L0_ffn_base_W, L0_ffn_base_b, L0_ffn_router_W, L0_ffn_router_b, L0_ffn_A, L0_ffn_B, L0_ffn_expert_map)
    return h

_drawn_inputs = setup_inputs


def setup_inputs(seed=0):
    import zlib

    import numpy as np

    out = dict(_drawn_inputs(seed))
    spreads = {'L0_tok_inv_A_real': (-0.6931471824645996, 0.2),
     'L0_attn_b_down': (0.0, 0.285),
     'L0_attn_b_up': (0.0, 0.1),
     'L0_attn_hy_conv_b': (0.0, 0.669),
     'L0_attn_hy_D': (1.0, 0.6),
     'L0_attn_hy_norm_w': (1.0, 0.6)}
    factors = {'L0_attn_hy_in_w': 4.988,
     'L0_attn_hy_conv_w': 8.0,
     'L0_attn_hy_dt_bias': 8.0,
     'L0_attn_hy_A_log': 8.0,
     'L0_attn_hy_fcD_w': 8.0,
     'L0_attn_hy_out_w': 5.183,
     'L0_ffn_base_b': 8.0,
     'L0_ffn_router_b': 7.275}
    for name, (base, spread) in spreads.items():
        noise = np.random.default_rng([zlib.crc32(name.encode()), seed]).standard_normal(out[name].shape)
        drawn = base * np.exp(spread * noise) if base else spread * noise
        out[name] = jnp.asarray(drawn.astype(out[name].dtype))
    for name, factor in factors.items():
        out[name] = (out[name] * factor).astype(out[name].dtype)
    return out
```

```python
from contextlib import ExitStack

import numpy as np

import concourse.bass as bass
from concourse import mybir

F32 = mybir.dt.float32
F32R = mybir.dt.float32r
I32 = mybir.dt.int32
ALU = mybir.AluOpType
ACT = mybir.ActivationFunctionType
AX = mybir.AxisListType

P = 128
PI = float(np.pi)
EPS = 1e-5
ROUND = float(1.5 * 2 ** 23)


class Step:

    def __init__(self, sem, per, unit=1):
        self.sem, self.per, self.unit = sem, per, unit

    def after(self, eng, n, j=None):
        if isinstance(n, int) and n < 0:
            return
        j = self.per if j is None else j
        eng.wait_ge(self.sem, (n * self.per + j) * self.unit)


def build(nc, x, cls_tok, log_dt, tok_B, inv_A_real, A_imag, w_down, b_down, w_up, b_up, gate1, in_w,
          conv_w, conv_b, dt_bias, A_log, hy_D, fcD_w, norm_w, out_w, base_W, base_b, router_W, router_b,
          lora_A, lora_B, expert_map, out, pairs=64):
    CS, NHT, NST, _ = x.shape
    DM, HID = w_down.shape
    KC = HID // P
    DIN = out_w.shape[1]
    NH = A_log.shape[0]
    HD = DIN // NH
    DST = (conv_w.shape[0] - DIN) // 2
    TAPS = conv_w.shape[2]
    NE, RK, _ = lora_A.shape
    NR = router_W.shape[0]
    FW = HID + P + NR + 1
    HALF = HID // 2
    BCP = 48
    TILES = pairs + 1
    CLS = pairs

    with ExitStack() as keep:
        def sb(name, shape, dt=F32, ctx=None):
            return (ctx or keep).enter_context(nc.sbuf_tensor(name, shape, dt))

        def sem(name):
            return keep.enter_context(nc.semaphore(name))

        w_hi = sb("w_hi", [P, KC, FW], F32R)
        w_lo = sb("w_lo", [P, KC, FW], F32R)
        wdT = sb("wdT", [P, KC, DM])
        wuT = sb("wuT", [P, HID])
        lbT = sb("lbT", [P, HID])
        wx = sb("wx", [P, DIN])
        wbc = sb("wbc", [P, BCP + 2 * NH])
        wz = sb("wz", [P, DIN])
        fcT = sb("fcT", [P, 2, NH])
        owT = sb("owT", [P, 2, DM])
        ident = sb("ident", [P, P])
        earlier = sb("earlier", [P, P])
        later = sb("later", [P, P])
        m_lt = sb("m_lt", [P, CS])
        m_gt = sb("m_gt", [P, CS])
        bup = sb("bup", [P, HID])
        bbase = sb("bbase", [P, HID])
        rbias = sb("rbias", [P, NR])
        onehot = sb("onehot", [P, NE, NR])
        dtb = sb("dtb", [P, NH])
        negA = sb("negA", [P, NH])
        Dbc = sb("Dbc", [P, NH])
        bdn = sb("bdn", [P, 1])
        al1 = sb("al1", [P, 1])
        be1 = sb("be1", [P, 1])
        cw = sb("cw", [P, 2, TAPS])
        cb = sb("cb", [P, 2])
        cwb = sb("cwb", [BCP, TAPS])
        cbb = sb("cbb", [BCP, 1])
        half_neg = sb("half_neg", [P, 2])
        TP, TQ, TJR, TJI = (slice(16 * k, 16 * k + 16) for k in range(4))
        TSR, TSI, NTAB = slice(64, 67), slice(67, 70), 70
        tables = nc.dram_tensor("tables", (NHT // 2, P, 2, NTAB), F32, kind="Internal").ap()
        T = sb("T", [P, 2, HID])
        HB = sb("HB", [P, 2, HID])
        Mt = sb("Mt", [P, 2, NH, P])
        GF = sb("GF", [P, 2, CS])
        GB = sb("GB", [P, 2, CS])
        U = sb("U", [P, 2, 2, P])
        banks = [keep.enter_context(nc.psum_tensor(f"bank{i}", [P, 512], F32)) for i in range(8)]

        with ExitStack() as tmp:
            def ts(name, shape, dt=F32):
                return sb(name, shape, dt, tmp)

            stage = [T[:, 0, :], T[:, 1, :], HB[:, 0, :], HB[:, 1, :], ts("st4", [P, HID])[:, :], ts("st5", [P, HID])[:, :]]
            NS = len(stage)
            inw_s = ts("inw_s", [P, 4, P])
            bc_s = ts("bc_s", [P, P])
            dt_s = ts("dt_s", [2 * NH, P])
            fc_s = ts("fc_s", [NH, DIN])
            ow_s = ts("ow_s", [P, DIN])
            nw = ts("nw", [P, 2])
            alog = ts("alog", [P, NH])
            gate = ts("gate", [P, 1])
            gt0 = ts("gt0", [P, 1])
            emap = ts("emap", [P, NR], I32)
            emf = ts("emf", [P, NR])
            cw0 = ts("cw0", [P, 2, TAPS])
            cb0 = ts("cb0", [P, 2])
            cwb0 = ts("cwb0", [BCP, TAPS])
            cbb0 = ts("cbb0", [BCP, 1])
            ones = ts("ones", [P, P])
            evm = ts("evm", [P, NST])
            ai_s = ts("ai_s", [P, NST])
            ar_s = ts("ar_s", [P, NST])
            b_s = ts("b_s", [P, NST, 2])
            dup = ts("dup", [P, 4, NST, 2])
            par = ts("par", [P, 4, NHT])
            ldt = ts("ldt", [P, NHT])
            lst = ts("lst", [P, 35])
            lst_i = ts("lst_i", [P, 35], I32)
            v = {n: ts("v_" + n, [P, NHT]) for n in
                 ("dt", "ar", "sg", "om", "t0", "t1", "t2", "t3", "t4", "er", "ei", "co", "Gr", "Gi", "al", "be")}
            evc = ts("evc", [P, 1])
            odc = ts("odc", [P, 1])
            sgn = ts("sgn", [P, 1])
            HCH = 16
            tab = ts("tab", [P, HCH, NTAB])
            big = {n: ts("g_" + n, [P, HCH, 35]) for n in ("arg", "k", "r", "s", "c", "e")}

            pieces = [("w", o) for o in range(KC)] + [("A", 0), ("r", 0), ("d", 0), ("u", 0), ("b", 0)]

            def tsem(name):
                return tmp.enter_context(nc.semaphore(name))

            s_ld = [tsem(f"s_ld{i}") for i in range(NS)]
            s_small, s_wt, s_hi, s_lo = tsem("s_small"), tsem("s_wt"), tsem("s_hi"), tsem("s_lo")
            s_pool, s_dve, s_act = tsem("s_pool"), tsem("s_dve"), tsem("s_act")
            s_zero, s_masks, s_consts = tsem("s_zero"), tsem("s_masks"), tsem("s_consts")
            s_dup, s_par, s_tdt, s_exps = tsem("s_dup"), tsem("s_par"), tsem("s_tdt"), tsem("s_exps")
            s_sg, s_om, s_trig = tsem("s_sg"), tsem("s_om"), tsem("s_trig")
            s_tab = tsem("s_tab")
            s_red, s_dec, s_sin, s_exp, s_kept = tsem("s_red"), tsem("s_dec"), tsem("s_sin"), tsem("s_exp"), tsem("s_kept")
            loaded, count = [], [0] * NS
            for n, (kind, _) in enumerate(pieces):
                count[n % NS] += 16 * (NE if kind == "b" else 1)
                loaded.append(count[n % NS])

            jobs = [([inw_s[:, 2, :], inw_s[:, 3, :]], P, wx[:, :].rearrange("p (a b) -> p a b", a=2), None, 1.0, -1),
                    ([inw_s[:, 0, :], inw_s[:, 1, :]], P, wz[:, :].rearrange("p (a b) -> p a b", a=2), None, 0.5, -1),
                    ([bc_s[0:BCP, :]], BCP, wbc[:, 0:BCP].unsqueeze(1), None, 1.0, -1),
                    ([dt_s[:, :]], 2 * NH, wbc[:, BCP:BCP + 2 * NH].unsqueeze(1), None, 1.0, -1),
                    ([fc_s[:, 0:P], fc_s[:, P:DIN]], NH, fcT[:, :, :], None, 1.0, -1),
                    ([ow_s[:, 0:P]], P, owT[:, 0:1, :], None, nw[:, 0:1], -1),
                    ([ow_s[:, P:DIN]], P, owT[:, 1:2, :], None, nw[:, 1:2], -1)]
            for n, (kind, o) in enumerate(pieces):
                rows = NR if kind == "r" else P
                for g in range(2):
                    ks = slice(4 * g, 4 * g + 4)
                    src = [stage[n % NS][0:rows, (4 * g + k) * P:(4 * g + k + 1) * P] for k in range(4)]
                    if kind in "wAr":
                        at = {"w": o * P, "A": HID, "r": HID + P}[kind]
                        jobs.append((src, rows, w_hi[:, ks, at:at + rows], w_lo[:, ks, at:at + rows], 1.0, n))
                    else:
                        dst = wdT[:, ks, :] if kind == "d" else \
                            (wuT if kind == "u" else lbT)[:, 512 * g:512 * g + 512].rearrange("p (a b) -> p a b", a=4)
                        jobs.append((src, rows, dst, None, 2.0 if kind == "b" else 1.0, n))
            splits = np.cumsum([j[3] is not None for j in jobs]).tolist()
            last_job = {j[5]: k for k, j in enumerate(jobs)}
            RING, SMALL_JOBS, PER_CHUNK = 4, 7, 2
            NSMALL = 29

            block = tmp.enter_context(nc.Block())

            @block.sync
            def _(sp):
                def small(dst, src):
                    sp.dma_start(dst, src).then_inc(s_small, 16)

                small(ai_s[:, :], A_imag)
                small(ar_s[:, :], inv_A_real)
                small(b_s[:, :, :], tok_B)
                small(ldt[:, :], log_dt.unsqueeze(0).broadcast_to([P, NHT]))
                small(inw_s[:, :, :], in_w[0:4 * P, :].rearrange("(a p) d -> p a d", p=P))
                small(dt_s[:, :], in_w[2 * DIN + 2 * DST:2 * DIN + 2 * DST + 2 * NH, :])
                small(fc_s[:, :], fcD_w)
                small(ow_s[:, :], out_w)
                small(nw[:, 0:1], norm_w[0:P].unsqueeze(1))
                small(nw[:, 1:2], norm_w[P:DIN].unsqueeze(1))
                cwr = conv_w.rearrange("c a k -> c (a k)")
                for c in range(2):
                    small(cw0[:, c, :], cwr[c * P:(c + 1) * P, :])
                    small(cb0[:, c:c + 1], conv_b[c * P:(c + 1) * P].unsqueeze(1))
                small(bup[:, :], b_up.unsqueeze(0).broadcast_to([P, HID]))
                small(bbase[:, :], base_b.unsqueeze(0).broadcast_to([P, HID]))
                small(rbias[:, :], router_b.unsqueeze(0).broadcast_to([P, NR]))
                small(emap[:, :], expert_map.unsqueeze(0).broadcast_to([P, NR]))
                small(dtb[:, :], dt_bias.unsqueeze(0).broadcast_to([P, NH]))
                small(alog[:, :], A_log.unsqueeze(0).broadcast_to([P, NH]))
                small(Dbc[:, :], hy_D.unsqueeze(0).broadcast_to([P, NH]))
                small(bdn[:, :], b_down.unsqueeze(1))
                small(gate[:, :], gate1.broadcast_to([P, 1]))
                sp.wait_ge(s_zero, 3)
                for k in range(2):
                    small(bc_s[32 * k:32 * k + DST, :], in_w[2 * DIN + DST * k:2 * DIN + DST * (k + 1), :])
                    small(cwb0[32 * k:32 * k + DST, :], cwr[DIN + DST * k:DIN + DST * (k + 1), :])
                    small(cbb0[32 * k:32 * k + DST, :], conv_b[DIN + DST * k:DIN + DST * (k + 1)].unsqueeze(1))

                for c in range(NHT // HCH):
                    sp.wait_ge(s_tab, c + 1)
                    sp.dma_start(tables[c * HCH // 2:(c + 1) * HCH // 2].rearrange("t f b k -> f t b k"),
                                 tab[:, :, :].rearrange("f (t b) k -> f t b k", b=2)).then_inc(s_kept, 16)
                sp.wait_ge(s_kept, 16 * (NHT // HCH))

            @block.gpsimd
            def _(pool):
                pool.memset(bc_s[:, :], 0.0).then_inc(s_zero, 1)
                pool.memset(cwb0[:, :], 0.0).then_inc(s_zero, 1)
                pool.memset(cbb0[:, :], 0.0).then_inc(s_zero, 1)
                pool.memset(ones[:, :], 1.0).then_inc(s_pool, 1)
                for t in (ident, earlier, later):
                    pool.memset(t[:, :], 0.0).then_inc(s_pool, 1)
                pool.wait_ge(s_pool, 4)
                pool.affine_select(out=ident[:, :], in_=ident[:, :], compare_op=ALU.not_equal, fill=1.0,
                                   base=0, pattern=[[-1, P]], channel_multiplier=1).then_inc(s_masks, 1)
                for b in range(2):
                    r = slice(CS * b, CS * (b + 1))
                    pool.wait_ge(s_masks, 1 + 4 * b)
                    for dst, cols, sign in ((earlier, r, 1), (later, r, -1), (m_gt, slice(0, CS), 1),
                                            (m_lt, slice(0, CS), -1)):
                        pool.affine_select(out=dst[r, cols], in_=ones[r, 0:CS], compare_op=ALU.is_gt, fill=0.0,
                                           base=0, pattern=[[-sign, CS]], channel_multiplier=sign).then_inc(s_masks, 1)
                pool.wait_ge(s_masks, 9)
                pool.affine_select(out=evm[:, :], in_=ones[:, 0:NST], compare_op=ALU.is_equal, fill=0.0,
                                   base=0, pattern=[[-2, NST]], channel_multiplier=1).then_inc(s_consts, 1)
                pool.iota(lst_i[:, 0:16], pattern=[[1, 16]], base=0, channel_multiplier=0).then_inc(s_consts, 1)
                pool.iota(lst_i[:, 16:32], pattern=[[16, 16]], base=0, channel_multiplier=0).then_inc(s_consts, 1)
                for k, s in enumerate((512, 256, 768)):
                    pool.iota(lst_i[:, 32 + k:33 + k], pattern=[[1, 1]], base=s,
                              channel_multiplier=0).then_inc(s_consts, 1)
                pool.memset(half_neg[:, :], -0.5)
                pool.memset(Mt[:, :, :, :], 0.0)
                pool.memset(GF[:, :, :], 0.0)
                pool.memset(GB[:, :, :], 0.0)
                pool.memset(U[:, :, :, :], 0.0)

            @block.tensor
            def _(pe):
                pe.wait_ge(s_masks, 1)
                pe.wait_ge(s_dup, 4)
                for k in range(4):
                    ins = pe.transpose(banks[7][:, k * P:(k + 1) * P], dup[:, k, :, :].rearrange("p a b -> p (a b)"),
                                       ident[:, :])
                ins.then_inc(s_par, 1)
                pe.wait_ge(s_small, 16 * NSMALL)
                for k, (src, m, _, lo, _, n) in enumerate(jobs):
                    if n >= 0:
                        pe.wait_ge(s_ld[n % NS], loaded[n])
                    if k >= RING:
                        pe.wait_ge(s_hi, k - RING + 1)
                        if splits[k - RING]:
                            pe.wait_ge(s_lo, splits[k - RING])
                    for c, a in enumerate(src):
                        ins = pe.transpose(banks[k % RING][:, c * m:(c + 1) * m], a, ident[0:m, 0:m])
                    ins.then_inc(s_wt, 1)

            @block.scalar
            def _(act):
                dram = {"w": lambda o: base_W[o * P:(o + 1) * P, :],
                        "A": lambda o: lora_A.rearrange("e r d -> (e r) d"),
                        "r": lambda o: router_W, "d": lambda o: w_down,
                        "u": lambda o: w_up.rearrange("(a p) d -> p a d", p=P)}

                def load(n):
                    kind, o = pieces[n]
                    st = stage[n % NS]
                    if n >= NS:
                        act.wait_ge(s_wt, last_job[n - NS] + 1)
                    if kind == "b":
                        st4 = st.rearrange("p (a e r) -> p a e r", a=KC, e=NE)
                        for e in range(NE):
                            act.dma_start(st4[:, :, e, :],
                                          lora_B[e].rearrange("(a p) r -> p a r", p=P)).then_inc(s_ld[n % NS], 16)
                        return
                    dst = st[0:NR, :] if kind == "r" else st
                    if kind == "u":
                        dst = st.rearrange("p (a d) -> p a d", a=KC)
                    act.dma_start(dst, dram[kind](o)).then_inc(s_ld[n % NS], 16)

                for n in range(NS):
                    load(n)
                act.wait_ge(s_small, 16 * NSMALL)
                act.activation(v["t0"][:, :], ldt[:, :], ACT.Tanh, scale=1.0 / 16).then_inc(s_tdt, 1)
                act.wait_ge(s_par, 1)
                act.activation(v["t1"][:, :], banks[7][:, P:2 * P], ACT.Exp).then_inc(s_exps, 1)
                act.activation(alog[:, :], alog[:, :], ACT.Exp).then_inc(s_exps, 1)
                act.activation(gt0[:, :], gate[:, :], ACT.Exp, scale=-1.0).then_inc(s_exps, 1)
                act.wait_ge(s_sg, 1)
                act.activation(v["t0"][:, :], v["sg"][:, :], ACT.Tanh, scale=0.5).then_inc(s_trig, 1)
                act.wait_ge(s_om, 1)
                act.activation(v["t2"][:, :], v["om"][:, :], ACT.Sin).then_inc(s_trig, 1)
                act.activation(v["t3"][:, :], v["om"][:, :], ACT.Sin, scale=0.5).then_inc(s_trig, 1)
                nxt, k = NS, 0

                def evacuate(k, nxt):
                    src, m, dst, lo, scale, n = jobs[k]
                    act.wait_ge(s_wt, k + 1)
                    cols = banks[k % RING][:, 0:len(src) * m].rearrange("p (a b) -> p a b", b=m)
                    act.activation(dst, cols, ACT.Copy, scale=scale).then_inc(s_hi, 1)
                    if n >= 0 and last_job[n] == k and nxt < len(pieces):
                        load(nxt)
                        nxt += 1
                    return nxt

                while k < SMALL_JOBS:
                    nxt = evacuate(k, nxt)
                    k += 1
                for c in range(NHT // HCH):
                    for _ in range(PER_CHUNK):
                        nxt = evacuate(k, nxt)
                        k += 1
                    act.wait_ge(s_red, c + 1)
                    act.activation(big["s"][:, :, :], big["r"][:, :, :], ACT.Sin).then_inc(s_sin, 1)
                    act.activation(big["c"][:, :, :], big["r"][:, :, :], ACT.Sin, scale=0.5).then_inc(s_sin, 1)
                    act.wait_ge(s_dec, c + 1)
                    act.activation(big["e"][:, :, :], big["arg"][:, :, :], ACT.Exp).then_inc(s_exp, 1)
                while k < len(jobs):
                    nxt = evacuate(k, nxt)
                    k += 1

            @block.vector
            def _(dve):
                cnt = [0]

                def link(ins):
                    cnt[0] += 1
                    ins.then_inc(s_dve, 1)
                    dve.wait_ge(s_dve, cnt[0])

                TT, TS, STT = dve.tensor_tensor, dve.tensor_scalar, dve.scalar_tensor_tensor
                V = {n: t[:, :] for n, t in v.items()}
                dve.wait_ge(s_small, 16 * NSMALL)
                for k, src in enumerate((ai_s[:, :], ar_s[:, :], b_s[:, :, 0], b_s[:, :, 1])):
                    dve.tensor_copy(dup[:, k, :, :], src.unsqueeze(2).broadcast_to([P, NST, 2])).then_inc(s_dup, 1)
                dve.wait_ge(s_consts, 6)
                link(dve.tensor_copy(lst[:, :], lst_i[:, :]))
                link(dve.tensor_reduce(evc[:, :], evm[:, :], AX.X, ALU.add))
                link(TS(odc[:, :], evc[:, :], -1.0, 1.0, ALU.mult, ALU.add))
                link(TT(sgn[:, :], odc[:, :], evc[:, :], ALU.subtract))
                dve.wait_ge(s_tdt, 1)
                link(TS(V["t2"], V["t0"], -1.0, 1.0, ALU.mult, ALU.add))
                link(dve.reciprocal(V["t3"], V["t2"]))
                link(STT(V["dt"], V["t0"], 1.0, V["t3"], ALU.add, ALU.mult))
                for _ in range(3):
                    link(TT(V["dt"], V["dt"], V["dt"], ALU.mult))
                dve.wait_ge(s_exps, 1)
                link(dve.tensor_copy(par[:, :, :], banks[7][:, :].rearrange("p (a b) -> p a b", a=4)))
                link(TS(V["ar"], V["t1"], -1.0, None, ALU.mult))
                TT(V["sg"], V["ar"], V["dt"], ALU.mult).then_inc(s_sg, 1)

                def reduce(arg, k, r):
                    c1 = 6.28125
                    c2 = float(np.floor((2 * np.pi - c1) * 2.0 ** 20) * 2.0 ** -20)
                    c3 = float(2 * np.pi - c1 - c2)
                    link(TS(k, arg, 0.5 / PI, ROUND, ALU.mult, ALU.add))
                    link(TS(k, k, ROUND, None, ALU.subtract))
                    link(STT(r, k, -c1, arg, ALU.mult, ALU.add))
                    link(STT(r, k, -c2, r, ALU.mult, ALU.add))
                    link(STT(r, k, -c3, r, ALU.mult, ALU.add))
                    return TS(r, r, 3.1415925, -3.1415925, ALU.min, ALU.max)

                ai, br, bi = par[:, 0, :], par[:, 2, :], par[:, 3, :]
                link(TT(V["t4"], ai, V["dt"], ALU.mult))
                reduce(V["t4"], V["er"], V["om"]).then_inc(s_om, 1)
                dve.wait_ge(s_trig, 3)
                link(TS(V["t1"], V["t0"], -1.0, 1.0, ALU.mult, ALU.add))
                link(dve.reciprocal(V["co"], V["t1"]))
                link(STT(V["t0"], V["t0"], 2.0, V["co"], ALU.mult, ALU.mult))
                link(TT(V["t3"], V["t3"], V["t3"], ALU.mult))
                link(TS(V["t3"], V["t3"], -2.0, None, ALU.mult))
                link(TS(V["co"], V["t3"], 1.0, None, ALU.add))
                link(TT(V["er"], V["t0"], V["co"], ALU.mult))
                link(TT(V["er"], V["er"], V["t3"], ALU.add))
                link(STT(V["ei"], V["t0"], 1.0, V["t2"], ALU.add, ALU.mult))
                link(TT(V["t1"], V["ar"], V["ar"], ALU.mult))
                link(TT(V["t0"], ai, ai, ALU.mult))
                link(TT(V["t1"], V["t1"], V["t0"], ALU.add))
                link(dve.reciprocal(V["t0"], V["t1"]))
                link(TT(V["t1"], V["er"], V["ar"], ALU.mult))
                link(TT(V["t2"], V["ei"], ai, ALU.mult))
                link(TT(V["t1"], V["t1"], V["t2"], ALU.add))
                link(TT(V["t2"], V["ei"], V["ar"], ALU.mult))
                link(TT(V["t3"], V["er"], ai, ALU.mult))
                link(TT(V["t2"], V["t2"], V["t3"], ALU.subtract))
                link(TT(V["t1"], V["t1"], V["t0"], ALU.mult))
                link(TT(V["t2"], V["t2"], V["t0"], ALU.mult))
                link(TT(V["t0"], bi, V["t2"], ALU.mult))
                link(TT(V["Gr"], br, V["t1"], ALU.mult))
                link(TT(V["Gr"], V["Gr"], V["t0"], ALU.subtract))
                link(TT(V["t0"], bi, V["t1"], ALU.mult))
                link(TT(V["Gi"], br, V["t2"], ALU.mult))
                link(TT(V["Gi"], V["Gi"], V["t0"], ALU.add))
                link(TS(V["t0"], V["Gi"], odc[:, 0:1], -2.0, ALU.mult, ALU.mult))
                link(TS(V["al"], V["Gr"], evc[:, 0:1], 2.0, ALU.mult, ALU.mult))
                link(TT(V["al"], V["al"], V["t0"], ALU.add))
                link(TS(V["t0"], V["Gi"], evc[:, 0:1], -2.0, ALU.mult, ALU.mult))
                link(TS(V["be"], V["Gr"], odc[:, 0:1], -2.0, ALU.mult, ALU.mult))
                link(TT(V["be"], V["be"], V["t0"], ALU.add))
                nlo = [0]

                def second_parts(n):
                    for k, (src, m, dst, lo, _, _) in enumerate(jobs):
                        if lo is None or k < nlo[0]:
                            continue
                        if n == 0:
                            return
                        n -= 1
                        nlo[0] = k + 1
                        dve.wait_ge(s_hi, k + 1)
                        cols = banks[k % RING][:, 0:len(src) * m].rearrange("p (a b) -> p a b", b=m)
                        TT(lo, cols, dst.bitcast(F32), ALU.subtract).then_inc(s_lo, 1)

                g = {n: t[:, :, :] for n, t in big.items()}
                NL = 35
                for c in range(NHT // HCH):
                    hs = slice(c * HCH, (c + 1) * HCH)

                    def per_h(t, n):
                        return t[:, hs].unsqueeze(2).broadcast_to([P, HCH, n])

                    L = lst[:, :].unsqueeze(1).broadcast_to([P, HCH, NL])
                    if c:
                        dve.wait_ge(s_exp, c)
                    link(TT(g["arg"], L, per_h(v["om"], NL), ALU.mult))
                    reduce(g["arg"], g["k"], g["r"]).then_inc(s_red, 1)
                    TT(g["arg"], L, per_h(v["sg"], NL), ALU.mult).then_inc(s_dec, 1)
                    second_parts(PER_CHUNK)
                    dve.wait_ge(s_sin, 2 * c + 2)
                    link(TT(g["c"], g["c"], g["c"], ALU.mult))
                    link(TS(g["c"], g["c"], -2.0, 1.0, ALU.mult, ALU.add))
                    dve.wait_ge(s_exp, c + 1)
                    link(TT(g["c"], g["c"], g["e"], ALU.mult))
                    link(TT(g["s"], g["s"], g["e"], ALU.mult))
                    Vr, Vi = g["c"][:, :, 0:16], g["s"][:, :, 0:16]
                    X1, X2 = g["k"][:, :, 0:16], g["r"][:, :, 0:16]
                    if c:
                        dve.wait_ge(s_kept, 16 * c)
                    link(TT(tab[:, :, TP], Vr, per_h(v["al"], 16), ALU.mult))
                    link(TT(X1, Vi, per_h(v["be"], 16), ALU.mult))
                    link(TT(tab[:, :, TP], tab[:, :, TP], X1, ALU.add))
                    link(TT(tab[:, :, TQ], Vr, per_h(v["be"], 16), ALU.mult))
                    link(TT(X2, Vi, per_h(v["al"], 16), ALU.mult))
                    link(TT(tab[:, :, TQ], tab[:, :, TQ], X2, ALU.subtract))
                    link(dve.tensor_copy(tab[:, :, TJR], g["c"][:, :, 16:32]))
                    link(dve.tensor_copy(tab[:, :, TJI], g["s"][:, :, 16:32]))
                    link(dve.tensor_copy(tab[:, :, TSR], g["c"][:, :, 32:35]))
                    TS(tab[:, :, TSI], g["s"][:, :, 32:35], sgn[:, 0:1], None, ALU.mult).then_inc(s_tab, 1)
                second_parts(1000)
                for dst, src in ((cw[:, :, :], cw0[:, :, :]), (cb[:, :], cb0[:, :]), (cwb[:, :], cwb0[:, :]),
                                 (cbb[:, :], cbb0[:, :])):
                    link(TS(dst, src, 0.5, None, ALU.mult))
                link(dve.tensor_copy(emf[:, :], emap[:, :]))
                for e in range(NE):
                    link(TS(onehot[:, e, :], emf[:, :], float(e), None, ALU.is_equal))
                dve.wait_ge(s_exps, 3)
                link(TS(negA[:, :], alog[:, :], -1.0, None, ALU.mult))
                link(TS(gate[:, :], gt0[:, :], 1.0, None, ALU.add))
                link(dve.reciprocal(al1[:, :], gate[:, :]))
                link(TS(be1[:, :], al1[:, :], -1.0, 1.0, ALU.mult, ALU.add))
                link(TS(al1[:, :], al1[:, :], 1.0, None, ALU.add))
                link(dve.memset(w_hi[:, :, FW - 1:FW].bitcast(F32), 0.0))
                link(dve.memset(w_lo[:, :, FW - 1:FW].bitcast(F32), 0.0))

        T2 = sb("T2", [P, HID])
        H0 = sb("H0", [P, HID])
        XHT = sb("XHT", [P, KC, P])
        XI = sb("XI", [P, 2, P])
        TB = sb("TB", [P, 2, 2, NTAB])
        XSW = sb("XSW", [P, NST, 2])
        XTC = sb("XTC", [P, 2, 2, CS])
        W = sb("W", [P, 2, 4, CS])
        WI = sb("WI", [P, 2, 3, CS])
        VB = sb("VB", [P, 2, 16, 16])
        V2 = sb("V2", [P, 2, 16, 16])
        ST1 = sb("ST1", [P, 2, 6])
        MV1 = sb("MV1", [P, 2])
        VE1 = sb("VE1", [P, 1])
        RS1 = sb("RS1", [P, 1])
        SD1 = sb("SD1", [P, 1])
        CX = sb("CX", [P, 2, 4, CS])
        CB = sb("CB", [BCP, 4, CS])
        TH = sb("TH", [P, 2 * 4 * CS])
        THB = sb("THB", [BCP, 4 * CS])
        BT = sb("BT", [DST, 4 * CS])
        CT = sb("CT", [DST, 4 * CS])
        SZ = sb("SZ", [P, 512])
        XS = TH
        RF = sb("RF", [P, 2 * NH, CS])
        RB = sb("RB", [P, 2 * NH, CS])
        EX, NB = RF, RB
        NF = sb("NF", [P, 2 * NH, CS])
        YT = NF
        XD = sb("XD", [P, 2 * NH, HD])
        XMA = sb("XMA", [P, 2, P])
        GT = sb("GT", [P, 2, P])
        SP16 = {n: sb("sp_" + n, [P, 2, 2, NH]) for n in ("x", "a", "u", "z", "w", "p", "dt", "aa")}
        DD = sb("DD", [P, 2 * NH])
        SSQ = sb("SSQ", [P, 2])
        MS = sb("MS", [P, 2])
        RS = sb("RS", [P, 2])
        ST2 = sb("ST2", [P, 2, 6])
        MV2 = sb("MV2", [P, 2])
        VE2 = sb("VE2", [P, 1])
        RS2 = sb("RS2", [P, 1])
        XHI = sb("XHI", [P, 2, KC, P], F32R)
        XLO = sb("XLO", [P, 2, KC, P], F32R)
        LG = sb("LG", [P, NR])
        NM = sb("NM", [P, 1])
        EL = sb("EL", [P, NR])
        SE = sb("SE", [P, 1])
        RE = sb("RE", [P, 1])
        PR = sb("PR", [P, NR])
        P8 = sb("P8", [P, 8])
        PQ = sb("PQ", [P, NR])
        PW = sb("PW", [P, NE, NR])
        WE = sb("WE", [P, NE])
        HW = sb("HW", [P, P])
        HWT = sb("HWT", [P, P])
        bO = banks[0:2]
        bR = banks[2]
        bK = banks[3]
        bT = banks[4]
        bX, bY, bZ = banks[5], banks[6], banks[7]
        FC0 = 4 * CS + 16

        NCONV, NDT, NSM = 3 * TAPS, 18, 9
        per = dict(cls_in=(1, 16), xswap=2, xt=1, xtc=1, wr=1, wi=2, wsum=1, v1=1, v2=1, vsum=1,
                   km=2, hev=4, st1=4, rs1=1, sd1=1, xh1=1, tt=2, tr1=2, xte=2, down=1, gelu=1,
                   pin=3, xms=1, conv=NCONV, dtc=NDT, edt=1, th=2, xs=3, thz=1, sz=1, trx=1, gram=1, xse=1,
                   rf=1, rb=1, seg=1, ex=1, g4=4, dd=1, nf=1, nb=1, ns=1, mm=2, xd=1, yy=1, y1=1, yz=1, sq=2,
                   ms=1, rs=1, yn=2, tyn=1, yte=1, outp=1, u2=1, gt=1,
                   tcopy=(1, 16), up=2, h1=2, st2=4, rs2=1, hb=1, xh2=1, tr2=2, xhi=2, xlo=2,
                   rt=1, sm=NSM, se=1, hw=1, trh=1, hwe=1, o=2, fin=2)
        S = {}
        for n, c in per.items():
            c, unit = c if isinstance(c, tuple) else (c, 1)
            S[n] = Step(sem(n), c, unit)

        x_in = [sem("x_in_even"), sem("x_in_odd")]
        stored = [sem("stored_even"), sem("stored_odd")]

        def wait_x(eng, i, p):
            eng.wait_ge(x_in[p], (i - p) * 24 + 48)

        def wait_stored(eng, t, p):
            if not (isinstance(t, int) and t < 0):
                eng.wait_ge(stored[p], (t - p) * 16 + 32)

        def inc(ins, name):
            ins.then_inc(S[name].sem, S[name].unit)

        def wait(eng, n, **at):
            for name, j in at.items():
                S[name].after(eng, n, j)

        def apart(eng):
            eng.nop(nofuse=True)

        def active(i, lag, count):
            return (not isinstance(i, int)) or 0 <= i - lag < count

        def v3(ap, b):
            return ap.rearrange("p (a b) -> p a b", b=b)

        def decays(d):
            return SP16["aa"][:, d, :, :].rearrange("p a h -> p (a h)").unsqueeze(2).broadcast_to([P, 2 * NH, CS])

        LOOP_FROM, LOOP_TO, LAST = 6, CLS - 2, TILES + 4
        assert CLS % 2 == 0 and LOOP_TO > LOOP_FROM

        def iterations(eng, body):
            for i in range(LOOP_FROM):
                body(i, i % 2)
            with eng.Fori(LOOP_FROM, LOOP_TO, 2) as m:
                for u in range(2):
                    body(m + u, u)
            for i in range(LOOP_TO, LAST):
                body(i, i % 2)

        with nc.Block() as block:

            @block.sync
            def _(sp):
                def body(i, p):
                    if isinstance(i, int) and i == 0:
                        load_x(0, 0)
                    if active(i, -1, CLS + 1) and not (isinstance(i, int) and i + 1 >= CLS):
                        load_x(i + 1, 1 - p)
                    if isinstance(i, int) and i == CLS:
                        wait(sp, i - 1, tr1=2, tt=2)
                        sp.dma_start(H0[:, :], cls_tok[0].broadcast_to([P, HID])).then_inc(S["cls_in"].sem, 16)
                    if active(i, 2, TILES):
                        wait(sp, i - 2, tt=2)
                        wait(sp, i - 3, tr2=2, hb=1)
                        sp.dma_start(T2[:, :], T[:, p, :]).then_inc(S["tcopy"].sem, 16)
                    if active(i, 4, TILES):
                        store(i - 4, p)

                def load_x(t, p):
                    wait(sp, t - 2, xt=1, xswap=2)
                    wait(sp, t - 2, v1=1, wr=1, v2=1, wi=2)
                    tb = tables[t] if isinstance(t, int) else tables[bass.ds(t, 1)].rearrange("a f b k -> (a f) b k")
                    sp.dma_start(TB[:, p, :, :], tb).then_inc(x_in[p], 16)
                    for b in range(2):
                        h = t * 2 + b
                        src = x[:, h, :, :] if isinstance(t, int) else x[:, bass.ds(h, 1), :, :]
                        sp.dma_start(XI[CS * b:CS * (b + 1), p, :],
                                     src.rearrange("c n r -> c (n r)") if isinstance(t, int)
                                     else src.rearrange("c a n r -> c (a n r)")).then_inc(x_in[p], 16)

                def store(t, p):
                    wait(sp, t, fin=2)
                    for b in range(2):
                        if isinstance(t, int) and t == CLS:
                            if b == 0:
                                sp.dma_start(out[:, 0, :], HB[0:CS, p, :]).then_inc(stored[p], 16)
                            continue
                        r = t * 2 + b + 1
                        dst = out[:, r, :] if isinstance(t, int) else out[:, bass.ds(r, 1), :].rearrange("c a d -> c (a d)")
                        sp.dma_start(dst, HB[CS * b:CS * (b + 1), p, :]).then_inc(stored[p], 16)

                iterations(sp, body)
                sp.wait_ge(stored[0], 16 * (CLS + 1))
                sp.wait_ge(stored[1], 16 * CLS)

            @block.gpsimd
            def _(pool):
                def body(i, p):
                    A, H, D = active(i, 0, CLS), active(i, 1, TILES + 1), active(i, 3, TILES)
                    q = i - 1
                    if A:
                        wait_x(pool, i, p)
                        wait(pool, i - 1, xt=1)
                        apart(pool)
                        xi = XI[:, p, :].rearrange("p (n r) -> p n r", r=2)
                        for r in range(2):
                            inc(pool.tensor_copy(XSW[:, :, r], xi[:, :, 1 - r]), "xswap")
                        wait(pool, i - 1, vsum=1)
                        inc(pool.tensor_tensor(V2[:, :, :, :], TB[:, p, :, TQ].unsqueeze(2).broadcast_to([P, 2, 16, 16]),
                                               TB[:, p, :, TJI].unsqueeze(3).broadcast_to([P, 2, 16, 16]), ALU.mult), "v2")
                        wait(pool, i, xtc=1)
                        wait(pool, i - 1, wsum=1, km=2)
                        inc(pool.tensor_tensor(WI[:, :, :, :], XTC[:, 1, :, :].unsqueeze(2).broadcast_to([P, 2, 3, CS]),
                                               TB[:, p, :, TSI].unsqueeze(3).broadcast_to([P, 2, 3, CS]), ALU.mult), "wi")
                        inc(pool.tensor_copy(W[:, :, 0, :], XTC[:, 0, :, :]), "wi")
                    if H:
                        wait(pool, q, dtc=NDT)
                        wait(pool, q - 1, ns=1)
                        inc(pool.tensor_tensor(RB[:, :, :], m_gt[:, :].unsqueeze(1).broadcast_to([P, 2 * NH, CS]),
                                               decays(1), ALU.mult), "rb")
                    if D:
                        wait(pool, i - 3, st2=4)
                        inc(pool.tensor_tensor(RS2[:, :], VE2[:, :], half_neg[:, 0:1], ALU.pow), "rs2")
                        wait_stored(pool, i - 5, 1 - p)
                        wait(pool, i - 5, fin=2)
                        inc(pool.tensor_tensor(HB[:, 1 - p, :], T2[:, :], bbase[:, :], ALU.add), "hb")
                    if H:
                        wait(pool, q, seg=1, g4=4)
                        dtB = SP16["dt"][:, 1, :, :].unsqueeze(3).broadcast_to([P, 2, NH, CS])
                        inc(pool.tensor_tensor(NB[:, :, :].rearrange("p (a h) t -> p a h t", a=2),
                                               GB[:, :, :].unsqueeze(2).broadcast_to([P, 2, NH, CS]), dtB, ALU.mult), "nb")
                        wait(pool, q, xse=1, dd=1)
                        wait(pool, q - 1, yn=2, tyn=1)
                        inc(pool.tensor_tensor(XD[:, :, :], v3(XS[:, :], HD),
                                               DD[:, :].unsqueeze(2).broadcast_to([P, 2 * NH, HD]), ALU.mult), "xd")
                    if active(i, 0, TILES):
                        wait(pool, i, st1=4)
                        inc(pool.tensor_tensor(RS1[:, :], VE1[:, :], half_neg[:, 0:1], ALU.pow), "rs1")
                        wait(pool, i, sd1=1, xh1=1)
                        wait(pool, i - 2, tcopy=1)
                        apart(pool)
                        inc(pool.tensor_scalar(T[:, p, :], H0[:, :], SD1[:, 0:1], MV1[:, 0:1], ALU.mult, ALU.add), "tt")
                        wait(pool, i, tt=1)
                        inc(pool.tensor_tensor(T[:, p, :], T[:, p, :], bup[:, :], ALU.add), "tt")
                    if H:
                        wait(pool, q, ms=1)
                        inc(pool.tensor_tensor(RS[:, :], MS[:, :], half_neg[:, :], ALU.pow), "rs")

                iterations(pool, body)

            @block.scalar
            def _(act):
                def copy(dst, src, name, scale=1.0):
                    inc(act.activation(dst, src, ACT.Copy, scale=scale), name)

                def body(i, p):
                    A, H = active(i, 0, CLS), active(i, 1, TILES + 1)
                    D, E = active(i, 3, TILES), active(i, 4, TILES)
                    A1 = active(i, 0, TILES)
                    q = i - 1
                    if A:
                        wait(act, i, xt=1)
                        wait(act, i - 1, wr=1, wi=2)
                        copy(XTC[:, :, :, :].rearrange("p a b c -> p (a b c)"), bK[:, 0:256], "xtc")
                    if H:
                        wait(act, q, pin=3)
                        wait(act, q - 1, yz=1)
                        inc(act.activation(SZ[:, :], bZ[:, :], ACT.Tanh), "thz")
                        wait(act, q, dtc=2)
                        wait(act, q - 1, dtc=4)
                        inc(act.activation(SP16["u"][:, :, :, :], SP16["a"][:, :, :, :], ACT.Exp), "edt")
                    if A:
                        for b in range(2):
                            wait(act, i, km=b + 1)
                            if b == 0:
                                wait(act, i - 1, tr1=2, tt=2)
                            for h in range(2):
                                copy(H0[CS * b:CS * (b + 1), HALF * h:HALF * (h + 1)], bK[CS * h:CS * (h + 1), :], "hev")
                    if H:
                        wait(act, q, conv=NCONV)
                        wait(act, q - 1, yy=1, xd=1)
                        inc(act.activation(TH[:, :], CX[:, :, :, :].rearrange("p a b c -> p (a b c)"), ACT.Tanh), "th")
                        wait(act, q - 1, xs=3)
                        inc(act.activation(THB[:, :], CB[:, :, :].rearrange("p b c -> p (b c)"), ACT.Tanh), "th")
                    if E:
                        wait(act, i - 4, sm=2)
                        wait(act, i - 5, sm=NSM)
                        inc(act.activation(EL[:, :], LG[:, :], ACT.Exp, bias=NM[:, 0:1], accum_out=SE[:, 0:1]), "se")
                    if H:
                        wait(act, q, trx=1, xs=3)
                        copy(XS[:, :], bX[:, :], "xse")
                        wait(act, q, seg=1)
                        inc(act.activation(EX[:, :, :].rearrange("p a b -> p (a b)"), bZ[:, :], ACT.Exp), "ex")
                    if D:
                        for g in range(2):
                            wait(act, i - 3, tr2=g + 1)
                            wait(act, i - 5, o=2)
                            copy(XHI[:, 1 - p, 4 * g:4 * g + 4, :], v3(bT[:, :], P), "xhi")
                    if E:
                        wait(act, i - 4, trh=1)
                        wait(act, i - 5, o=2)
                        copy(HWT[:, :], bR[:, 256:384], "hwe")
                    if H:
                        wait(act, q, yz=1)
                        wait(act, q - 1, ms=1)
                        for a in range(2):
                            inc(act.activation(TH[:, 0:256], v3(XD[:, :, :].rearrange("p a b -> p (a b)"), 256)[:, a, :],
                                               ACT.Square, accum_out=SSQ[:, a:a + 1]), "sq")
                            wait(act, q, sq=a + 1)
                    if A1:
                        for g in range(2):
                            wait(act, i, tr1=g + 1)
                            wait(act, i - 1, down=1)
                            copy(XHT[:, 4 * g:4 * g + 4, :], v3(bT[:, :], P), "xte")
                    if H:
                        wait(act, q, tyn=1, mm=2)
                        wait(act, q - 1, outp=1)
                        copy(YT[:, :, :].rearrange("p a b -> p (a b)"), bZ[:, :], "yte")
                    if A1:
                        wait(act, i, down=1)
                        wait(act, i - 2, pin=3, xms=1)
                        inc(act.activation(U[:, p, 0, :], bK[:, 0:P], ACT.Gelu, bias=bdn[:, 0:1]), "gelu")

                iterations(act, body)

            @block.vector
            def _(dve):
                TT, TS, STT = dve.tensor_tensor, dve.tensor_scalar, dve.scalar_tensor_tensor

                def conv_tap(q, s):
                    hx = bX[:, :].rearrange("p (c g t) -> p c g t", c=2, g=4)
                    hb = bY[0:BCP, 0:256].rearrange("p (g t) -> p g t", g=4)
                    for c, (dst, src, w, bias) in enumerate(((CX[:, 0], hx[:, 0], cw[:, 0], cb[:, 0:1]),
                                                             (CX[:, 1], hx[:, 1], cw[:, 1], cb[:, 1:2]),
                                                             (CB[:, :, :], hb, cwb[:, :], cbb[:, 0:1]))):
                        k = TAPS - 1 - s
                        if s == 0:
                            if c == 0:
                                wait(dve, q - 1, trx=1, gram=1)
                            inc(TS(dst, src, w[:, k:k + 1], bias, ALU.mult, ALU.add), "conv")
                        else:
                            wait(dve, q, conv=3 * (s - 1) + c + 1)
                            inc(STT(dst[:, :, s:CS], src[:, :, 0:CS - s], w[:, k:k + 1], dst[:, :, s:CS],
                                    ALU.mult, ALU.add), "conv")

                def softplus(q, js):
                    f = {n: t[:, :, :, :] for n, t in SP16.items()}
                    for j in js:
                        if j > 0:
                            wait(dve, q, dtc=j)
                        if j == 0:
                            wait(dve, q, pin=2)
                            wait(dve, q - 1, rb=1, nb=1)
                            ins = TT(f["x"], bY[:, 256:272].rearrange("p (a d h) -> p d a h", a=2, d=2),
                                     dtb[:, :].unsqueeze(1).unsqueeze(1).broadcast_to([P, 2, 2, NH]), ALU.add)
                        elif j == 1:
                            wait(dve, q - 1, edt=1)
                            ins = STT(f["a"], f["x"], -1.0, f["x"], ALU.mult, ALU.min)
                        elif j == 2:
                            wait(dve, q, edt=1)
                            ins = TS(f["z"], f["u"], 2.0, None, ALU.add)
                        elif j == 3:
                            ins = dve.reciprocal(f["w"], f["z"])
                        elif j == 4:
                            ins = TT(f["z"], f["u"], f["w"], ALU.mult)
                        elif j == 5:
                            ins = TT(f["w"], f["z"], f["z"], ALU.mult)
                        elif j == 6:
                            ins = TS(f["p"], f["w"], 1.0 / 17, None, ALU.mult)
                        elif j < 14:
                            ins = STT(f["p"], f["p"], 1.0 / (29 - 2 * j), f["w"], ALU.add, ALU.mult)
                        elif j == 14:
                            ins = STT(f["p"], f["p"], 1.0, f["z"], ALU.add, ALU.mult)
                        elif j == 15:
                            ins = TS(f["x"], f["x"], 0.0, None, ALU.max)
                        elif j == 16:
                            wait(dve, q - 1, nb=1, rb=1)
                            ins = STT(f["dt"], f["p"], 2.0, f["x"], ALU.mult, ALU.add)
                        elif j == 17:
                            ins = TT(f["aa"], f["dt"],
                                     negA[:, :].unsqueeze(1).unsqueeze(1).broadcast_to([P, 2, 2, NH]), ALU.mult)
                        inc(ins, "dtc")

                def body(i, p):
                    A, H = active(i, 0, CLS), active(i, 1, TILES + 1)
                    D, E = active(i, 3, TILES), active(i, 4, TILES)
                    A1 = active(i, 0, TILES)
                    q = i - 1
                    if H:
                        softplus(q, range(0, 1))
                        wait(dve, q, pin=2)
                        conv_tap(q, 0)
                        softplus(q, range(1, 2))
                        conv_tap(q, 1)
                        conv_tap(q, 2)
                        if not isinstance(i, int) or q < TILES:
                            wait(dve, q, gelu=1)
                        inc(TS(XMA[:, 1 - p, :], U[:, 1 - p, 0, :], al1[:, 0:1], None, ALU.mult), "xms")
                    if A:
                        wait_x(dve, i, p)
                        wait(dve, i - 1, km=2)
                        inc(TT(VB[:, :, :, :], TB[:, p, :, TP].unsqueeze(2).broadcast_to([P, 2, 16, 16]),
                               TB[:, p, :, TJR].unsqueeze(3).broadcast_to([P, 2, 16, 16]), ALU.mult), "v1")
                        wait(dve, i, xtc=1)
                        inc(TT(W[:, :, 1:4, :], XTC[:, 0, :, :].unsqueeze(2).broadcast_to([P, 2, 3, CS]),
                               TB[:, p, :, TSR].unsqueeze(3).broadcast_to([P, 2, 3, CS]), ALU.mult), "wr")
                        wait(dve, i, v2=1, v1=1)
                        inc(TT(VB[:, :, :, :], VB[:, :, :, :], V2[:, :, :, :], ALU.add), "vsum")
                        wait(dve, i, wi=1, wr=1)
                        inc(TT(W[:, :, 1:4, :], W[:, :, 1:4, :], WI[:, :, :, :], ALU.add), "wsum")
                    if D:
                        wait(dve, i - 3, tcopy=1)
                        for h in range(2):
                            wait(dve, i - 3, up=h + 1)
                            c = slice(HALF * h, HALF * (h + 1))
                            inc(TT(T2[:, c], bT[:, :], T2[:, c], ALU.add), "h1")
                            wait(dve, i - 3, h1=h + 1)
                            inc(dve.bn_stats(ST2[:, h, :], T2[:, c]), "st2")
                        wait(dve, i - 3, st2=2)
                        apart(dve)
                        inc(dve.bn_aggr(MV2[:, :], ST2[:, :, :].rearrange("p a b -> p (a b)")), "st2")
                        wait(dve, i - 3, st2=3)
                        inc(TS(VE2[:, :], MV2[:, 1:2], EPS, None, ALU.add), "st2")
                    if H:
                        for s in range(3, 5):
                            conv_tap(q, s)
                    if E:
                        router_logits(i - 4)
                    if H:
                        for s in range(5, TAPS):
                            conv_tap(q, s)
                        wait(dve, q, thz=1)
                        wait(dve, q, pin=3)
                        inc(STT(SZ[:, :], SZ[:, :], 1.0, bZ[:, :], ALU.add, ALU.mult), "sz")
                        softplus(q, range(2, NDT))
                        wait(dve, q, dtc=NDT)
                        wait(dve, q - 1, seg=1, mm=2)
                        inc(TT(RF[:, :, :], m_lt[:, :].unsqueeze(1).broadcast_to([P, 2 * NH, CS]), decays(0), ALU.mult), "rf")
                    if D:
                        wait(dve, i - 3, rs2=1, hb=1)
                        inc(TS(T2[:, :], T2[:, :], MV2[:, 0:1], RS2[:, 0:1], ALU.subtract, ALU.mult), "xh2")
                    if H:
                        wait(dve, q, th=1)
                        wait(dve, q - 1, trx=1, gram=1)
                        cx = CX[:, :, :, :].rearrange("p a b c -> p (a b c)")
                        inc(STT(cx, TH[:, :], 1.0, cx, ALU.add, ALU.mult), "xs")
                        wait(dve, q, th=2)
                        cbf = CB[:, :, :].rearrange("p b c -> p (b c)")
                        inc(STT(BT[:, :], THB[0:DST, :], 1.0, cbf[0:DST, :], ALU.add, ALU.mult), "xs")
                        inc(STT(CT[:, :], THB[32:32 + DST, :], 1.0, cbf[32:32 + DST, :], ALU.add, ALU.mult), "xs")
                    if E:
                        router_weights(i - 4)
                    if H:
                        wait(dve, q, gram=1)
                        wait(dve, q - 1, nb=1, nf=1)
                        for b in range(2):
                            r = slice(CS * b, CS * (b + 1))
                            gr = bY[r, 0:256].rearrange("p (a c) -> p a c", a=2)
                            mf = m_lt[r, 1:CS].unsqueeze(1).broadcast_to([CS, 2, CS - 1])
                            mb = m_gt[r, 0:CS - 1].unsqueeze(1).broadcast_to([CS, 2, CS - 1])
                            inc(TT(GF[r, :, 1:CS], gr[:, :, CS * b:CS * b + CS - 1], mf, ALU.mult), "g4")
                            inc(TT(GB[r, :, 0:CS - 1], gr[:, :, CS * b + 1:CS * b + CS], mb, ALU.mult), "g4")
                        wait(dve, q - 1, xd=1)
                        inc(TT(DD[:, :].rearrange("p (a h) -> p a h", a=2), v3(bY[:, FC0:FC0 + 2 * NH], NH),
                               Dbc[:, :].unsqueeze(1).broadcast_to([P, 2, NH]), ALU.add), "dd")
                        wait(dve, q, g4=4)
                        wait(dve, q - 1, outp=1, mm=2)
                        dtF = SP16["dt"][:, 0, :, :].unsqueeze(3).broadcast_to([P, 2, NH, CS])
                        inc(TT(NF[:, :, :].rearrange("p (a h) t -> p a h t", a=2),
                               GF[:, :, :].unsqueeze(2).broadcast_to([P, 2, NH, CS]), dtF, ALU.mult), "nf")
                        wait(dve, q, nf=1, nb=1)
                        inc(TT(NF[:, :, :], NF[:, :, :], NB[:, :, :], ALU.add), "ns")
                        wait(dve, q, ns=1, ex=1)
                        wait(dve, q - 1, yy=1)
                        for b in range(2):
                            r = slice(CS * b, CS * (b + 1))
                            inc(TT(Mt[r, :, :, r].rearrange("p a h t -> p (a h) t"), NF[r, :, :], EX[r, :, :], ALU.mult), "mm")
                    if D:
                        for g in range(2):
                            wait(dve, i - 3, xhi=g + 1)
                            wait(dve, i - 5, o=2)
                            ks = slice(4 * g, 4 * g + 4)
                            inc(TT(XLO[:, 1 - p, ks, :], v3(bT[:, :], P), XHI[:, 1 - p, ks, :].bitcast(F32), ALU.subtract), "xlo")
                    if E:
                        final(i - 4, p, 0)
                    if A1:
                        if isinstance(i, int) and i == CLS:
                            dve.wait_ge(S["cls_in"].sem, 16)
                        else:
                            wait(dve, i, hev=4)
                        for h in range(2):
                            inc(dve.bn_stats(ST1[:, h, :], H0[:, HALF * h:HALF * (h + 1)]), "st1")
                        wait(dve, i, st1=2)
                        wait(dve, i - 1, tt=2)
                        apart(dve)
                        inc(dve.bn_aggr(MV1[:, :], ST1[:, :, :].rearrange("p a b -> p (a b)")), "st1")
                        wait(dve, i, st1=3)
                        inc(TS(VE1[:, :], MV1[:, 1:2], EPS, None, ALU.add), "st1")
                    if H:
                        wait(dve, q, yy=1, xd=1)
                        xd = XD[:, :, :].rearrange("p a b -> p (a b)")
                        inc(TT(xd, bX[:, :], xd, ALU.add), "y1")
                        wait(dve, q, y1=1)
                        inc(TT(xd, xd, SZ[:, :], ALU.mult), "yz")
                    if A1:
                        wait(dve, i, rs1=1)
                        inc(TS(H0[:, :], H0[:, :], MV1[:, 0:1], RS1[:, 0:1], ALU.subtract, ALU.mult), "xh1")
                        inc(TS(SD1[:, :], VE1[:, :], RS1[:, 0:1], 1.0, ALU.mult, ALU.add), "sd1")
                    if H:
                        wait(dve, q, sq=2)
                        wait(dve, q - 1, rs=1)
                        inc(TS(MS[:, :], SSQ[:, :], 1.0 / DIN, EPS, ALU.mult, ALU.add), "ms")
                        wait(dve, q, rs=1)
                        for a in range(2):
                            ya = v3(XD[:, :, :].rearrange("p a b -> p (a b)"), 256)[:, a, :]
                            inc(TS(ya, ya, RS[:, a:a + 1], None, ALU.mult), "yn")
                        wait(dve, q, outp=1)
                        if not isinstance(i, int) or q < TILES:
                            wait(dve, q - 1, pin=3)
                        inc(dve.tensor_copy(U[:, p, 1, :], bY[:, 0:P]), "u2")
                        if not isinstance(i, int) or q >= 1:
                            wait(dve, q - 3, up=2)
                            inc(STT(GT[:, p, :], bY[:, P:2 * P], be1[:, 0:1], XMA[:, p, :], ALU.mult, ALU.add), "gt")
                    if E:
                        final(i - 4, p, 1)

                def router_logits(t):
                    wait(dve, t, rt=1)
                    wait(dve, t - 1, se=1)
                    inc(TT(LG[:, :], bR[:, P:P + NR], rbias[:, :], ALU.add), "sm")
                    wait(dve, t, sm=1)
                    inc(dve.tensor_reduce(NM[:, :], LG[:, :], AX.X, ALU.max, negate=True), "sm")

                def router_weights(t):
                    wait(dve, t, se=1)
                    inc(dve.reciprocal(RE[:, :], SE[:, :]), "sm")
                    wait(dve, t, sm=3)
                    inc(TS(PR[:, :], EL[:, :], RE[:, 0:1], None, ALU.mult), "sm")
                    wait(dve, t, sm=4)
                    apart(dve)
                    inc(dve.max(P8[:, :], PR[:, :]), "sm")
                    wait(dve, t, sm=5)
                    apart(dve)
                    inc(dve.match_replace(PQ[:, :], P8[:, :], PR[:, :], 0.0), "sm")
                    wait(dve, t, sm=6)
                    inc(TT(PQ[:, :], PR[:, :], PQ[:, :], ALU.subtract), "sm")
                    wait(dve, t, sm=7)
                    inc(TT(PW[:, :, :], onehot[:, :, :], PQ[:, :].unsqueeze(1).broadcast_to([P, NE, NR]), ALU.mult), "sm")
                    wait(dve, t, sm=8)
                    inc(dve.tensor_reduce(WE[:, :], PW[:, :, :], AX.X, ALU.add), "sm")
                    wait(dve, t, sm=9)
                    wait(dve, t - 1, trh=1)
                    inc(TT(HW[:, :].rearrange("p (e r) -> p e r", e=NE), bR[:, 0:P].rearrange("p (e r) -> p e r", e=NE),
                           WE[:, :].unsqueeze(2).broadcast_to([P, NE, RK]), ALU.mult), "hw")

                def final(t, p, h):
                    wait(dve, t, o=h + 1, hb=1)
                    c = slice(HALF * h, HALF * (h + 1))
                    inc(TT(HB[:, p, c], bO[h][:, :], HB[:, p, c], ALU.add), "fin")

                iterations(dve, body)

            @block.tensor
            def _(pe):
                mm, tr = pe.matmul, pe.transpose

                def body(i, p):
                    A, H = active(i, 0, CLS), active(i, 1, TILES + 1)
                    D, E = active(i, 3, TILES), active(i, 4, TILES)
                    A1 = active(i, 0, TILES)
                    q, td, te = i - 1, i - 3, i - 4

                    def ffn(c0, c1, bank, ks, name=None, last=None):
                        for k in ks:
                            for n, (xs_, ws) in enumerate(((XHI, w_hi), (XHI, w_lo), (XLO, w_hi))):
                                ins = mm(bank[:, 0:c1 - c0], xs_[:, p, k, :], ws[:, k, c0:c1],
                                         start=(k == 0 and n == 0), stop=(last == k and n == 2))
                        return ins

                    def bases(h, ks):
                        if E:
                            if ks[0] == 0:
                                wait(pe, te - 1, fin=h + 1)
                            ffn(HALF * h, HALF * (h + 1), bO[h], ks)

                    def lora(h):
                        if E:
                            wait(pe, te, hwe=1)
                            inc(mm(bO[h][:, :], HWT[:, :], lbT[:, HALF * h:HALF * (h + 1)], start=False, stop=True), "o")

                    def up(h):
                        if D:
                            if h == 0:
                                wait(pe, td, gt=1)
                                wait(pe, min(i - 1, CLS) if isinstance(i, int) else i - 1, xte=2)
                            else:
                                wait(pe, td, h1=1)
                            inc(mm(bT[:, :], GT[:, 1 - p, :], wuT[:, HALF * h:HALF * (h + 1)], start=True, stop=True), "up")

                    def s4d(b):
                        if A:
                            if b == 0:
                                wait(pe, i, xtc=1, wsum=1, wi=2, vsum=1)
                            else:
                                wait(pe, i, hev=2)
                            for s in range(2):
                                ins = mm(bK[:, 256 * s:256 * (s + 1)], W[:, b, 2 * s:2 * s + 2, :].rearrange("p a c -> p (a c)"),
                                         VB[:, b, :, :].rearrange("p a c -> p (a c)"), start=True, stop=True)
                            inc(ins, "km")

                    def turn_d(g):
                        if D:
                            if g == 0:
                                wait(pe, td, xh2=1)
                            else:
                                wait(pe, td, xlo=1)
                            for k in range(4):
                                ins = tr(bT[:, P * k:P * (k + 1)], T2[:, (4 * g + k) * P:(4 * g + k + 1) * P], ident[:, :])
                            inc(ins, "tr2")

                    def turn_a(g):
                        if A1:
                            if g == 0:
                                wait(pe, i, xh1=1)
                                if D:
                                    wait(pe, td, xlo=2)
                            else:
                                wait(pe, i, xte=1)
                            for k in range(4):
                                ins = tr(bT[:, P * k:P * (k + 1)], H0[:, (4 * g + k) * P:(4 * g + k + 1) * P], ident[:, :])
                            inc(ins, "tr1")

                    if A:
                        wait_x(pe, i, p)
                        wait(pe, i, xswap=2)
                        wait(pe, i - 1, gelu=1)
                        tr(bK[:, 0:P], XI[:, p, :], ident[:, :])
                        inc(tr(bK[:, P:2 * P], XSW[:, :, :].rearrange("p n r -> p (n r)"), ident[:, :]), "xt")
                    if H:
                        u = U[:, 1 - p, :, :].rearrange("p a t -> p (a t)")
                        if not isinstance(i, int) or q < TILES:
                            wait(pe, q, gelu=1)
                        wait(pe, q - 1, u2=1, y1=1, yte=1)
                        wait(pe, q - 2, gt=1)
                        for c in range(2):
                            ins = mm(bX[:, 256 * c:256 * (c + 1)], wx[:, P * c:P * (c + 1)], u, start=True, stop=True)
                        inc(ins, "pin")
                        for a in range(2):
                            mm(bY[:, 256 + 8 * a:264 + 8 * a], U[:, 1 - p, a, :], wbc[:, BCP:BCP + 2 * NH], start=True, stop=True)
                        inc(mm(bY[0:BCP, 0:256], wbc[:, 0:BCP], u, start=True, stop=True), "pin")
                        for a in range(2):
                            ins = mm(bZ[:, 256 * a:256 * (a + 1)], U[:, 1 - p, a, :], wz[:, :], start=True, stop=True)
                        inc(ins, "pin")
                    if E:
                        wait(pe, te, xlo=2)
                        wait(pe, te - 1, hwe=1)
                        ffn(HID, FW, bR, range(0, 4))
                    up(0)
                    if E:
                        inc(ffn(HID, FW, bR, range(4, KC), last=KC - 1), "rt")
                    up(1)
                    s4d(0)
                    bases(0, range(0, 2))
                    s4d(1)
                    bases(0, range(2, 4))
                    if H:
                        wait(pe, q, xs=3, conv=NCONV)
                        for a in range(2):
                            for c in range(2):
                                ins = tr(bX[:, (2 * a + c) * P:(2 * a + c + 1) * P],
                                         CX[:, c, 2 * a:2 * a + 2, :].rearrange("p g t -> p (g t)"), ident[:, :])
                        inc(ins, "trx")
                        wait(pe, q, dtc=1)
                        for a in range(2):
                            for c in range(2):
                                mm(bY[:, FC0 + NH * a:FC0 + NH * (a + 1)], CX[:, c, 2 * a:2 * a + 2, :].rearrange("p g t -> p (g t)"),
                                   fcT[:, c, :], start=(c == 0), stop=(c == 1))
                        for a in range(2):
                            ins = mm(bY[:, P * a:P * (a + 1)], BT[:, P * a:P * (a + 1)], CT[:, P * a:P * (a + 1)], start=True, stop=True)
                        inc(ins, "gram")
                    bases(0, range(4, 6))
                    if H:
                        wait(pe, q, rf=1, rb=1, sz=1)
                        for a in range(2):
                            for n, (m, r) in enumerate(((earlier, RF), (later, RB))):
                                ins = mm(bZ[:, 256 * a:256 * (a + 1)], m[:, :],
                                         r[:, NH * a:NH * (a + 1), :].rearrange("p h t -> p (h t)"), start=(n == 0), stop=(n == 1))
                        inc(ins, "seg")
                    turn_d(0)
                    bases(0, range(6, 8))
                    turn_d(1)
                    if E:
                        wait(pe, te, hw=1)
                        inc(tr(bR[:, 256:256 + P], HW[:, :], ident[:, :]), "trh")
                    bases(1, range(0, 1))
                    lora(0)
                    if H:
                        wait(pe, q, mm=2, xse=1)
                        for a in range(2):
                            for h in range(NH):
                                ins = mm(bX[:, 256 * a + HD * h:256 * a + HD * (h + 1)], Mt[:, a, h, :],
                                         XS[:, 256 * a + HD * h:256 * a + HD * (h + 1)], start=True, stop=True)
                        inc(ins, "yy")
                    bases(1, range(1, 3))
                    turn_a(0)
                    bases(1, range(3, 4))
                    turn_a(1)
                    bases(1, range(4, 6))
                    if H:
                        wait(pe, q, yn=2, ex=1)
                        for c in range(2):
                            for a in range(2):
                                ins = tr(bZ[:, (2 * c + a) * P:(2 * c + a + 1) * P],
                                         XD[:, NH * a + 2 * c:NH * a + 2 * c + 2, :].rearrange("p a b -> p (a b)"), ident[:, :])
                        inc(ins, "tyn")
                    if A1:
                        wait(pe, i, xte=2)
                        if A:
                            wait(pe, i, hev=4)
                        for k in range(KC):
                            ins = mm(bK[:, 0:P], wdT[:, k, :], XHT[:, k, :], start=(k == 0), stop=(k == KC - 1))
                        inc(ins, "down")
                    bases(1, range(6, 7))
                    if H:
                        wait(pe, q, yte=1, g4=4, dd=1)
                        yt = YT[:, :, :].rearrange("p a b -> p (a b)")
                        for c in range(2):
                            ins = mm(bY[:, 0:256], owT[:, c, :], yt[:, 256 * c:256 * (c + 1)], start=(c == 0), stop=(c == 1))
                        inc(ins, "outp")
                    bases(1, range(7, 8))
                    lora(1)

                iterations(pe, body)


_INS = ["x", "cls_tok", "L0_tok_log_dt", "L0_tok_B", "L0_tok_inv_A_real", "L0_tok_A_imag", "L0_attn_w_down",
        "L0_attn_b_down", "L0_attn_w_up", "L0_attn_b_up", "L0_attn_gate1", "L0_attn_hy_in_w", "L0_attn_hy_conv_w",
        "L0_attn_hy_conv_b", "L0_attn_hy_dt_bias", "L0_attn_hy_A_log", "L0_attn_hy_D", "L0_attn_hy_fcD_w",
        "L0_attn_hy_norm_w", "L0_attn_hy_out_w", "L0_ffn_base_W", "L0_ffn_base_b", "L0_ffn_router_W",
        "L0_ffn_router_b", "L0_ffn_A", "L0_ffn_B", "L0_ffn_expert_map"]


def kernel(**inputs):
    import concourse.bacc as bacc
    from concourse.bass_utils import run_bass_kernel_spmd

    nc = bacc.Bacc("TRN2", target_bir_lowering=False, num_devices=1)
    arrays, args = {}, []
    for name in _INS:
        a = np.ascontiguousarray(inputs[name])
        if a.ndim == 0:
            a = a.reshape(1, 1)
        arrays[f"in_{name}"] = a
        args.append(nc.dram_tensor(f"in_{name}", a.shape, mybir.dt.from_np(a.dtype), kind="ExternalInput").ap())
    steps, rows, states, _ = inputs["x"].shape
    shape = (steps, rows + 1, inputs["cls_tok"].shape[-1])
    args.append(nc.dram_tensor("out_0", shape, F32, kind="ExternalOutput").ap())
    build(nc, *args, pairs=rows // 2)
    r = run_bass_kernel_spmd(nc, [arrays], core_ids=[0])
    return r.results[0]["out_0"]
```

```python
from contextlib import ExitStack

import numpy as np

import concourse.bass as bass
from concourse import mybir

F32 = mybir.dt.float32
F32R = mybir.dt.float32r
I32 = mybir.dt.int32
ALU = mybir.AluOpType
ACT = mybir.ActivationFunctionType
AX = mybir.AxisListType

P = 128
PI = float(np.pi)
EPS = 1e-5
ROUND = float(1.5 * 2 ** 23)


class Step:

    def __init__(self, sem, per, unit=1):
        self.sem, self.per, self.unit = sem, per, unit

    def after(self, eng, n, j=None):
        if isinstance(n, int) and n < 0:
            return
        j = self.per if j is None else j
        eng.wait_ge(self.sem, (n * self.per + j) * self.unit)


def build(nc, x, cls_tok, log_dt, tok_B, inv_A_real, A_imag, w_down, b_down, w_up, b_up, gate1, in_w,
          conv_w, conv_b, dt_bias, A_log, hy_D, fcD_w, norm_w, out_w, base_W, base_b, router_W, router_b,
          lora_A, lora_B, expert_map, out, pairs=64):
    CS, NHT, NST, _ = x.shape
    DM, HID = w_down.shape
    KC = HID // P
    DIN = out_w.shape[1]
    NH = A_log.shape[0]
    HD = DIN // NH
    DST = (conv_w.shape[0] - DIN) // 2
    TAPS = conv_w.shape[2]
    NE, RK, _ = lora_A.shape
    NR = router_W.shape[0]
    FW = HID + P + NR + 1
    HALF = HID // 2
    BCP = 48
    TILES = pairs + 1
    CLS = pairs

    with ExitStack() as keep:
        def sb(name, shape, dt=F32, ctx=None):
            return (ctx or keep).enter_context(nc.sbuf_tensor(name, shape, dt))

        def sem(name):
            return keep.enter_context(nc.semaphore(name))

        w_hi = sb("w_hi", [P, KC, FW], F32R)
        w_lo = sb("w_lo", [P, KC, FW], F32R)
        wdT = sb("wdT", [P, KC, DM])
        wuT = sb("wuT", [P, HID])
        lbT = sb("lbT", [P, HID])
        wx = sb("wx", [P, DIN])
        wbc = sb("wbc", [P, BCP + 2 * NH])
        wz = sb("wz", [P, DIN])
        fcT = sb("fcT", [P, 2, NH])
        owT = sb("owT", [P, 2, DM])
        ident = sb("ident", [P, P])
        earlier = sb("earlier", [P, P])
        later = sb("later", [P, P])
        m_lt = sb("m_lt", [P, CS])
        m_gt = sb("m_gt", [P, CS])
        bup = sb("bup", [P, HID])
        bbase = sb("bbase", [P, HID])
        rbias = sb("rbias", [P, NR])
        onehot = sb("onehot", [P, NE, NR])
        dtb = sb("dtb", [P, NH])
        negA = sb("negA", [P, NH])
        Dbc = sb("Dbc", [P, NH])
        bdn = sb("bdn", [P, 1])
        al1 = sb("al1", [P, 1])
        be1 = sb("be1", [P, 1])
        cw = sb("cw", [P, 2, TAPS])
        cb = sb("cb", [P, 2])
        cwb = sb("cwb", [BCP, TAPS])
        cbb = sb("cbb", [BCP, 1])
        half_neg = sb("half_neg", [P, 2])
        TP, TQ, TJR, TJI = (slice(16 * k, 16 * k + 16) for k in range(4))
        TSR, TSI, NTAB = slice(64, 67), slice(67, 70), 70
        tables = nc.dram_tensor("tables", (NHT // 2, P, 2, NTAB), F32, kind="Internal").ap()
        T = sb("T", [P, 2, HID])
        HB = sb("HB", [P, 2, HID])
        Mt = sb("Mt", [P, 2, NH, P])
        GF = sb("GF", [P, 2, CS])
        GB = sb("GB", [P, 2, CS])
        U = sb("U", [P, 2, 2, P])
        banks = [keep.enter_context(nc.psum_tensor(f"bank{i}", [P, 512], F32)) for i in range(8)]

        with ExitStack() as tmp:
            def ts(name, shape, dt=F32):
                return sb(name, shape, dt, tmp)

            stage = [T[:, 0, :], T[:, 1, :], HB[:, 0, :], HB[:, 1, :], ts("st4", [P, HID])[:, :], ts("st5", [P, HID])[:, :]]
            NS = len(stage)
            inw_s = ts("inw_s", [P, 4, P])
            bc_s = ts("bc_s", [P, P])
            dt_s = ts("dt_s", [2 * NH, P])
            fc_s = ts("fc_s", [NH, DIN])
            ow_s = ts("ow_s", [P, DIN])
            nw = ts("nw", [P, 2])
            alog = ts("alog", [P, NH])
            gate = ts("gate", [P, 1])
            gt0 = ts("gt0", [P, 1])
            emap = ts("emap", [P, NR], I32)
            emf = ts("emf", [P, NR])
            cw0 = ts("cw0", [P, 2, TAPS])
            cb0 = ts("cb0", [P, 2])
            cwb0 = ts("cwb0", [BCP, TAPS])
            cbb0 = ts("cbb0", [BCP, 1])
            ones = ts("ones", [P, P])
            evm = ts("evm", [P, NST])
            ai_s = ts("ai_s", [P, NST])
            ar_s = ts("ar_s", [P, NST])
            b_s = ts("b_s", [P, NST, 2])
            dup = ts("dup", [P, 4, NST, 2])
            par = ts("par", [P, 4, NHT])
            ldt = ts("ldt", [P, NHT])
            lst = ts("lst", [P, 35])
            lst_i = ts("lst_i", [P, 35], I32)
            v = {n: ts("v_" + n, [P, NHT]) for n in
                 ("dt", "ar", "sg", "om", "t0", "t1", "t2", "t3", "t4", "er", "ei", "co", "Gr", "Gi", "al", "be")}
            evc = ts("evc", [P, 1])
            odc = ts("odc", [P, 1])
            sgn = ts("sgn", [P, 1])
            HCH = 16
            tab = ts("tab", [P, HCH, NTAB])
            big = {n: ts("g_" + n, [P, HCH, 35]) for n in ("arg", "k", "r", "s", "c", "e")}

            pieces = [("w", o) for o in range(KC)] + [("A", 0), ("r", 0), ("d", 0), ("u", 0), ("b", 0)]

            def tsem(name):
                return tmp.enter_context(nc.semaphore(name))

            s_ld = [tsem(f"s_ld{i}") for i in range(NS)]
            s_small, s_wt, s_hi, s_lo = tsem("s_small"), tsem("s_wt"), tsem("s_hi"), tsem("s_lo")
            s_pool, s_dve, s_act = tsem("s_pool"), tsem("s_dve"), tsem("s_act")
            s_zero, s_masks, s_consts = tsem("s_zero"), tsem("s_masks"), tsem("s_consts")
            s_dup, s_par, s_tdt, s_exps = tsem("s_dup"), tsem("s_par"), tsem("s_tdt"), tsem("s_exps")
            s_sg, s_om, s_trig = tsem("s_sg"), tsem("s_om"), tsem("s_trig")
            s_tab = tsem("s_tab")
            s_red, s_dec, s_sin, s_exp, s_kept = tsem("s_red"), tsem("s_dec"), tsem("s_sin"), tsem("s_exp"), tsem("s_kept")
            loaded, count = [], [0] * NS
            for n, (kind, _) in enumerate(pieces):
                count[n % NS] += 16 * (NE if kind == "b" else 1)
                loaded.append(count[n % NS])

            jobs = [([inw_s[:, 2, :], inw_s[:, 3, :]], P, wx[:, :].rearrange("p (a b) -> p a b", a=2), None, 1.0, -1),
                    ([inw_s[:, 0, :], inw_s[:, 1, :]], P, wz[:, :].rearrange("p (a b) -> p a b", a=2), None, 0.5, -1),
                    ([bc_s[0:BCP, :]], BCP, wbc[:, 0:BCP].unsqueeze(1), None, 1.0, -1),
                    ([dt_s[:, :]], 2 * NH, wbc[:, BCP:BCP + 2 * NH].unsqueeze(1), None, 1.0, -1),
                    ([fc_s[:, 0:P], fc_s[:, P:DIN]], NH, fcT[:, :, :], None, 1.0, -1),
                    ([ow_s[:, 0:P]], P, owT[:, 0:1, :], None, nw[:, 0:1], -1),
                    ([ow_s[:, P:DIN]], P, owT[:, 1:2, :], None, nw[:, 1:2], -1)]
            for n, (kind, o) in enumerate(pieces):
                rows = NR if kind == "r" else P
                for g in range(2):
                    ks = slice(4 * g, 4 * g + 4)
                    src = [stage[n % NS][0:rows, (4 * g + k) * P:(4 * g + k + 1) * P] for k in range(4)]
                    if kind in "wAr":
                        at = {"w": o * P, "A": HID, "r": HID + P}[kind]
                        jobs.append((src, rows, w_hi[:, ks, at:at + rows], w_lo[:, ks, at:at + rows], 1.0, n))
                    else:
                        dst = wdT[:, ks, :] if kind == "d" else \
                            (wuT if kind == "u" else lbT)[:, 512 * g:512 * g + 512].rearrange("p (a b) -> p a b", a=4)
                        jobs.append((src, rows, dst, None, 2.0 if kind == "b" else 1.0, n))
            splits = np.cumsum([j[3] is not None for j in jobs]).tolist()
            last_job = {j[5]: k for k, j in enumerate(jobs)}
            RING, SMALL_JOBS, PER_CHUNK = 4, 7, 2
            NSMALL = 29

            block = tmp.enter_context(nc.Block())

            @block.sync
            def _(sp):
                def small(dst, src):
                    sp.dma_start(dst, src).then_inc(s_small, 16)

                small(ai_s[:, :], A_imag)
                small(ar_s[:, :], inv_A_real)
                small(b_s[:, :, :], tok_B)
                small(ldt[:, :], log_dt.unsqueeze(0).broadcast_to([P, NHT]))
                small(inw_s[:, :, :], in_w[0:4 * P, :].rearrange("(a p) d -> p a d", p=P))
                small(dt_s[:, :], in_w[2 * DIN + 2 * DST:2 * DIN + 2 * DST + 2 * NH, :])
                small(fc_s[:, :], fcD_w)
                small(ow_s[:, :], out_w)
                small(nw[:, 0:1], norm_w[0:P].unsqueeze(1))
                small(nw[:, 1:2], norm_w[P:DIN].unsqueeze(1))
                cwr = conv_w.rearrange("c a k -> c (a k)")
                for c in range(2):
                    small(cw0[:, c, :], cwr[c * P:(c + 1) * P, :])
                    small(cb0[:, c:c + 1], conv_b[c * P:(c + 1) * P].unsqueeze(1))
                small(bup[:, :], b_up.unsqueeze(0).broadcast_to([P, HID]))
                small(bbase[:, :], base_b.unsqueeze(0).broadcast_to([P, HID]))
                small(rbias[:, :], router_b.unsqueeze(0).broadcast_to([P, NR]))
                small(emap[:, :], expert_map.unsqueeze(0).broadcast_to([P, NR]))
                small(dtb[:, :], dt_bias.unsqueeze(0).broadcast_to([P, NH]))
                small(alog[:, :], A_log.unsqueeze(0).broadcast_to([P, NH]))
                small(Dbc[:, :], hy_D.unsqueeze(0).broadcast_to([P, NH]))
                small(bdn[:, :], b_down.unsqueeze(1))
                small(gate[:, :], gate1.broadcast_to([P, 1]))
                sp.wait_ge(s_zero, 3)
                for k in range(2):
                    small(bc_s[32 * k:32 * k + DST, :], in_w[2 * DIN + DST * k:2 * DIN + DST * (k + 1), :])
                    small(cwb0[32 * k:32 * k + DST, :], cwr[DIN + DST * k:DIN + DST * (k + 1), :])
                    small(cbb0[32 * k:32 * k + DST, :], conv_b[DIN + DST * k:DIN + DST * (k + 1)].unsqueeze(1))

                for c in range(NHT // HCH):
                    sp.wait_ge(s_tab, c + 1)
                    sp.dma_start(tables[c * HCH // 2:(c + 1) * HCH // 2].rearrange("t f b k -> f t b k"),
                                 tab[:, :, :].rearrange("f (t b) k -> f t b k", b=2)).then_inc(s_kept, 16)
                sp.wait_ge(s_kept, 16 * (NHT // HCH))

            @block.gpsimd
            def _(pool):
                pool.memset(bc_s[:, :], 0.0).then_inc(s_zero, 1)
                pool.memset(cwb0[:, :], 0.0).then_inc(s_zero, 1)
                pool.memset(cbb0[:, :], 0.0).then_inc(s_zero, 1)
                pool.memset(ones[:, :], 1.0).then_inc(s_pool, 1)
                for t in (ident, earlier, later):
                    pool.memset(t[:, :], 0.0).then_inc(s_pool, 1)
                pool.wait_ge(s_pool, 4)
                pool.affine_select(out=ident[:, :], in_=ident[:, :], compare_op=ALU.not_equal, fill=1.0,
                                   base=0, pattern=[[-1, P]], channel_multiplier=1).then_inc(s_masks, 1)
                for b in range(2):
                    r = slice(CS * b, CS * (b + 1))
                    pool.wait_ge(s_masks, 1 + 4 * b)
                    for dst, cols, sign in ((earlier, r, 1), (later, r, -1), (m_gt, slice(0, CS), 1),
                                            (m_lt, slice(0, CS), -1)):
                        pool.affine_select(out=dst[r, cols], in_=ones[r, 0:CS], compare_op=ALU.is_gt, fill=0.0,
                                           base=0, pattern=[[-sign, CS]], channel_multiplier=sign).then_inc(s_masks, 1)
                pool.wait_ge(s_masks, 9)
                pool.affine_select(out=evm[:, :], in_=ones[:, 0:NST], compare_op=ALU.is_equal, fill=0.0,
                                   base=0, pattern=[[-2, NST]], channel_multiplier=1).then_inc(s_consts, 1)
                pool.iota(lst_i[:, 0:16], pattern=[[1, 16]], base=0, channel_multiplier=0).then_inc(s_consts, 1)
                pool.iota(lst_i[:, 16:32], pattern=[[16, 16]], base=0, channel_multiplier=0).then_inc(s_consts, 1)
                for k, s in enumerate((512, 256, 768)):
                    pool.iota(lst_i[:, 32 + k:33 + k], pattern=[[1, 1]], base=s,
                              channel_multiplier=0).then_inc(s_consts, 1)
                pool.memset(half_neg[:, :], -0.5)
                pool.memset(Mt[:, :, :, :], 0.0)
                pool.memset(GF[:, :, :], 0.0)
                pool.memset(GB[:, :, :], 0.0)
                pool.memset(U[:, :, :, :], 0.0)

            @block.tensor
            def _(pe):
                pe.wait_ge(s_masks, 1)
                pe.wait_ge(s_dup, 4)
                for k in range(4):
                    ins = pe.transpose(banks[7][:, k * P:(k + 1) * P], dup[:, k, :, :].rearrange("p a b -> p (a b)"),
                                       ident[:, :])
                ins.then_inc(s_par, 1)
                pe.wait_ge(s_small, 16 * NSMALL)
                for k, (src, m, _, lo, _, n) in enumerate(jobs):
                    if n >= 0:
                        pe.wait_ge(s_ld[n % NS], loaded[n])
                    if k >= RING:
                        pe.wait_ge(s_hi, k - RING + 1)
                        if splits[k - RING]:
                            pe.wait_ge(s_lo, splits[k - RING])
                    for c, a in enumerate(src):
                        ins = pe.transpose(banks[k % RING][:, c * m:(c + 1) * m], a, ident[0:m, 0:m])
                    ins.then_inc(s_wt, 1)

            @block.scalar
            def _(act):
                dram = {"w": lambda o: base_W[o * P:(o + 1) * P, :],
                        "A": lambda o: lora_A.rearrange("e r d -> (e r) d"),
                        "r": lambda o: router_W, "d": lambda o: w_down,
                        "u": lambda o: w_up.rearrange("(a p) d -> p a d", p=P)}

                def load(n):
                    kind, o = pieces[n]
                    st = stage[n % NS]
                    if n >= NS:
                        act.wait_ge(s_wt, last_job[n - NS] + 1)
                    if kind == "b":
                        st4 = st.rearrange("p (a e r) -> p a e r", a=KC, e=NE)
                        for e in range(NE):
                            act.dma_start(st4[:, :, e, :],
                                          lora_B[e].rearrange("(a p) r -> p a r", p=P)).then_inc(s_ld[n % NS], 16)
                        return
                    dst = st[0:NR, :] if kind == "r" else st
                    if kind == "u":
                        dst = st.rearrange("p (a d) -> p a d", a=KC)
                    act.dma_start(dst, dram[kind](o)).then_inc(s_ld[n % NS], 16)

                for n in range(NS):
                    load(n)
                act.wait_ge(s_small, 16 * NSMALL)
                act.activation(v["t0"][:, :], ldt[:, :], ACT.Tanh, scale=1.0 / 16).then_inc(s_tdt, 1)
                act.wait_ge(s_par, 1)
                act.activation(v["t1"][:, :], banks[7][:, P:2 * P], ACT.Exp).then_inc(s_exps, 1)
                act.activation(alog[:, :], alog[:, :], ACT.Exp).then_inc(s_exps, 1)
                act.activation(gt0[:, :], gate[:, :], ACT.Exp, scale=-1.0).then_inc(s_exps, 1)
                act.wait_ge(s_sg, 1)
                act.activation(v["t0"][:, :], v["sg"][:, :], ACT.Tanh, scale=0.5).then_inc(s_trig, 1)
                act.wait_ge(s_om, 1)
                act.activation(v["t2"][:, :], v["om"][:, :], ACT.Sin).then_inc(s_trig, 1)
                act.activation(v["t3"][:, :], v["om"][:, :], ACT.Sin, scale=0.5).then_inc(s_trig, 1)
                nxt, k = NS, 0

                def evacuate(k, nxt):
                    src, m, dst, lo, scale, n = jobs[k]
                    act.wait_ge(s_wt, k + 1)
                    cols = banks[k % RING][:, 0:len(src) * m].rearrange("p (a b) -> p a b", b=m)
                    act.activation(dst, cols, ACT.Copy, scale=scale).then_inc(s_hi, 1)
                    if n >= 0 and last_job[n] == k and nxt < len(pieces):
                        load(nxt)
                        nxt += 1
                    return nxt

                while k < SMALL_JOBS:
                    nxt = evacuate(k, nxt)
                    k += 1
                for c in range(NHT // HCH):
                    for _ in range(PER_CHUNK):
                        nxt = evacuate(k, nxt)
                        k += 1
                    act.wait_ge(s_red, c + 1)
                    act.activation(big["s"][:, :, :], big["r"][:, :, :], ACT.Sin).then_inc(s_sin, 1)
                    act.activation(big["c"][:, :, :], big["r"][:, :, :], ACT.Sin, scale=0.5).then_inc(s_sin, 1)
                    act.wait_ge(s_dec, c + 1)
                    act.activation(big["e"][:, :, :], big["arg"][:, :, :], ACT.Exp).then_inc(s_exp, 1)
                while k < len(jobs):
                    nxt = evacuate(k, nxt)
                    k += 1

            @block.vector
            def _(dve):
                cnt = [0]

                def link(ins):
                    cnt[0] += 1
                    ins.then_inc(s_dve, 1)
                    dve.wait_ge(s_dve, cnt[0])

                TT, TS, STT = dve.tensor_tensor, dve.tensor_scalar, dve.scalar_tensor_tensor
                V = {n: t[:, :] for n, t in v.items()}
                dve.wait_ge(s_small, 16 * NSMALL)
                for k, src in enumerate((ai_s[:, :], ar_s[:, :], b_s[:, :, 0], b_s[:, :, 1])):
                    dve.tensor_copy(dup[:, k, :, :], src.unsqueeze(2).broadcast_to([P, NST, 2])).then_inc(s_dup, 1)
                dve.wait_ge(s_consts, 6)
                link(dve.tensor_copy(lst[:, :], lst_i[:, :]))
                link(dve.tensor_reduce(evc[:, :], evm[:, :], AX.X, ALU.add))
                link(TS(odc[:, :], evc[:, :], -1.0, 1.0, ALU.mult, ALU.add))
                link(TT(sgn[:, :], odc[:, :], evc[:, :], ALU.subtract))
                dve.wait_ge(s_tdt, 1)
                link(TS(V["t2"], V["t0"], -1.0, 1.0, ALU.mult, ALU.add))
                link(dve.reciprocal(V["t3"], V["t2"]))
                link(STT(V["dt"], V["t0"], 1.0, V["t3"], ALU.add, ALU.mult))
                for _ in range(3):
                    link(TT(V["dt"], V["dt"], V["dt"], ALU.mult))
                dve.wait_ge(s_exps, 1)
                link(dve.tensor_copy(par[:, :, :], banks[7][:, :].rearrange("p (a b) -> p a b", a=4)))
                link(TS(V["ar"], V["t1"], -1.0, None, ALU.mult))
                TT(V["sg"], V["ar"], V["dt"], ALU.mult).then_inc(s_sg, 1)

                def reduce(arg, k, r):
                    c1 = 6.28125
                    c2 = float(np.floor((2 * np.pi - c1) * 2.0 ** 20) * 2.0 ** -20)
                    c3 = float(2 * np.pi - c1 - c2)
                    link(TS(k, arg, 0.5 / PI, ROUND, ALU.mult, ALU.add))
                    link(TS(k, k, ROUND, None, ALU.subtract))
                    link(STT(r, k, -c1, arg, ALU.mult, ALU.add))
                    link(STT(r, k, -c2, r, ALU.mult, ALU.add))
                    link(STT(r, k, -c3, r, ALU.mult, ALU.add))
                    return TS(r, r, 3.1415925, -3.1415925, ALU.min, ALU.max)

                ai, br, bi = par[:, 0, :], par[:, 2, :], par[:, 3, :]
                link(TT(V["t4"], ai, V["dt"], ALU.mult))
                reduce(V["t4"], V["er"], V["om"]).then_inc(s_om, 1)
                dve.wait_ge(s_trig, 3)
                link(TS(V["t1"], V["t0"], -1.0, 1.0, ALU.mult, ALU.add))
                link(dve.reciprocal(V["co"], V["t1"]))
                link(STT(V["t0"], V["t0"], 2.0, V["co"], ALU.mult, ALU.mult))
                link(TT(V["t3"], V["t3"], V["t3"], ALU.mult))
                link(TS(V["t3"], V["t3"], -2.0, None, ALU.mult))
                link(TS(V["co"], V["t3"], 1.0, None, ALU.add))
                link(TT(V["er"], V["t0"], V["co"], ALU.mult))
                link(TT(V["er"], V["er"], V["t3"], ALU.add))
                link(STT(V["ei"], V["t0"], 1.0, V["t2"], ALU.add, ALU.mult))
                link(TT(V["t1"], V["ar"], V["ar"], ALU.mult))
                link(TT(V["t0"], ai, ai, ALU.mult))
                link(TT(V["t1"], V["t1"], V["t0"], ALU.add))
                link(dve.reciprocal(V["t0"], V["t1"]))
                link(TT(V["t1"], V["er"], V["ar"], ALU.mult))
                link(TT(V["t2"], V["ei"], ai, ALU.mult))
                link(TT(V["t1"], V["t1"], V["t2"], ALU.add))
                link(TT(V["t2"], V["ei"], V["ar"], ALU.mult))
                link(TT(V["t3"], V["er"], ai, ALU.mult))
                link(TT(V["t2"], V["t2"], V["t3"], ALU.subtract))
                link(TT(V["t1"], V["t1"], V["t0"], ALU.mult))
                link(TT(V["t2"], V["t2"], V["t0"], ALU.mult))
                link(TT(V["t0"], bi, V["t2"], ALU.mult))
                link(TT(V["Gr"], br, V["t1"], ALU.mult))
                link(TT(V["Gr"], V["Gr"], V["t0"], ALU.subtract))
                link(TT(V["t0"], bi, V["t1"], ALU.mult))
                link(TT(V["Gi"], br, V["t2"], ALU.mult))
                link(TT(V["Gi"], V["Gi"], V["t0"], ALU.add))
                link(TS(V["t0"], V["Gi"], odc[:, 0:1], -2.0, ALU.mult, ALU.mult))
                link(TS(V["al"], V["Gr"], evc[:, 0:1], 2.0, ALU.mult, ALU.mult))
                link(TT(V["al"], V["al"], V["t0"], ALU.add))
                link(TS(V["t0"], V["Gi"], evc[:, 0:1], -2.0, ALU.mult, ALU.mult))
                link(TS(V["be"], V["Gr"], odc[:, 0:1], -2.0, ALU.mult, ALU.mult))
                link(TT(V["be"], V["be"], V["t0"], ALU.add))
                nlo = [0]

                def second_parts(n):
                    for k, (src, m, dst, lo, _, _) in enumerate(jobs):
                        if lo is None or k < nlo[0]:
                            continue
                        if n == 0:
                            return
                        n -= 1
                        nlo[0] = k + 1
                        dve.wait_ge(s_hi, k + 1)
                        cols = banks[k % RING][:, 0:len(src) * m].rearrange("p (a b) -> p a b", b=m)
                        TT(lo, cols, dst.bitcast(F32), ALU.subtract).then_inc(s_lo, 1)

                g = {n: t[:, :, :] for n, t in big.items()}
                NL = 35
                for c in range(NHT // HCH):
                    hs = slice(c * HCH, (c + 1) * HCH)

                    def per_h(t, n):
                        return t[:, hs].unsqueeze(2).broadcast_to([P, HCH, n])

                    L = lst[:, :].unsqueeze(1).broadcast_to([P, HCH, NL])
                    if c:
                        dve.wait_ge(s_exp, c)
                    link(TT(g["arg"], L, per_h(v["om"], NL), ALU.mult))
                    reduce(g["arg"], g["k"], g["r"]).then_inc(s_red, 1)
                    TT(g["arg"], L, per_h(v["sg"], NL), ALU.mult).then_inc(s_dec, 1)
                    second_parts(PER_CHUNK)
                    dve.wait_ge(s_sin, 2 * c + 2)
                    link(TT(g["c"], g["c"], g["c"], ALU.mult))
                    link(TS(g["c"], g["c"], -2.0, 1.0, ALU.mult, ALU.add))
                    dve.wait_ge(s_exp, c + 1)
                    link(TT(g["c"], g["c"], g["e"], ALU.mult))
                    link(TT(g["s"], g["s"], g["e"], ALU.mult))
                    Vr, Vi = g["c"][:, :, 0:16], g["s"][:, :, 0:16]
                    X1, X2 = g["k"][:, :, 0:16], g["r"][:, :, 0:16]
                    if c:
                        dve.wait_ge(s_kept, 16 * c)
                    link(TT(tab[:, :, TP], Vr, per_h(v["al"], 16), ALU.mult))
                    link(TT(X1, Vi, per_h(v["be"], 16), ALU.mult))
                    link(TT(tab[:, :, TP], tab[:, :, TP], X1, ALU.add))
                    link(TT(tab[:, :, TQ], Vr, per_h(v["be"], 16), ALU.mult))
                    link(TT(X2, Vi, per_h(v["al"], 16), ALU.mult))
                    link(TT(tab[:, :, TQ], tab[:, :, TQ], X2, ALU.subtract))
                    link(dve.tensor_copy(tab[:, :, TJR], g["c"][:, :, 16:32]))
                    link(dve.tensor_copy(tab[:, :, TJI], g["s"][:, :, 16:32]))
                    link(dve.tensor_copy(tab[:, :, TSR], g["c"][:, :, 32:35]))
                    TS(tab[:, :, TSI], g["s"][:, :, 32:35], sgn[:, 0:1], None, ALU.mult).then_inc(s_tab, 1)
                second_parts(1000)
                for dst, src in ((cw[:, :, :], cw0[:, :, :]), (cb[:, :], cb0[:, :]), (cwb[:, :], cwb0[:, :]),
                                 (cbb[:, :], cbb0[:, :])):
                    link(TS(dst, src, 0.5, None, ALU.mult))
                link(dve.tensor_copy(emf[:, :], emap[:, :]))
                for e in range(NE):
                    link(TS(onehot[:, e, :], emf[:, :], float(e), None, ALU.is_equal))
                dve.wait_ge(s_exps, 3)
                link(TS(negA[:, :], alog[:, :], -1.0, None, ALU.mult))
                link(TS(gate[:, :], gt0[:, :], 1.0, None, ALU.add))
                link(dve.reciprocal(al1[:, :], gate[:, :]))
                link(TS(be1[:, :], al1[:, :], -1.0, 1.0, ALU.mult, ALU.add))
                link(TS(al1[:, :], al1[:, :], 1.0, None, ALU.add))
                link(dve.memset(w_hi[:, :, FW - 1:FW].bitcast(F32), 0.0))
                link(dve.memset(w_lo[:, :, FW - 1:FW].bitcast(F32), 0.0))

        T2 = sb("T2", [P, HID])
        XM = sb("XM", [P, P])
        carried = nc.dram_tensor("carried", (TILES, P, HID + P), F32, kind="Internal").ap()
        H0 = sb("H0", [P, HID])
        XHT = sb("XHT", [P, KC, P])
        XI = sb("XI", [P, 2, P])
        TB = sb("TB", [P, 2, 2, NTAB])
        XSW = sb("XSW", [P, NST, 2])
        XTC = sb("XTC", [P, 2, 2, CS])
        W = sb("W", [P, 2, 4, CS])
        WI = sb("WI", [P, 2, 3, CS])
        VB = sb("VB", [P, 2, 16, 16])
        V2 = sb("V2", [P, 2, 16, 16])
        ST1 = sb("ST1", [P, 2, 6])
        MV1 = sb("MV1", [P, 2])
        VE1 = sb("VE1", [P, 1])
        RS1 = sb("RS1", [P, 1])
        SD1 = sb("SD1", [P, 1])
        CX = sb("CX", [P, 2, 4, CS])
        CB = sb("CB", [BCP, 4, CS])
        TH = sb("TH", [P, 2 * 4 * CS])
        THB = sb("THB", [BCP, 4 * CS])
        BT = sb("BT", [DST, 4 * CS])
        CT = sb("CT", [DST, 4 * CS])
        SZ = sb("SZ", [P, 512])
        XS = TH
        SQ = sb("SQ", [P, 256])
        RF = sb("RF", [P, 2 * NH, CS])
        RB = sb("RB", [P, 2 * NH, CS])
        EX, NB = RF, RB
        NF = sb("NF", [P, 2 * NH, CS])
        YT = NF
        XD = sb("XD", [P, 2 * NH, HD])
        XMA = sb("XMA", [P, P])
        GT = sb("GT", [P, P])
        SP16 = {n: sb("sp_" + n, [P, 2, 2, NH]) for n in ("x", "a", "u", "z", "w", "p", "dt", "aa")}
        DD = sb("DD", [P, 2 * NH])
        SSQ = sb("SSQ", [P, 2])
        MS = sb("MS", [P, 2])
        RS = sb("RS", [P, 2])
        ST2 = sb("ST2", [P, 2, 6])
        MV2 = sb("MV2", [P, 2])
        VE2 = sb("VE2", [P, 1])
        RS2 = sb("RS2", [P, 1])
        XHI = sb("XHI", [P, 2, KC, P], F32R)
        XLO = sb("XLO", [P, 2, KC, P], F32R)
        LG = sb("LG", [P, NR])
        NM = sb("NM", [P, 1])
        EL = sb("EL", [P, NR])
        SE = sb("SE", [P, 1])
        RE = sb("RE", [P, 1])
        PR = sb("PR", [P, NR])
        P8 = sb("P8", [P, 8])
        PQ = sb("PQ", [P, NR])
        PW = sb("PW", [P, NE, NR])
        WE = sb("WE", [P, NE])
        HW = sb("HW", [P, P])
        HWT = sb("HWT", [P, P])
        bO = banks[0:2]
        bR = banks[2]
        bK = banks[3]
        bT = banks[4]
        bX, bY, bZ = banks[5], banks[6], banks[7]
        FC0 = 4 * CS + 16

        NCONV, NDT, NSM = 3 * TAPS, 18, 9
        per = dict(cls_in=(1, 16), xswap=2, xt=1, xtc=1, wr=1, wi=2, wsum=1, v1=1, v2=1, vsum=1,
                   km=2, hev=4, st1=4, rs1=1, sd1=1, xh1=1, tt=2, tr1=2, xte=2, down=1, gelu=1,
                   pin=3, xms=1, conv=NCONV, dtc=NDT, edt=1, th=2, xs=3, thz=1, sz=1, trx=1, gram=1, xse=1,
                   rf=1, rb=1, seg=1, ex=1, g4=4, dd=1, nf=1, nb=1, ns=1, mm=2, xd=1, yy=1, y1=1, yz=1, sq=2,
                   ms=1, rs=1, yn=2, tyn=1, yte=1, outp=1, u2=1, gt=1,
                   fetched=(2, 16), up=2, h1=2, st2=4, rs2=1, hb=1, xh2=1, tr2=2, xhi=2, xlo=2,
                   rt=1, sm=NSM, se=1, hw=1, trh=1, hwe=1, o=2, fin=2)
        S = {}
        for n, c in per.items():
            c, unit = c if isinstance(c, tuple) else (c, 1)
            S[n] = Step(sem(n), c, unit)

        x_in = [sem("x_in_even"), sem("x_in_odd")]
        stored = [sem("stored_even"), sem("stored_odd")]
        carry = [sem("carry_even"), sem("carry_odd")]

        def wait_x(eng, i, p):
            eng.wait_ge(x_in[p], (i - p) * 24 + 48)

        def wait_carry(eng, t, p):
            if not (isinstance(t, int) and t < 0):
                eng.wait_ge(carry[p], (t - p) * 16 + 32)

        def wait_stored(eng, t, p):
            if not (isinstance(t, int) and t < 0):
                eng.wait_ge(stored[p], (t - p) * 16 + 32)

        def inc(ins, name):
            ins.then_inc(S[name].sem, S[name].unit)

        def wait(eng, n, **at):
            for name, j in at.items():
                S[name].after(eng, n, j)

        def apart(eng):
            eng.nop(nofuse=True)

        def active(i, lag, count):
            return (not isinstance(i, int)) or 0 <= i - lag < count

        def v3(ap, b):
            return ap.rearrange("p (a b) -> p a b", b=b)

        def decays(d):
            return SP16["aa"][:, d, :, :].rearrange("p a h -> p (a h)").unsqueeze(2).broadcast_to([P, 2 * NH, CS])

        LOOP_FROM, LOOP_TO, LAST = 8, CLS - 2, TILES + 5
        assert CLS % 2 == 0 and LOOP_TO > LOOP_FROM

        def iterations(eng, body):
            for i in range(LOOP_FROM):
                body(i, i % 2)
            with eng.Fori(LOOP_FROM, LOOP_TO, 2) as m:
                for u in range(2):
                    body(m + u, u)
            for i in range(LOOP_TO, LAST):
                body(i, i % 2)

        with nc.Block() as block:

            @block.sync
            def _(sp):
                def body(i, p):
                    if isinstance(i, int) and i == 0:
                        load_x(0, 0)
                    if active(i, -1, CLS + 1) and not (isinstance(i, int) and i + 1 >= CLS):
                        load_x(i + 1, 1 - p)
                    if isinstance(i, int) and i == CLS:
                        wait(sp, i - 1, tr1=2, tt=2)
                        sp.dma_start(H0[:, :], cls_tok[0].broadcast_to([P, HID])).then_inc(S["cls_in"].sem, 16)
                    if active(i, 5, TILES):
                        store(i - 5, 1 - p)
                    if active(i, 3, TILES):
                        src = at(carried, i - 3)
                        wait_carry(sp, i - 3, 1 - p)
                        wait(sp, i - 4, tr2=2)
                        apart(sp)
                        wait(sp, i - 4, hb=1, gt=1)
                        apart(sp)
                        inc(sp.dma_start(T2[:, :], src[:, 0:HID]), "fetched")
                        inc(sp.dma_start(XM[:, :], src[:, HID:HID + P]), "fetched")
                    if active(i, 0, TILES):
                        dst = at(carried, i)
                        wait(sp, i, gelu=1)
                        apart(sp)
                        sp.dma_start(dst[:, HID:HID + P], U[:, p, 0, :]).then_inc(carry[p], 16)
                        wait(sp, i, tt=2)
                        apart(sp)
                        sp.dma_start(dst[:, 0:HID], T[:, p, :]).then_inc(carry[p], 16)

                def at(dram, t):
                    return dram[t] if isinstance(t, int) else dram[bass.ds(t, 1)].rearrange("a f k -> (a f) k")

                def load_x(t, p):
                    wait(sp, t - 2, xt=1, xswap=2, v1=1, wr=1, v2=1, wi=2)
                    apart(sp)
                    tb = tables[t] if isinstance(t, int) else tables[bass.ds(t, 1)].rearrange("a f b k -> (a f) b k")
                    sp.dma_start(TB[:, p, :, :], tb).then_inc(x_in[p], 16)
                    for b in range(2):
                        h = t * 2 + b
                        src = x[:, h, :, :].rearrange("c n r -> c (n r)") if isinstance(t, int) \
                            else x[:, bass.ds(h, 1), :, :].rearrange("c a n r -> c (a n r)")
                        sp.dma_start(XI[CS * b:CS * (b + 1), p, :], src).then_inc(x_in[p], 16)

                def store(t, p):
                    wait(sp, t, fin=2)
                    apart(sp)
                    if isinstance(t, int) and t == CLS:
                        sp.dma_start(out[:, 0, :], HB[0:CS, p, :]).then_inc(stored[p], 16)
                        return
                    for b in range(2):
                        row = t * 2 + b + 1
                        dst = out[:, row, :] if isinstance(t, int) else out[:, bass.ds(row, 1), :].rearrange("c a d -> c (a d)")
                        sp.dma_start(dst, HB[CS * b:CS * (b + 1), p, :]).then_inc(stored[p], 16)

                iterations(sp, body)
                sp.wait_ge(stored[0], 16 * (CLS + 1))
                sp.wait_ge(stored[1], 16 * CLS)

            @block.gpsimd
            def _(pool):
                def body(i, p):
                    A, A1, D = active(i, 0, CLS), active(i, 0, TILES), active(i, 4, TILES)
                    H, G = active(i, 1, TILES + 2), active(i, 2, TILES + 2)
                    q, r, td = i - 1, i - 2, i - 4

                    def swap(k):
                        if A:
                            wait_x(pool, i, p)
                            wait(pool, i - 1, xt=1)
                            apart(pool)
                            xi = XI[:, p, :].rearrange("p (n r) -> p n r", r=2)
                            inc(pool.tensor_copy(XSW[:, :, k], xi[:, :, 1 - k]), "xswap")

                    def kernel_q():
                        if A:
                            wait_x(pool, i, p)
                            wait(pool, i - 1, vsum=1)
                            inc(pool.tensor_tensor(V2[:, :, :, :], TB[:, p, :, TQ].unsqueeze(2).broadcast_to([P, 2, 16, 16]),
                                                   TB[:, p, :, TJI].unsqueeze(3).broadcast_to([P, 2, 16, 16]), ALU.mult), "v2")

                    def shift_imag():
                        if A:
                            wait(pool, i, xtc=1)
                            wait(pool, i - 1, wsum=1)
                            inc(pool.tensor_tensor(WI[:, :, :, :], XTC[:, 1, :, :].unsqueeze(2).broadcast_to([P, 2, 3, CS]),
                                                   TB[:, p, :, TSI].unsqueeze(3).broadcast_to([P, 2, 3, CS]), ALU.mult), "wi")

                    def shift_none():
                        if A:
                            wait(pool, i, xtc=1)
                            wait(pool, i - 1, km=2)
                            apart(pool)
                            inc(pool.tensor_copy(W[:, :, 0, :], XTC[:, 0, :, :]), "wi")

                    def gram_back():
                        if G:
                            wait(pool, r, seg=1, g4=4)
                            dtB = SP16["dt"][:, 1, :, :].unsqueeze(3).broadcast_to([P, 2, NH, CS])
                            inc(pool.tensor_tensor(NB[:, :, :].rearrange("p (a h) t -> p a h t", a=2),
                                                   GB[:, :, :].unsqueeze(2).broadcast_to([P, 2, NH, CS]), dtB, ALU.mult), "nb")

                    def skip():
                        if G:
                            wait(pool, r, xse=1, dd=1)
                            wait(pool, r - 1, yn=2, tyn=1)
                            inc(pool.tensor_tensor(XD[:, :, :], v3(XS[:, :], HD),
                                                   DD[:, :].unsqueeze(2).broadcast_to([P, 2 * NH, HD]), ALU.mult), "xd")

                    def root_y():
                        if G:
                            wait(pool, r, ms=1)
                            wait(pool, r - 1, yn=2)
                            inc(pool.tensor_tensor(RS[:, :], MS[:, :], half_neg[:, :], ALU.pow), "rs")

                    def root_1():
                        if A1:
                            wait(pool, i, st1=4)
                            wait(pool, i - 1, xh1=1, sd1=1)
                            inc(pool.tensor_tensor(RS1[:, :], VE1[:, :], half_neg[:, 0:1], ALU.pow), "rs1")

                    def root_2():
                        if D:
                            wait(pool, td, st2=4)
                            wait(pool, td - 1, xh2=1)
                            inc(pool.tensor_tensor(RS2[:, :], VE2[:, :], half_neg[:, 0:1], ALU.pow), "rs2")

                    def start_out():
                        if D:
                            wait(pool, td, h1=2)
                            wait_stored(pool, td - 2, p)
                            inc(pool.tensor_tensor(HB[:, p, :], T2[:, :], bbase[:, :], ALU.add), "hb")

                    def decays_back():
                        if H:
                            wait(pool, q, dtc=NDT)
                            wait(pool, r, ns=1)
                            inc(pool.tensor_tensor(RB[:, :, :], m_gt[:, :].unsqueeze(1).broadcast_to([P, 2 * NH, CS]),
                                                   decays(1), ALU.mult), "rb")

                    def carry_h():
                        if A1:
                            wait(pool, i, sd1=1, xh1=1)
                            wait_carry(pool, i - 2, p)
                            apart(pool)
                            inc(pool.tensor_scalar(T[:, p, :], H0[:, :], SD1[:, 0:1], MV1[:, 0:1], ALU.mult, ALU.add), "tt")

                    def carry_bias():
                        if A1:
                            wait(pool, i, tt=1)
                            inc(pool.tensor_tensor(T[:, p, :], T[:, p, :], bup[:, :], ALU.add), "tt")

                    swap(0)
                    swap(1)
                    gram_back()
                    kernel_q()
                    skip()
                    shift_imag()
                    shift_none()
                    root_y()
                    root_1()
                    carry_h()
                    start_out()
                    root_2()
                    carry_bias()
                    decays_back()

                iterations(pool, body)

            @block.scalar
            def _(act):
                def copy(dst, src, name, scale=1.0):
                    inc(act.activation(dst, src, ACT.Copy, scale=scale), name)

                def body(i, p):
                    A, A1 = active(i, 0, CLS), active(i, 0, TILES)
                    D, E = active(i, 4, TILES), active(i, 5, TILES)
                    H, G = active(i, 1, TILES + 2), active(i, 2, TILES + 2)
                    q, r, td, te = i - 1, i - 2, i - 4, i - 5

                    def keep_x():
                        if A:
                            wait(act, i, xt=1)
                            wait(act, i - 1, wr=1, wi=2)
                            copy(XTC[:, :, :, :].rearrange("p a b c -> p (a b c)"), bK[:, 0:256], "xtc")

                    def keep_xs():
                        if G:
                            wait(act, r, trx=1, xs=3)
                            wait(act, r - 1, xd=1)
                            copy(XS[:, :], bX[:, :], "xse")

                    def exp_decays():
                        if G:
                            wait(act, r, seg=1)
                            inc(act.activation(EX[:, :, :].rearrange("p a b -> p (a b)"), bZ[:, :], ACT.Exp), "ex")

                    def keep_h(b, h):
                        if A:
                            wait(act, i, km=b + 1)
                            wait(act, i - 1, tr1=2, tt=2)
                            copy(H0[CS * b:CS * (b + 1), HALF * h:HALF * (h + 1)], bK[CS * h:CS * (h + 1), :], "hev")

                    def exp_router():
                        if E:
                            wait(act, te, sm=2)
                            wait(act, te - 1, sm=NSM)
                            inc(act.activation(EL[:, :], LG[:, :], ACT.Exp, bias=NM[:, 0:1], accum_out=SE[:, 0:1]), "se")

                    def squares(a):
                        if G:
                            wait(act, r, yz=1)
                            wait(act, r - 1, ms=1)
                            if a:
                                wait(act, r, sq=1)
                            inc(act.activation(SQ[:, :], v3(XD[:, :, :].rearrange("p a b -> p (a b)"), 256)[:, a, :],
                                               ACT.Square, accum_out=SSQ[:, a:a + 1]), "sq")

                    def keep_y():
                        if G:
                            wait(act, r, tyn=1, mm=2)
                            wait(act, r - 1, outp=1)
                            copy(YT[:, :, :].rearrange("p a b -> p (a b)"), bZ[:, :], "yte")

                    def keep_w():
                        if E:
                            wait(act, te, trh=1)
                            wait(act, te - 1, o=2)
                            copy(HWT[:, :], bR[:, 256:384], "hwe")

                    def exp_dt():
                        if H:
                            wait(act, q, dtc=2)
                            inc(act.activation(SP16["u"][:, :, :, :], SP16["a"][:, :, :, :], ACT.Exp), "edt")

                    def tanh_z():
                        if H:
                            wait(act, q, pin=3)
                            wait(act, r, yz=1)
                            inc(act.activation(SZ[:, :], bZ[:, :], ACT.Tanh), "thz")

                    def keep_turned(g):
                        if A1:
                            wait(act, i, tr1=g + 1)
                            wait(act, i - 1, down=1)
                            copy(XHT[:, 4 * g:4 * g + 4, :], v3(bT[:, :], P), "xte")

                    def tanh_x():
                        if H:
                            wait(act, q, conv=NCONV)
                            wait(act, r, yy=1, xd=1)
                            inc(act.activation(TH[:, :], CX[:, :, :, :].rearrange("p a b c -> p (a b c)"), ACT.Tanh), "th")

                    def tanh_bc():
                        if H:
                            wait(act, q, conv=NCONV)
                            wait(act, r, xs=3)
                            inc(act.activation(THB[:, :], CB[:, :, :].rearrange("p b c -> p (b c)"), ACT.Tanh), "th")

                    def split_hi(g):
                        if D:
                            wait(act, td, tr2=g + 1)
                            wait(act, td - 2, o=2)
                            copy(XHI[:, p, 4 * g:4 * g + 4, :], v3(bT[:, :], P), "xhi")

                    def gelu():
                        if A1:
                            wait(act, i, down=1)
                            wait(act, i - 2, pin=3)
                            wait_carry(act, i - 2, p)
                            inc(act.activation(U[:, p, 0, :], bK[:, 0:P], ACT.Gelu, bias=bdn[:, 0:1]), "gelu")

                    exp_decays()
                    keep_xs()
                    keep_x()
                    exp_router()
                    squares(0)
                    squares(1)
                    keep_h(0, 0)
                    keep_h(0, 1)
                    keep_h(1, 0)
                    keep_h(1, 1)
                    keep_y()
                    exp_dt()
                    keep_w()
                    keep_turned(0)
                    keep_turned(1)
                    split_hi(0)
                    tanh_z()
                    tanh_x()
                    tanh_bc()
                    gelu()
                    split_hi(1)

                iterations(act, body)

            @block.vector
            def _(dve):
                TT, TS, STT = dve.tensor_tensor, dve.tensor_scalar, dve.scalar_tensor_tensor

                def body(i, p):
                    A, A1 = active(i, 0, CLS), active(i, 0, TILES)
                    D, E = active(i, 4, TILES), active(i, 5, TILES)
                    H, G = active(i, 1, TILES + 2), active(i, 2, TILES + 2)
                    q, r, td, te = i - 1, i - 2, i - 4, i - 5
                    xd = XD[:, :, :].rearrange("p a b -> p (a b)")

                    def conv(s, c):
                        if not H:
                            return
                        hx = bX[:, :].rearrange("p (c g t) -> p c g t", c=2, g=4)
                        hb = bY[0:BCP, 0:256].rearrange("p (g t) -> p g t", g=4)
                        dst, src, w, bias = ((CX[:, 0], hx[:, 0], cw[:, 0], cb[:, 0:1]),
                                             (CX[:, 1], hx[:, 1], cw[:, 1], cb[:, 1:2]),
                                             (CB[:, :, :], hb, cwb[:, :], cbb[:, 0:1]))[c]
                        k = TAPS - 1 - s
                        if s == 0:
                            wait(dve, q, pin=1 if c < 2 else 2)
                            wait(dve, q - 1, trx=1, gram=1)
                            inc(TS(dst, src, w[:, k:k + 1], bias, ALU.mult, ALU.add), "conv")
                        else:
                            wait(dve, q, conv=3 * (s - 1) + c + 1)
                            inc(STT(dst[:, :, s:CS], src[:, :, 0:CS - s], w[:, k:k + 1], dst[:, :, s:CS],
                                    ALU.mult, ALU.add), "conv")

                    def softplus(j):
                        if not H:
                            return
                        f = {n: t[:, :, :, :] for n, t in SP16.items()}
                        if j > 0:
                            wait(dve, q, dtc=j)
                        if j == 0:
                            wait(dve, q, pin=2)
                            wait(dve, q - 1, rb=1, nb=1)
                            ins = TT(f["x"], bY[:, 256:272].rearrange("p (a d h) -> p d a h", a=2, d=2),
                                     dtb[:, :].unsqueeze(1).unsqueeze(1).broadcast_to([P, 2, 2, NH]), ALU.add)
                        elif j == 1:
                            wait(dve, q - 1, edt=1)
                            ins = STT(f["a"], f["x"], -1.0, f["x"], ALU.mult, ALU.min)
                        elif j == 2:
                            wait(dve, q, edt=1)
                            ins = TS(f["z"], f["u"], 2.0, None, ALU.add)
                        elif j == 3:
                            ins = dve.reciprocal(f["w"], f["z"])
                        elif j == 4:
                            ins = TT(f["z"], f["u"], f["w"], ALU.mult)
                        elif j == 5:
                            ins = TT(f["w"], f["z"], f["z"], ALU.mult)
                        elif j == 6:
                            ins = TS(f["p"], f["w"], 1.0 / 17, None, ALU.mult)
                        elif j < 14:
                            ins = STT(f["p"], f["p"], 1.0 / (29 - 2 * j), f["w"], ALU.add, ALU.mult)
                        elif j == 14:
                            ins = STT(f["p"], f["p"], 1.0, f["z"], ALU.add, ALU.mult)
                        elif j == 15:
                            ins = TS(f["x"], f["x"], 0.0, None, ALU.max)
                        elif j == 16:
                            wait(dve, q - 1, nb=1, rb=1)
                            ins = STT(f["dt"], f["p"], 2.0, f["x"], ALU.mult, ALU.add)
                        elif j == 17:
                            ins = TT(f["aa"], f["dt"],
                                     negA[:, :].unsqueeze(1).unsqueeze(1).broadcast_to([P, 2, 2, NH]), ALU.mult)
                        inc(ins, "dtc")

                    def kernel_p():
                        if A:
                            wait_x(dve, i, p)
                            wait(dve, i - 1, km=2)
                            inc(TT(VB[:, :, :, :], TB[:, p, :, TP].unsqueeze(2).broadcast_to([P, 2, 16, 16]),
                                   TB[:, p, :, TJR].unsqueeze(3).broadcast_to([P, 2, 16, 16]), ALU.mult), "v1")

                    def kernel_sum():
                        if A:
                            wait(dve, i, v2=1, v1=1)
                            inc(TT(VB[:, :, :, :], VB[:, :, :, :], V2[:, :, :, :], ALU.add), "vsum")

                    def shift_real():
                        if A:
                            wait(dve, i, xtc=1)
                            wait(dve, i - 1, km=2)
                            inc(TT(W[:, :, 1:4, :], XTC[:, 0, :, :].unsqueeze(2).broadcast_to([P, 2, 3, CS]),
                                   TB[:, p, :, TSR].unsqueeze(3).broadcast_to([P, 2, 3, CS]), ALU.mult), "wr")

                    def shift_sum():
                        if A:
                            wait(dve, i, wi=1, wr=1)
                            inc(TT(W[:, :, 1:4, :], W[:, :, 1:4, :], WI[:, :, :, :], ALU.add), "wsum")

                    def gram(b, d):
                        if G:
                            wait(dve, r, gram=1)
                            wait(dve, r - 1, nb=1, nf=1)
                            rows = slice(CS * b, CS * (b + 1))
                            gr = bY[rows, 0:256].rearrange("p (a c) -> p a c", a=2)
                            if d == 0:
                                ins = TT(GF[rows, :, 1:CS], gr[:, :, CS * b:CS * b + CS - 1],
                                         m_lt[rows, 1:CS].unsqueeze(1).broadcast_to([CS, 2, CS - 1]), ALU.mult)
                            else:
                                ins = TT(GB[rows, :, 0:CS - 1], gr[:, :, CS * b + 1:CS * b + CS],
                                         m_gt[rows, 0:CS - 1].unsqueeze(1).broadcast_to([CS, 2, CS - 1]), ALU.mult)
                            inc(ins, "g4")

                    def skip_scale():
                        if G:
                            wait(dve, r, gram=1)
                            wait(dve, r - 1, xd=1)
                            inc(TT(DD[:, :].rearrange("p (a h) -> p a h", a=2), v3(bY[:, FC0:FC0 + 2 * NH], NH),
                                   Dbc[:, :].unsqueeze(1).broadcast_to([P, 2, NH]), ALU.add), "dd")

                    def gram_forth():
                        if G:
                            wait(dve, r, g4=4)
                            wait(dve, r - 1, outp=1, mm=2)
                            dtF = SP16["dt"][:, 0, :, :].unsqueeze(3).broadcast_to([P, 2, NH, CS])
                            inc(TT(NF[:, :, :].rearrange("p (a h) t -> p a h t", a=2),
                                   GF[:, :, :].unsqueeze(2).broadcast_to([P, 2, NH, CS]), dtF, ALU.mult), "nf")

                    def gram_sum():
                        if G:
                            wait(dve, r, nf=1, nb=1)
                            inc(TT(NF[:, :, :], NF[:, :, :], NB[:, :, :], ALU.add), "ns")

                    def mix_matrix(b):
                        if G:
                            wait(dve, r, ns=1, ex=1)
                            wait(dve, r - 1, yy=1)
                            rows = slice(CS * b, CS * (b + 1))
                            inc(TT(Mt[rows, :, :, rows].rearrange("p a h t -> p (a h) t"), NF[rows, :, :], EX[rows, :, :],
                                   ALU.mult), "mm")

                    def add_skip():
                        if G:
                            wait(dve, r, yy=1, xd=1)
                            inc(TT(xd, bX[:, :], xd, ALU.add), "y1")

                    def times_z():
                        if G:
                            wait(dve, r, y1=1, sz=1)
                            inc(TT(xd, xd, SZ[:, :], ALU.mult), "yz")

                    def mean_square():
                        if G:
                            wait(dve, r, sq=2)
                            wait(dve, r - 1, rs=1)
                            inc(TS(MS[:, :], SSQ[:, :], 1.0 / DIN, EPS, ALU.mult, ALU.add), "ms")

                    def norm_y(a):
                        if G:
                            wait(dve, r, rs=1)
                            ya = v3(xd, 256)[:, a, :]
                            inc(TS(ya, ya, RS[:, a:a + 1], None, ALU.mult), "yn")

                    def layer_out():
                        if G:
                            wait(dve, r, outp=1)
                            wait(dve, r - 1, pin=3)
                            inc(dve.tensor_copy(U[:, p, 1, :], bY[:, 0:P]), "u2")

                    def router(j):
                        if not E:
                            return
                        if j:
                            wait(dve, te, sm=j)
                        if j == 0:
                            wait(dve, te, rt=1)
                            wait(dve, te - 1, se=1)
                            inc(TT(LG[:, :], bR[:, P:P + NR], rbias[:, :], ALU.add), "sm")
                        elif j == 1:
                            wait(dve, te - 1, se=1)
                            inc(dve.tensor_reduce(NM[:, :], LG[:, :], AX.X, ALU.max, negate=True), "sm")
                        elif j == 2:
                            wait(dve, te, se=1)
                            inc(dve.reciprocal(RE[:, :], SE[:, :]), "sm")
                        elif j == 3:
                            inc(TS(PR[:, :], EL[:, :], RE[:, 0:1], None, ALU.mult), "sm")
                        elif j == 4:
                            apart(dve)
                            inc(dve.max(P8[:, :], PR[:, :]), "sm")
                        elif j == 5:
                            apart(dve)
                            inc(dve.match_replace(PQ[:, :], P8[:, :], PR[:, :], 0.0), "sm")
                        elif j == 6:
                            inc(TT(PQ[:, :], PR[:, :], PQ[:, :], ALU.subtract), "sm")
                        elif j == 7:
                            inc(TT(PW[:, :, :], onehot[:, :, :], PQ[:, :].unsqueeze(1).broadcast_to([P, NE, NR]),
                                   ALU.mult), "sm")
                        elif j == 8:
                            inc(dve.tensor_reduce(WE[:, :], PW[:, :, :], AX.X, ALU.add), "sm")
                        elif j == 9:
                            wait(dve, te - 1, trh=1)
                            inc(TT(HW[:, :].rearrange("p (e r) -> p e r", e=NE), bR[:, 0:P].rearrange("p (e r) -> p e r", e=NE),
                                   WE[:, :].unsqueeze(2).broadcast_to([P, NE, RK]), ALU.mult), "hw")

                    def stats_1(j):
                        if not A1:
                            return
                        if j < 2:
                            if isinstance(i, int) and i == CLS:
                                dve.wait_ge(S["cls_in"].sem, 16)
                            else:
                                wait(dve, i, hev=4)
                            inc(dve.bn_stats(ST1[:, j, :], H0[:, HALF * j:HALF * (j + 1)]), "st1")
                        elif j == 2:
                            wait(dve, i, st1=2)
                            wait(dve, i - 1, tt=2)
                            apart(dve)
                            inc(dve.bn_aggr(MV1[:, :], ST1[:, :, :].rearrange("p a b -> p (a b)")), "st1")
                        else:
                            wait(dve, i, st1=3)
                            inc(TS(VE1[:, :], MV1[:, 1:2], EPS, None, ALU.add), "st1")

                    def norm_1():
                        if A1:
                            wait(dve, i, rs1=1)
                            inc(TS(H0[:, :], H0[:, :], MV1[:, 0:1], RS1[:, 0:1], ALU.subtract, ALU.mult), "xh1")

                    def deviation_1():
                        if A1:
                            wait(dve, i, rs1=1)
                            wait(dve, i - 1, tt=1)
                            inc(TS(SD1[:, :], VE1[:, :], RS1[:, 0:1], 1.0, ALU.mult, ALU.add), "sd1")

                    def gated_a():
                        if D:
                            wait(dve, td, fetched=2)
                            inc(TS(XMA[:, :], XM[:, :], al1[:, 0:1], None, ALU.mult), "xms")

                    def gated_b():
                        if D:
                            wait(dve, td, xms=1)
                            wait(dve, r, outp=1)
                            wait(dve, td - 1, up=2)
                            inc(STT(GT[:, :], bY[:, P:2 * P], be1[:, 0:1], XMA[:, :], ALU.mult, ALU.add), "gt")

                    def residual(h):
                        if D:
                            wait(dve, td, up=h + 1, fetched=2)
                            c = slice(HALF * h, HALF * (h + 1))
                            inc(TT(T2[:, c], bT[:, :], T2[:, c], ALU.add), "h1")

                    def stats_2(j):
                        if not D:
                            return
                        if j < 2:
                            wait(dve, td, h1=j + 1)
                            inc(dve.bn_stats(ST2[:, j, :], T2[:, HALF * j:HALF * (j + 1)]), "st2")
                        elif j == 2:
                            wait(dve, td, st2=2)
                            apart(dve)
                            inc(dve.bn_aggr(MV2[:, :], ST2[:, :, :].rearrange("p a b -> p (a b)")), "st2")
                        else:
                            wait(dve, td, st2=3)
                            inc(TS(VE2[:, :], MV2[:, 1:2], EPS, None, ALU.add), "st2")

                    def norm_2():
                        if D:
                            wait(dve, td, rs2=1, hb=1)
                            inc(TS(T2[:, :], T2[:, :], MV2[:, 0:1], RS2[:, 0:1], ALU.subtract, ALU.mult), "xh2")

                    def split_lo(g):
                        if D:
                            wait(dve, td, xhi=g + 1)
                            wait(dve, td - 2, o=2)
                            ks = slice(4 * g, 4 * g + 4)
                            inc(TT(XLO[:, p, ks, :], v3(bT[:, :], P), XHI[:, p, ks, :].bitcast(F32), ALU.subtract), "xlo")

                    def silu_z():
                        if H:
                            wait(dve, q, thz=1, pin=3)
                            inc(STT(SZ[:, :], SZ[:, :], 1.0, bZ[:, :], ALU.add, ALU.mult), "sz")

                    def decays_forth():
                        if H:
                            wait(dve, q, dtc=NDT)
                            wait(dve, r, seg=1, mm=2)
                            inc(TT(RF[:, :, :], m_lt[:, :].unsqueeze(1).broadcast_to([P, 2 * NH, CS]), decays(0),
                                   ALU.mult), "rf")

                    def silu_x():
                        if H:
                            wait(dve, q, th=1)
                            wait(dve, r, trx=1, gram=1)
                            cx = CX[:, :, :, :].rearrange("p a b c -> p (a b c)")
                            inc(STT(cx, TH[:, :], 1.0, cx, ALU.add, ALU.mult), "xs")

                    def silu_bc(k):
                        if H:
                            wait(dve, q, th=2)
                            wait(dve, r, gram=1)
                            cbf = CB[:, :, :].rearrange("p b c -> p (b c)")
                            n = slice(32 * k, 32 * k + DST)
                            inc(STT((BT, CT)[k][:, :], THB[n, :], 1.0, cbf[n, :], ALU.add, ALU.mult), "xs")

                    def final(h):
                        if E:
                            wait(dve, te, o=h + 1, hb=1)
                            c = slice(HALF * h, HALF * (h + 1))
                            inc(TT(HB[:, 1 - p, c], bO[h][:, :], HB[:, 1 - p, c], ALU.add), "fin")

                    gram(0, 0)
                    skip_scale()
                    gram(0, 1)
                    gram(1, 0)
                    gram(1, 1)
                    kernel_p()
                    gram_forth()
                    gram_sum()
                    mix_matrix(0)
                    mix_matrix(1)
                    shift_real()
                    kernel_sum()
                    router(0)
                    router(1)
                    shift_sum()
                    add_skip()
                    router(2)
                    times_z()
                    router(3)
                    gated_a()
                    router(4)
                    mean_square()
                    router(5)
                    router(6)
                    norm_y(0)
                    norm_y(1)
                    router(7)
                    conv(0, 0)
                    router(8)
                    conv(0, 1)
                    router(9)
                    stats_1(0)
                    stats_1(1)
                    stats_1(2)
                    stats_1(3)
                    layer_out()
                    gated_b()
                    norm_1()
                    deviation_1()
                    softplus(0)
                    conv(0, 2)
                    softplus(1)
                    conv(1, 0)
                    conv(1, 1)
                    conv(1, 2)
                    softplus(2)
                    residual(0)
                    conv(2, 0)
                    softplus(3)
                    stats_2(0)
                    softplus(4)
                    conv(2, 1)
                    softplus(5)
                    conv(2, 2)
                    residual(1)
                    conv(3, 0)
                    softplus(6)
                    stats_2(1)
                    conv(3, 1)
                    softplus(7)
                    conv(3, 2)
                    stats_2(2)
                    conv(4, 0)
                    stats_2(3)
                    conv(4, 1)
                    conv(4, 2)
                    softplus(8)
                    conv(5, 0)
                    softplus(9)
                    norm_2()
                    softplus(10)
                    conv(5, 1)
                    softplus(11)
                    conv(5, 2)
                    softplus(12)
                    conv(6, 0)
                    softplus(13)
                    conv(6, 1)
                    softplus(14)
                    conv(6, 2)
                    softplus(15)
                    split_lo(0)
                    softplus(16)
                    silu_z()
                    silu_x()
                    silu_bc(0)
                    softplus(17)
                    silu_bc(1)
                    decays_forth()
                    final(0)
                    final(1)
                    split_lo(1)

                iterations(dve, body)

            @block.tensor
            def _(pe):
                mm, tr = pe.matmul, pe.transpose

                def body(i, p):
                    A, A1 = active(i, 0, CLS), active(i, 0, TILES)
                    D, E = active(i, 4, TILES), active(i, 5, TILES)
                    H, G = active(i, 1, TILES + 2), active(i, 2, TILES + 2)
                    q, r, td, te = i - 1, i - 2, i - 4, i - 5
                    u = U[:, 1 - p, :, :].rearrange("p a t -> p (a t)")

                    def ffn(c0, c1, bank, ks, last=None):
                        for k in ks:
                            for n, (xs_, ws) in enumerate(((XHI, w_hi), (XHI, w_lo), (XLO, w_hi))):
                                ins = mm(bank[:, 0:c1 - c0], xs_[:, 1 - p, k, :], ws[:, k, c0:c1],
                                         start=(k == 0 and n == 0), stop=(last == k and n == 2))
                        return ins

                    def route(a, b):
                        if E:
                            if a == 0:
                                wait(pe, te, xlo=2)
                                wait(pe, te - 1, hwe=1)
                            ins = ffn(HID, FW, bR, range(a, b), last=KC - 1)
                            if b == KC:
                                inc(ins, "rt")

                    def bases(h, a, b):
                        if E:
                            if a == 0:
                                wait(pe, te, xlo=2)
                                wait(pe, te - 1, fin=h + 1)
                            ffn(HALF * h, HALF * (h + 1), bO[h], range(a, b))

                    def turn_h():
                        if E:
                            wait(pe, te, hw=1)
                            inc(tr(bR[:, 256:256 + P], HW[:, :], ident[:, :]), "trh")

                    def lora(h):
                        if E:
                            wait(pe, te, hwe=1)
                            inc(mm(bO[h][:, :], HWT[:, :], lbT[:, HALF * h:HALF * (h + 1)], start=False, stop=True), "o")

                    def up(h):
                        if D:
                            if h == 0:
                                wait(pe, td, gt=1)
                                bT_free(UP)
                            else:
                                wait(pe, td, h1=1)
                            inc(mm(bT[:, :], GT[:, :], wuT[:, HALF * h:HALF * (h + 1)], start=True, stop=True), "up")

                    def turn_d(g):
                        if D:
                            if g == 0:
                                wait(pe, td, xh2=1)
                                bT_free(TURN_D)
                            else:
                                wait(pe, td, xlo=1)
                            for k in range(4):
                                ins = tr(bT[:, P * k:P * (k + 1)], T2[:, (4 * g + k) * P:(4 * g + k + 1) * P], ident[:, :])
                            inc(ins, "tr2")

                    def turn_a(g):
                        if A1:
                            if g == 0:
                                wait(pe, i, xh1=1)
                                bT_free(TURN_A)
                            else:
                                wait(pe, i, xte=1)
                            for k in range(4):
                                ins = tr(bT[:, P * k:P * (k + 1)], H0[:, (4 * g + k) * P:(4 * g + k + 1) * P], ident[:, :])
                            inc(ins, "tr1")

                    def bT_free(user):
                        if user == TURN_D:
                            wait(pe, min(i, CLS) if isinstance(i, int) else i, xte=2)
                            wait(pe, td, h1=2)
                        elif user == TURN_A:
                            if D:
                                wait(pe, td, h1=2)
                            wait(pe, td - 1, xlo=2)
                        else:
                            wait(pe, td - 1, xlo=2)
                            wait(pe, min(i - 1, CLS) if isinstance(i, int) else i - 1, xte=2)

                    def s4d(b):
                        if A:
                            if b == 0:
                                wait(pe, i, xtc=1, wsum=1, wi=2, vsum=1)
                            else:
                                wait(pe, i, hev=2)
                            for s in range(2):
                                ins = mm(bK[:, 256 * s:256 * (s + 1)], W[:, b, 2 * s:2 * s + 2, :].rearrange("p a c -> p (a c)"),
                                         VB[:, b, :, :].rearrange("p a c -> p (a c)"), start=True, stop=True)
                            inc(ins, "km")

                    def down():
                        if A1:
                            wait(pe, i, xte=2)
                            if A:
                                wait(pe, i, hev=4)
                            for k in range(KC):
                                ins = mm(bK[:, 0:P], wdT[:, k, :], XHT[:, k, :], start=(k == 0), stop=(k == KC - 1))
                            inc(ins, "down")

                    def turn_x():
                        if A:
                            wait_x(pe, i, p)
                            wait(pe, i, xswap=2)
                            wait(pe, i - 1, gelu=1)
                            tr(bK[:, 0:P], XI[:, p, :], ident[:, :])
                            inc(tr(bK[:, P:2 * P], XSW[:, :, :].rearrange("p n r -> p (n r)"), ident[:, :]), "xt")

                    def project_x():
                        if H:
                            u_ready()
                            wait(pe, r, y1=1)
                            for c in range(2):
                                ins = mm(bX[:, 256 * c:256 * (c + 1)], wx[:, P * c:P * (c + 1)], u, start=True, stop=True)
                            inc(ins, "pin")

                    def project_bc():
                        if H:
                            wait(pe, min(q, TILES - 1) if isinstance(i, int) else q, gelu=1)
                            wait(pe, r, u2=1)
                            wait(pe, td, gt=1)
                            for a in range(2):
                                mm(bY[:, 256 + 8 * a:264 + 8 * a], U[:, 1 - p, a, :], wbc[:, BCP:BCP + 2 * NH],
                                   start=True, stop=True)
                            inc(mm(bY[0:BCP, 0:256], wbc[:, 0:BCP], u, start=True, stop=True), "pin")

                    def project_z():
                        if H:
                            u_ready()
                            wait(pe, r, yte=1)
                            for a in range(2):
                                ins = mm(bZ[:, 256 * a:256 * (a + 1)], U[:, 1 - p, a, :], wz[:, :], start=True, stop=True)
                            inc(ins, "pin")

                    def u_ready():
                        wait(pe, min(q, TILES - 1) if isinstance(i, int) else q, gelu=1)
                        wait(pe, r - 1, u2=1)

                    def turn_xs():
                        if G:
                            wait(pe, r, xs=1, conv=NCONV)
                            for a in range(2):
                                for c in range(2):
                                    ins = tr(bX[:, (2 * a + c) * P:(2 * a + c + 1) * P],
                                             CX[:, c, 2 * a:2 * a + 2, :].rearrange("p g t -> p (g t)"), ident[:, :])
                            inc(ins, "trx")

                    def grams():
                        if G:
                            wait(pe, r, dtc=1, xs=3, conv=NCONV)
                            for a in range(2):
                                for c in range(2):
                                    mm(bY[:, FC0 + NH * a:FC0 + NH * (a + 1)],
                                       CX[:, c, 2 * a:2 * a + 2, :].rearrange("p g t -> p (g t)"),
                                       fcT[:, c, :], start=(c == 0), stop=(c == 1))
                            for a in range(2):
                                ins = mm(bY[:, P * a:P * (a + 1)], BT[:, P * a:P * (a + 1)], CT[:, P * a:P * (a + 1)],
                                         start=True, stop=True)
                            inc(ins, "gram")

                    def decay_sums():
                        if G:
                            wait(pe, r, rf=1, rb=1, sz=1)
                            for a in range(2):
                                for n, (m, dec) in enumerate(((earlier, RF), (later, RB))):
                                    ins = mm(bZ[:, 256 * a:256 * (a + 1)], m[:, :],
                                             dec[:, NH * a:NH * (a + 1), :].rearrange("p h t -> p (h t)"),
                                             start=(n == 0), stop=(n == 1))
                            inc(ins, "seg")

                    def mix():
                        if G:
                            wait(pe, r, mm=2, xse=1)
                            for a in range(2):
                                for h in range(NH):
                                    ins = mm(bX[:, 256 * a + HD * h:256 * a + HD * (h + 1)], Mt[:, a, h, :],
                                             XS[:, 256 * a + HD * h:256 * a + HD * (h + 1)], start=True, stop=True)
                            inc(ins, "yy")

                    def turn_y():
                        if G:
                            wait(pe, r, yn=2, ex=1)
                            for c in range(2):
                                for a in range(2):
                                    ins = tr(bZ[:, (2 * c + a) * P:(2 * c + a + 1) * P],
                                             XD[:, NH * a + 2 * c:NH * a + 2 * c + 2, :].rearrange("p a b -> p (a b)"),
                                             ident[:, :])
                            inc(ins, "tyn")

                    def project_out():
                        if G:
                            wait(pe, r, yte=1, g4=4, dd=1)
                            yt = YT[:, :, :].rearrange("p a b -> p (a b)")
                            for c in range(2):
                                ins = mm(bY[:, 0:256], owT[:, c, :], yt[:, 256 * c:256 * (c + 1)], start=(c == 0), stop=(c == 1))
                            inc(ins, "outp")

                    turn_xs()
                    grams()
                    decay_sums()
                    route(0, 1)
                    route(1, 2)
                    route(2, 3)
                    route(3, 4)
                    route(4, 5)
                    bases(1, 0, 1)
                    turn_x()
                    route(5, 6)
                    route(6, 7)
                    route(7, 8)
                    mix()
                    s4d(0)
                    project_x()
                    bases(0, 0, 1)
                    bases(1, 1, 2)
                    s4d(1)
                    turn_y()
                    bases(1, 2, 3)
                    bases(0, 1, 2)
                    project_out()
                    bases(1, 3, 4)
                    turn_h()
                    project_bc()
                    bases(0, 2, 3)
                    up(0)
                    bases(0, 3, 4)
                    bases(0, 4, 5)
                    bases(0, 5, 6)
                    up(1)
                    bases(1, 4, 5)
                    bases(0, 6, 7)
                    turn_a(0)
                    bases(0, 7, 8)
                    bases(1, 5, 6)
                    bases(1, 6, 7)
                    turn_a(1)
                    lora(0)
                    bases(1, 7, 8)
                    turn_d(0)
                    project_z()
                    down()
                    lora(1)
                    turn_d(1)

                UP, TURN_A, TURN_D = range(3)
                iterations(pe, body)


_INS = ["x", "cls_tok", "L0_tok_log_dt", "L0_tok_B", "L0_tok_inv_A_real", "L0_tok_A_imag", "L0_attn_w_down",
        "L0_attn_b_down", "L0_attn_w_up", "L0_attn_b_up", "L0_attn_gate1", "L0_attn_hy_in_w", "L0_attn_hy_conv_w",
        "L0_attn_hy_conv_b", "L0_attn_hy_dt_bias", "L0_attn_hy_A_log", "L0_attn_hy_D", "L0_attn_hy_fcD_w",
        "L0_attn_hy_norm_w", "L0_attn_hy_out_w", "L0_ffn_base_W", "L0_ffn_base_b", "L0_ffn_router_W",
        "L0_ffn_router_b", "L0_ffn_A", "L0_ffn_B", "L0_ffn_expert_map"]


def kernel(**inputs):
    import concourse.bacc as bacc
    from concourse.bass_utils import run_bass_kernel_spmd

    nc = bacc.Bacc("TRN2", target_bir_lowering=False, num_devices=1)
    arrays, args = {}, []
    for name in _INS:
        a = np.ascontiguousarray(inputs[name])
        if a.ndim == 0:
            a = a.reshape(1, 1)
        arrays[f"in_{name}"] = a
        args.append(nc.dram_tensor(f"in_{name}", a.shape, mybir.dt.from_np(a.dtype), kind="ExternalInput").ap())
    steps, rows, states, _ = inputs["x"].shape
    shape = (steps, rows + 1, inputs["cls_tok"].shape[-1])
    args.append(nc.dram_tensor("out_0", shape, F32, kind="ExternalOutput").ap())
    build(nc, *args, pairs=rows // 2)
    r = run_bass_kernel_spmd(nc, [arrays], core_ids=[0])
    return r.results[0]["out_0"]
```

```python
from contextlib import ExitStack

import numpy as np

import concourse.bass as bass
from concourse import mybir

F32 = mybir.dt.float32
F32R = mybir.dt.float32r
I32 = mybir.dt.int32
ALU = mybir.AluOpType
ACT = mybir.ActivationFunctionType
AX = mybir.AxisListType

P = 128
PI = float(np.pi)
EPS = 1e-5
ROUND = float(1.5 * 2 ** 23)


class Step:

    def __init__(self, sem, per, unit=1):
        self.sem, self.per, self.unit = sem, per, unit

    def after(self, eng, n, j=None):
        if isinstance(n, int) and n < 0:
            return
        j = self.per if j is None else j
        eng.wait_ge(self.sem, (n * self.per + j) * self.unit)


def build(nc, x, cls_tok, log_dt, tok_B, inv_A_real, A_imag, w_down, b_down, w_up, b_up, gate1, in_w,
          conv_w, conv_b, dt_bias, A_log, hy_D, fcD_w, norm_w, out_w, base_W, base_b, router_W, router_b,
          lora_A, lora_B, expert_map, out, pairs=64):
    CS, NHT, NST, _ = x.shape
    DM, HID = w_down.shape
    KC = HID // P
    DIN = out_w.shape[1]
    NH = A_log.shape[0]
    HD = DIN // NH
    DST = (conv_w.shape[0] - DIN) // 2
    TAPS = conv_w.shape[2]
    NE, RK, _ = lora_A.shape
    NR = router_W.shape[0]
    FW = HID + P + NR + 1
    HALF = HID // 2
    BCP = 48
    TILES = pairs + 1
    CLS = pairs

    with ExitStack() as keep:
        def sb(name, shape, dt=F32, ctx=None):
            return (ctx or keep).enter_context(nc.sbuf_tensor(name, shape, dt))

        def sem(name):
            return keep.enter_context(nc.semaphore(name))

        w_hi = sb("w_hi", [P, KC, FW], F32R)
        w_lo = sb("w_lo", [P, KC, FW], F32R)
        wdT = sb("wdT", [P, KC, DM])
        wu_hi = sb("wu_hi", [P, HID], F32R)
        wu_lo = sb("wu_lo", [P, HID], F32R)
        lb_hi = sb("lb_hi", [P, HID], F32R)
        lb_lo = sb("lb_lo", [P, HID], F32R)
        wx = sb("wx", [P, DIN])
        wbc = sb("wbc", [P, BCP + 2 * NH])
        wz = sb("wz", [P, DIN])
        fcT = sb("fcT", [P, 2, NH])
        owT = sb("owT", [P, 2, DM])
        ident = sb("ident", [P, P])
        earlier = sb("earlier", [P, P], F32R)
        later = sb("later", [P, P], F32R)
        m_lt = sb("m_lt", [P, CS])
        m_gt = sb("m_gt", [P, CS])
        bup = sb("bup", [P, HID])
        bbase = sb("bbase", [P, HID])
        rbias = sb("rbias", [P, NR])
        onehot = sb("onehot", [P, NE, NR])
        dtb = sb("dtb", [P, NH])
        negA = sb("negA", [P, NH])
        Dbc = sb("Dbc", [P, NH])
        bdn = sb("bdn", [P, 1])
        al1 = sb("al1", [P, 1])
        be1 = sb("be1", [P, 1])
        cw = sb("cw", [P, 2, TAPS])
        cb = sb("cb", [P, 2])
        cwb = sb("cwb", [BCP, TAPS])
        cbb = sb("cbb", [BCP, 1])
        half_neg = sb("half_neg", [P, 2])
        TP, TQ, TJR, TJI = (slice(16 * k, 16 * k + 16) for k in range(4))
        TSR, TSI, NTAB = slice(64, 67), slice(67, 70), 70
        tables = nc.dram_tensor("tables", (NHT // 2, P, 2, NTAB), F32, kind="Internal").ap()
        T = sb("T", [P, 2, HID])
        HB = sb("HB", [P, 2, HID])
        Mt = sb("Mt", [P, 2, NH, P])
        GF = sb("GF", [P, 2, CS])
        GB = sb("GB", [P, 2, CS])
        U = sb("U", [P, 2, 2, P])
        banks = [keep.enter_context(nc.psum_tensor(f"bank{i}", [P, 512], F32)) for i in range(8)]

        with ExitStack() as tmp:
            def ts(name, shape, dt=F32):
                return sb(name, shape, dt, tmp)

            stage = [T[:, 0, :], T[:, 1, :], HB[:, 0, :], HB[:, 1, :], ts("st4", [P, HID])[:, :], ts("st5", [P, HID])[:, :]]
            NS = len(stage)
            inw_s = ts("inw_s", [P, 4, P])
            bc_s = ts("bc_s", [P, P])
            dt_s = ts("dt_s", [2 * NH, P])
            fc_s = ts("fc_s", [NH, DIN])
            ow_s = ts("ow_s", [P, DIN])
            nw = ts("nw", [P, 2])
            alog = ts("alog", [P, NH])
            gate = ts("gate", [P, 1])
            gt0 = ts("gt0", [P, 1])
            emap = ts("emap", [P, NR], I32)
            emf = ts("emf", [P, NR])
            cw0 = ts("cw0", [P, 2, TAPS])
            cb0 = ts("cb0", [P, 2])
            cwb0 = ts("cwb0", [BCP, TAPS])
            cbb0 = ts("cbb0", [BCP, 1])
            ones = ts("ones", [P, P])
            earlier0 = ts("earlier0", [P, P])
            later0 = ts("later0", [P, P])
            evm = ts("evm", [P, NST])
            ai_s = ts("ai_s", [P, NST])
            ar_s = ts("ar_s", [P, NST])
            b_s = ts("b_s", [P, NST, 2])
            dup = ts("dup", [P, 4, NST, 2])
            par = ts("par", [P, 4, NHT])
            ldt = ts("ldt", [P, NHT])
            lst = ts("lst", [P, 35])
            lst_i = ts("lst_i", [P, 35], I32)
            v = {n: ts("v_" + n, [P, NHT]) for n in
                 ("dt", "ar", "sg", "om", "t0", "t1", "t2", "t3", "t4", "er", "ei", "co", "Gr", "Gi", "al", "be")}
            evc = ts("evc", [P, 1])
            odc = ts("odc", [P, 1])
            sgn = ts("sgn", [P, 1])
            HCH = 16
            tab = ts("tab", [P, HCH, NTAB])
            big = {n: ts("g_" + n, [P, HCH, 35]) for n in ("arg", "k", "r", "e")}
            vre, vim = ts("vre", [P, 2, HCH, 35]), ts("vim", [P, 2, HCH, 35])
            px, py = ts("px", [P, HCH, 16]), ts("py", [P, HCH, 16])

            pieces = [("w", o) for o in range(KC)] + [("A", 0), ("r", 0), ("d", 0), ("u", 0), ("b", 0)]

            def tsem(name):
                return tmp.enter_context(nc.semaphore(name))

            s_ld = [tsem(f"s_ld{i}") for i in range(NS)]
            s_small, s_wt, s_hi, s_lo = tsem("s_small"), tsem("s_wt"), tsem("s_hi"), tsem("s_lo")
            s_pool, s_dve, s_act = tsem("s_pool"), tsem("s_dve"), tsem("s_act")
            s_zero, s_masks, s_consts = tsem("s_zero"), tsem("s_masks"), tsem("s_consts")
            s_dup, s_par, s_tdt, s_exps = tsem("s_dup"), tsem("s_par"), tsem("s_tdt"), tsem("s_exps")
            s_sg, s_om, s_trig = tsem("s_sg"), tsem("s_om"), tsem("s_trig")
            s_albe, s_tab, s_vals, s_chain = tsem("s_albe"), tsem("s_tab"), tsem("s_vals"), tsem("s_chain")
            s_red, s_dec, s_sin, s_exp, s_kept = tsem("s_red"), tsem("s_dec"), tsem("s_sin"), tsem("s_exp"), tsem("s_kept")
            loaded, count = [], [0] * NS
            for n, (kind, _) in enumerate(pieces):
                count[n % NS] += 16 * (NE if kind == "b" else 1)
                loaded.append(count[n % NS])

            jobs = [([inw_s[:, 2, :], inw_s[:, 3, :]], P, wx[:, :].rearrange("p (a b) -> p a b", a=2), None, 1.0, -1),
                    ([inw_s[:, 0, :], inw_s[:, 1, :]], P, wz[:, :].rearrange("p (a b) -> p a b", a=2), None, 0.5, -1),
                    ([bc_s[0:BCP, :]], BCP, wbc[:, 0:BCP].unsqueeze(1), None, 1.0, -1),
                    ([dt_s[:, :]], 2 * NH, wbc[:, BCP:BCP + 2 * NH].unsqueeze(1), None, 1.0, -1),
                    ([fc_s[:, 0:P], fc_s[:, P:DIN]], NH, fcT[:, :, :], None, 1.0, -1),
                    ([ow_s[:, 0:P]], P, owT[:, 0:1, :], None, nw[:, 0:1], -1),
                    ([ow_s[:, P:DIN]], P, owT[:, 1:2, :], None, nw[:, 1:2], -1)]
            for n, (kind, o) in enumerate(pieces):
                rows = NR if kind == "r" else P
                for g in range(2):
                    ks = slice(4 * g, 4 * g + 4)
                    src = [stage[n % NS][0:rows, (4 * g + k) * P:(4 * g + k + 1) * P] for k in range(4)]
                    if kind in "wAr":
                        at = {"w": o * P, "A": HID, "r": HID + P}[kind]
                        jobs.append((src, rows, w_hi[:, ks, at:at + rows], w_lo[:, ks, at:at + rows], 1.0, n))
                    elif kind == "d":
                        jobs.append((src, rows, wdT[:, ks, :], None, 1.0, n))
                    else:
                        hi, lo = (wu_hi, wu_lo) if kind == "u" else (lb_hi, lb_lo)
                        hi, lo = (w[:, 512 * g:512 * g + 512].rearrange("p (a b) -> p a b", a=4) for w in (hi, lo))
                        jobs.append((src, rows, hi, lo, 1.0, n))
            splits = np.cumsum([j[3] is not None for j in jobs]).tolist()
            last_job = {j[5]: k for k, j in enumerate(jobs)}
            RING, SMALL_JOBS, PER_CHUNK = 4, 7, 2
            NSMALL = 29

            block = tmp.enter_context(nc.Block())

            @block.sync
            def _(sp):
                def small(dst, src):
                    sp.dma_start(dst, src).then_inc(s_small, 16)

                small(ai_s[:, :], A_imag)
                small(ar_s[:, :], inv_A_real)
                small(b_s[:, :, :], tok_B)
                small(ldt[:, :], log_dt.unsqueeze(0).broadcast_to([P, NHT]))
                small(inw_s[:, :, :], in_w[0:4 * P, :].rearrange("(a p) d -> p a d", p=P))
                small(dt_s[:, :], in_w[2 * DIN + 2 * DST:2 * DIN + 2 * DST + 2 * NH, :])
                small(fc_s[:, :], fcD_w)
                small(ow_s[:, :], out_w)
                small(nw[:, 0:1], norm_w[0:P].unsqueeze(1))
                small(nw[:, 1:2], norm_w[P:DIN].unsqueeze(1))
                cwr = conv_w.rearrange("c a k -> c (a k)")
                for c in range(2):
                    small(cw0[:, c, :], cwr[c * P:(c + 1) * P, :])
                    small(cb0[:, c:c + 1], conv_b[c * P:(c + 1) * P].unsqueeze(1))
                small(bup[:, :], b_up.unsqueeze(0).broadcast_to([P, HID]))
                small(bbase[:, :], base_b.unsqueeze(0).broadcast_to([P, HID]))
                small(rbias[:, :], router_b.unsqueeze(0).broadcast_to([P, NR]))
                small(emap[:, :], expert_map.unsqueeze(0).broadcast_to([P, NR]))
                small(dtb[:, :], dt_bias.unsqueeze(0).broadcast_to([P, NH]))
                small(alog[:, :], A_log.unsqueeze(0).broadcast_to([P, NH]))
                small(Dbc[:, :], hy_D.unsqueeze(0).broadcast_to([P, NH]))
                small(bdn[:, :], b_down.unsqueeze(1))
                small(gate[:, :], gate1.broadcast_to([P, 1]))
                sp.wait_ge(s_zero, 3)
                for k in range(2):
                    small(bc_s[32 * k:32 * k + DST, :], in_w[2 * DIN + DST * k:2 * DIN + DST * (k + 1), :])
                    small(cwb0[32 * k:32 * k + DST, :], cwr[DIN + DST * k:DIN + DST * (k + 1), :])
                    small(cbb0[32 * k:32 * k + DST, :], conv_b[DIN + DST * k:DIN + DST * (k + 1)].unsqueeze(1))

                for c in range(NHT // HCH):
                    sp.wait_ge(s_tab, c + 1)
                    sp.dma_start(tables[c * HCH // 2:(c + 1) * HCH // 2].rearrange("t f b k -> f t b k"),
                                 tab[:, :, :].rearrange("f (t b) k -> f t b k", b=2)).then_inc(s_kept, 16)
                sp.wait_ge(s_kept, 16 * (NHT // HCH))

            @block.gpsimd
            def _(pool):
                pool.memset(bc_s[:, :], 0.0).then_inc(s_zero, 1)
                pool.memset(cwb0[:, :], 0.0).then_inc(s_zero, 1)
                pool.memset(cbb0[:, :], 0.0).then_inc(s_zero, 1)
                pool.memset(ones[:, :], 1.0).then_inc(s_pool, 1)
                for t in (ident, earlier0, later0):
                    pool.memset(t[:, :], 0.0).then_inc(s_pool, 1)
                pool.wait_ge(s_pool, 4)
                pool.affine_select(out=ident[:, :], in_=ident[:, :], compare_op=ALU.not_equal, fill=1.0,
                                   base=0, pattern=[[-1, P]], channel_multiplier=1).then_inc(s_masks, 1)
                for b in range(2):
                    r = slice(CS * b, CS * (b + 1))
                    pool.wait_ge(s_masks, 1 + 4 * b)
                    for dst, cols, sign in ((earlier0, r, 1), (later0, r, -1), (m_gt, slice(0, CS), 1),
                                            (m_lt, slice(0, CS), -1)):
                        pool.affine_select(out=dst[r, cols], in_=ones[r, 0:CS], compare_op=ALU.is_gt, fill=0.0,
                                           base=0, pattern=[[-sign, CS]], channel_multiplier=sign).then_inc(s_masks, 1)
                pool.wait_ge(s_masks, 9)
                pool.affine_select(out=evm[:, :], in_=ones[:, 0:NST], compare_op=ALU.is_equal, fill=0.0,
                                   base=0, pattern=[[-2, NST]], channel_multiplier=1).then_inc(s_consts, 1)
                pool.iota(lst_i[:, 0:16], pattern=[[1, 16]], base=0, channel_multiplier=0).then_inc(s_consts, 1)
                pool.iota(lst_i[:, 16:32], pattern=[[16, 16]], base=0, channel_multiplier=0).then_inc(s_consts, 1)
                for k, s in enumerate((512, 256, 768)):
                    pool.iota(lst_i[:, 32 + k:33 + k], pattern=[[1, 1]], base=s,
                              channel_multiplier=0).then_inc(s_consts, 1)
                pool.memset(half_neg[:, :], -0.5)
                pool.memset(Mt[:, :, :, :], 0.0)
                pool.memset(GF[:, :, :], 0.0)
                pool.memset(GB[:, :, :], 0.0)
                pool.memset(U[:, :, :, :], 0.0)

                links = [0]

                def link(ins):
                    links[0] += 1
                    ins.then_inc(s_chain, 1)
                    pool.wait_ge(s_chain, links[0])

                TT = pool.tensor_tensor
                pool.wait_ge(s_albe, 1)
                for c in range(NHT // HCH):
                    hs = slice(c * HCH, (c + 1) * HCH)
                    al, be = (v[n][:, hs].unsqueeze(2).broadcast_to([P, HCH, 16]) for n in ("al", "be"))
                    vc, vs = vre[:, c % 2], vim[:, c % 2]
                    Vr, Vi = vc[:, :, 0:16], vs[:, :, 0:16]
                    pool.wait_ge(s_vals, 2 * c + 2)
                    if c:
                        pool.wait_ge(s_kept, 16 * c)
                    TT(tab[:, :, TP], Vr, al, ALU.mult)
                    TT(px[:, :, :], Vi, be, ALU.mult)
                    TT(tab[:, :, TQ], Vr, be, ALU.mult)
                    link(TT(py[:, :, :], Vi, al, ALU.mult))
                    TT(tab[:, :, TP], tab[:, :, TP], px[:, :, :], ALU.add)
                    TT(tab[:, :, TQ], tab[:, :, TQ], py[:, :, :], ALU.subtract)
                    pool.tensor_copy(tab[:, :, TJR], vc[:, :, 16:32])
                    pool.tensor_copy(tab[:, :, TJI], vs[:, :, 16:32])
                    pool.tensor_copy(tab[:, :, TSR], vc[:, :, 32:35])
                    pool.tensor_scalar(tab[:, :, TSI], vs[:, :, 32:35], sgn[:, 0:1], None, ALU.mult).then_inc(s_tab, 1)

            @block.tensor
            def _(pe):
                pe.wait_ge(s_masks, 1)
                pe.wait_ge(s_dup, 4)
                for k in range(4):
                    ins = pe.transpose(banks[7][:, k * P:(k + 1) * P], dup[:, k, :, :].rearrange("p a b -> p (a b)"),
                                       ident[:, :])
                ins.then_inc(s_par, 1)
                pe.wait_ge(s_small, 16 * NSMALL)
                for k, (src, m, _, lo, _, n) in enumerate(jobs):
                    if n >= 0:
                        pe.wait_ge(s_ld[n % NS], loaded[n])
                    if k >= RING:
                        pe.wait_ge(s_hi, k - RING + 1)
                        if splits[k - RING]:
                            pe.wait_ge(s_lo, splits[k - RING])
                    for c, a in enumerate(src):
                        ins = pe.transpose(banks[k % RING][:, c * m:(c + 1) * m], a, ident[0:m, 0:m])
                    ins.then_inc(s_wt, 1)

            @block.scalar
            def _(act):
                dram = {"w": lambda o: base_W[o * P:(o + 1) * P, :],
                        "A": lambda o: lora_A.rearrange("e r d -> (e r) d"),
                        "r": lambda o: router_W, "d": lambda o: w_down,
                        "u": lambda o: w_up.rearrange("(a p) d -> p a d", p=P)}

                def load(n):
                    kind, o = pieces[n]
                    st = stage[n % NS]
                    if n >= NS:
                        act.wait_ge(s_wt, last_job[n - NS] + 1)
                    if kind == "b":
                        st4 = st.rearrange("p (a e r) -> p a e r", a=KC, e=NE)
                        for e in range(NE):
                            act.dma_start(st4[:, :, e, :],
                                          lora_B[e].rearrange("(a p) r -> p a r", p=P)).then_inc(s_ld[n % NS], 16)
                        return
                    dst = st[0:NR, :] if kind == "r" else st
                    if kind == "u":
                        dst = st.rearrange("p (a d) -> p a d", a=KC)
                    act.dma_start(dst, dram[kind](o)).then_inc(s_ld[n % NS], 16)

                for n in range(NS):
                    load(n)
                act.wait_ge(s_small, 16 * NSMALL)
                act.activation(v["t0"][:, :], ldt[:, :], ACT.Tanh, scale=1.0 / 16).then_inc(s_tdt, 1)
                act.wait_ge(s_par, 1)
                act.activation(v["t1"][:, :], banks[7][:, P:2 * P], ACT.Exp).then_inc(s_exps, 1)
                act.activation(alog[:, :], alog[:, :], ACT.Exp).then_inc(s_exps, 1)
                act.activation(gt0[:, :], gate[:, :], ACT.Exp, scale=-1.0).then_inc(s_exps, 1)
                act.wait_ge(s_sg, 1)
                act.activation(v["t0"][:, :], v["sg"][:, :], ACT.Tanh, scale=0.5).then_inc(s_trig, 1)
                act.wait_ge(s_om, 1)
                act.activation(v["t2"][:, :], v["om"][:, :], ACT.Sin).then_inc(s_trig, 1)
                act.activation(v["t3"][:, :], v["om"][:, :], ACT.Sin, scale=0.5).then_inc(s_trig, 1)
                nxt, k = NS, 0

                def evacuate(k, nxt):
                    src, m, dst, lo, scale, n = jobs[k]
                    act.wait_ge(s_wt, k + 1)
                    cols = banks[k % RING][:, 0:len(src) * m].rearrange("p (a b) -> p a b", b=m)
                    act.activation(dst, cols, ACT.Copy, scale=scale).then_inc(s_hi, 1)
                    if n >= 0 and last_job[n] == k and nxt < len(pieces):
                        load(nxt)
                        nxt += 1
                    return nxt

                while k < SMALL_JOBS:
                    nxt = evacuate(k, nxt)
                    k += 1
                for c in range(NHT // HCH):
                    for _ in range(PER_CHUNK):
                        nxt = evacuate(k, nxt)
                        k += 1
                    act.wait_ge(s_red, c + 1)
                    if c >= 2:
                        act.wait_ge(s_tab, c - 1)
                    act.activation(vim[:, c % 2], big["r"][:, :, :], ACT.Sin).then_inc(s_sin, 1)
                    act.activation(vre[:, c % 2], big["r"][:, :, :], ACT.Sin, scale=0.5).then_inc(s_sin, 1)
                    act.wait_ge(s_dec, c + 1)
                    act.activation(big["e"][:, :, :], big["arg"][:, :, :], ACT.Exp).then_inc(s_exp, 1)
                while k < len(jobs):
                    nxt = evacuate(k, nxt)
                    k += 1

            @block.vector
            def _(dve):
                cnt = [0]

                def link(ins):
                    cnt[0] += 1
                    ins.then_inc(s_dve, 1)
                    dve.wait_ge(s_dve, cnt[0])

                TT, TS, STT = dve.tensor_tensor, dve.tensor_scalar, dve.scalar_tensor_tensor
                V = {n: t[:, :] for n, t in v.items()}
                dve.wait_ge(s_small, 16 * NSMALL)
                for k, src in enumerate((ai_s[:, :], ar_s[:, :], b_s[:, :, 0], b_s[:, :, 1])):
                    dve.tensor_copy(dup[:, k, :, :], src.unsqueeze(2).broadcast_to([P, NST, 2])).then_inc(s_dup, 1)
                dve.wait_ge(s_consts, 6)
                link(dve.tensor_copy(lst[:, :], lst_i[:, :]))
                link(dve.tensor_reduce(evc[:, :], evm[:, :], AX.X, ALU.add))
                link(TS(odc[:, :], evc[:, :], -1.0, 1.0, ALU.mult, ALU.add))
                link(TT(sgn[:, :], odc[:, :], evc[:, :], ALU.subtract))
                dve.wait_ge(s_tdt, 1)
                link(TS(V["t2"], V["t0"], -1.0, 1.0, ALU.mult, ALU.add))
                link(dve.reciprocal(V["t3"], V["t2"]))
                link(STT(V["dt"], V["t0"], 1.0, V["t3"], ALU.add, ALU.mult))
                for _ in range(3):
                    link(TT(V["dt"], V["dt"], V["dt"], ALU.mult))
                dve.wait_ge(s_exps, 1)
                link(dve.tensor_copy(par[:, :, :], banks[7][:, :].rearrange("p (a b) -> p a b", a=4)))
                link(TS(V["ar"], V["t1"], -1.0, None, ALU.mult))
                TT(V["sg"], V["ar"], V["dt"], ALU.mult).then_inc(s_sg, 1)

                def reduce(arg, k, r):
                    c1 = 6.28125
                    c2 = float(np.floor((2 * np.pi - c1) * 2.0 ** 20) * 2.0 ** -20)
                    c3 = float(2 * np.pi - c1 - c2)
                    link(TS(k, arg, 0.5 / PI, ROUND, ALU.mult, ALU.add))
                    link(TS(k, k, ROUND, None, ALU.subtract))
                    link(STT(r, k, -c1, arg, ALU.mult, ALU.add))
                    link(STT(r, k, -c2, r, ALU.mult, ALU.add))
                    link(STT(r, k, -c3, r, ALU.mult, ALU.add))
                    return TS(r, r, 3.1415925, -3.1415925, ALU.min, ALU.max)

                ai, br, bi = par[:, 0, :], par[:, 2, :], par[:, 3, :]
                link(TT(V["t4"], ai, V["dt"], ALU.mult))
                reduce(V["t4"], V["er"], V["om"]).then_inc(s_om, 1)
                dve.wait_ge(s_trig, 3)
                link(TS(V["t1"], V["t0"], -1.0, 1.0, ALU.mult, ALU.add))
                link(dve.reciprocal(V["co"], V["t1"]))
                link(STT(V["t0"], V["t0"], 2.0, V["co"], ALU.mult, ALU.mult))
                link(TT(V["t3"], V["t3"], V["t3"], ALU.mult))
                link(TS(V["t3"], V["t3"], -2.0, None, ALU.mult))
                link(TS(V["co"], V["t3"], 1.0, None, ALU.add))
                link(TT(V["er"], V["t0"], V["co"], ALU.mult))
                link(TT(V["er"], V["er"], V["t3"], ALU.add))
                link(STT(V["ei"], V["t0"], 1.0, V["t2"], ALU.add, ALU.mult))
                link(TT(V["t1"], V["ar"], V["ar"], ALU.mult))
                link(TT(V["t0"], ai, ai, ALU.mult))
                link(TT(V["t1"], V["t1"], V["t0"], ALU.add))
                link(dve.reciprocal(V["t0"], V["t1"]))
                link(TT(V["t1"], V["er"], V["ar"], ALU.mult))
                link(TT(V["t2"], V["ei"], ai, ALU.mult))
                link(TT(V["t1"], V["t1"], V["t2"], ALU.add))
                link(TT(V["t2"], V["ei"], V["ar"], ALU.mult))
                link(TT(V["t3"], V["er"], ai, ALU.mult))
                link(TT(V["t2"], V["t2"], V["t3"], ALU.subtract))
                link(TT(V["t1"], V["t1"], V["t0"], ALU.mult))
                link(TT(V["t2"], V["t2"], V["t0"], ALU.mult))
                link(TT(V["t0"], bi, V["t2"], ALU.mult))
                link(TT(V["Gr"], br, V["t1"], ALU.mult))
                link(TT(V["Gr"], V["Gr"], V["t0"], ALU.subtract))
                link(TT(V["t0"], bi, V["t1"], ALU.mult))
                link(TT(V["Gi"], br, V["t2"], ALU.mult))
                link(TT(V["Gi"], V["Gi"], V["t0"], ALU.add))
                link(TS(V["t0"], V["Gi"], odc[:, 0:1], -2.0, ALU.mult, ALU.mult))
                link(TS(V["al"], V["Gr"], evc[:, 0:1], 2.0, ALU.mult, ALU.mult))
                link(TT(V["al"], V["al"], V["t0"], ALU.add))
                link(TS(V["t0"], V["Gi"], evc[:, 0:1], -2.0, ALU.mult, ALU.mult))
                link(TS(V["be"], V["Gr"], odc[:, 0:1], -2.0, ALU.mult, ALU.mult))
                TT(V["be"], V["be"], V["t0"], ALU.add).then_inc(s_albe, 1)
                nlo = [0]

                def second_parts(n):
                    for k, (src, m, dst, lo, _, _) in enumerate(jobs):
                        if lo is None or k < nlo[0]:
                            continue
                        if n == 0:
                            return
                        n -= 1
                        nlo[0] = k + 1
                        dve.wait_ge(s_hi, k + 1)
                        cols = banks[k % RING][:, 0:len(src) * m].rearrange("p (a b) -> p a b", b=m)
                        TT(lo, cols, dst.bitcast(F32), ALU.subtract).then_inc(s_lo, 1)

                g = {n: t[:, :, :] for n, t in big.items()}
                NL = 35
                for c in range(NHT // HCH):
                    hs = slice(c * HCH, (c + 1) * HCH)

                    def per_h(t, n):
                        return t[:, hs].unsqueeze(2).broadcast_to([P, HCH, n])

                    L = lst[:, :].unsqueeze(1).broadcast_to([P, HCH, NL])
                    if c:
                        dve.wait_ge(s_exp, c)
                        dve.wait_ge(s_sin, 2 * c)
                    link(TT(g["arg"], L, per_h(v["om"], NL), ALU.mult))
                    reduce(g["arg"], g["k"], g["r"]).then_inc(s_red, 1)
                    TT(g["arg"], L, per_h(v["sg"], NL), ALU.mult).then_inc(s_dec, 1)
                    second_parts(PER_CHUNK)
                    dve.wait_ge(s_sin, 2 * c + 2)
                    vc, vs = vre[:, c % 2], vim[:, c % 2]
                    link(TT(vc, vc, vc, ALU.mult))
                    link(TS(vc, vc, -2.0, 1.0, ALU.mult, ALU.add))
                    dve.wait_ge(s_exp, c + 1)
                    TT(vc, vc, g["e"], ALU.mult).then_inc(s_vals, 1)
                    TT(vs, vs, g["e"], ALU.mult).then_inc(s_vals, 1)
                second_parts(1000)
                for dst, src in ((cw[:, :, :], cw0[:, :, :]), (cb[:, :], cb0[:, :]), (cwb[:, :], cwb0[:, :]),
                                 (cbb[:, :], cbb0[:, :])):
                    link(TS(dst, src, 0.5, None, ALU.mult))
                link(dve.tensor_copy(emf[:, :], emap[:, :]))
                dve.wait_ge(s_masks, 9)
                link(dve.tensor_copy(earlier[:, :], earlier0[:, :]))
                link(dve.tensor_copy(later[:, :], later0[:, :]))
                for e in range(NE):
                    link(TS(onehot[:, e, :], emf[:, :], float(e), None, ALU.is_equal))
                dve.wait_ge(s_exps, 3)
                link(TS(negA[:, :], alog[:, :], -1.0, None, ALU.mult))
                link(TS(gate[:, :], gt0[:, :], 1.0, None, ALU.add))
                link(dve.reciprocal(al1[:, :], gate[:, :]))
                link(TS(be1[:, :], al1[:, :], -1.0, 1.0, ALU.mult, ALU.add))
                link(TS(al1[:, :], al1[:, :], 1.0, None, ALU.add))
                link(dve.memset(w_hi[:, :, FW - 1:FW].bitcast(F32), 0.0))
                link(dve.memset(w_lo[:, :, FW - 1:FW].bitcast(F32), 0.0))

        T2 = sb("T2", [P, HID])
        XM = sb("XM", [P, P])
        carried = nc.dram_tensor("carried", (TILES, P, HID + P), F32, kind="Internal").ap()
        H0 = sb("H0", [P, HID])
        XHT = sb("XHT", [P, KC, P])
        XI = sb("XI", [P, 2, P])
        TB = sb("TB", [P, 2, 2, NTAB])
        XSW = sb("XSW", [P, NST, 2])
        XTC = sb("XTC", [P, 2, 2, CS])
        W = sb("W", [P, 2, 4, CS])
        WI = sb("WI", [P, 2, 3, CS])
        VB = sb("VB", [P, 2, 16, 16])
        V2 = sb("V2", [P, 2, 16, 16])
        ST1 = sb("ST1", [P, 2, 6])
        MV1 = sb("MV1", [P, 2])
        VE1 = sb("VE1", [P, 1])
        RS1 = sb("RS1", [P, 1])
        SD1 = sb("SD1", [P, 1])
        CX = sb("CX", [P, 2, 4, CS])
        CB = sb("CB", [BCP, 4, CS])
        TH = sb("TH", [P, 2 * 4 * CS])
        THB = sb("THB", [BCP, 4 * CS])
        BT = sb("BT", [DST, 4 * CS])
        CT = sb("CT", [DST, 4 * CS])
        SZ = sb("SZ", [P, 512])
        XS = TH
        SQ = sb("SQ", [P, 256])
        RF = sb("RF", [P, 2, 2 * NH, CS], F32R)
        RB = sb("RB", [P, 2, 2 * NH, CS], F32R)
        AS = sb("AS", [P, 2, 2, 2, NH], F32R)
        CR = sb("CR", [BCP, 4, CS])
        CM = sb("CM", [BCP, 3, 4, CS])
        NM1 = sb("NM1", [P, 1])
        NM2 = sb("NM2", [P, 1])
        GTS = sb("GTS", [P, 2, P], F32R)
        HWS = sb("HWS", [P, 2, P], F32R)
        EX = sb("EX", [P, 2 * NH, CS])
        NB = sb("NB", [P, 2 * NH, CS])
        NF = sb("NF", [P, 2 * NH, CS])
        YT = NF
        XD = sb("XD", [P, 2 * NH, HD])
        GT = sb("GT", [P, P])
        SP16 = {n: sb("sp_" + n, [P, 2, 2, NH]) for n in ("x", "a", "u", "z", "w", "p", "dt", "aa")}
        DD = sb("DD", [P, 2 * NH])
        SSQ = sb("SSQ", [P, 2])
        MS = sb("MS", [P, 2])
        RS = sb("RS", [P, 2])
        ST2 = sb("ST2", [P, 2, 6])
        MV2 = sb("MV2", [P, 2])
        VE2 = sb("VE2", [P, 1])
        RS2 = sb("RS2", [P, 1])
        XHI = sb("XHI", [P, 2, KC, P], F32R)
        XLO = sb("XLO", [P, 2, KC, P], F32R)
        LG = sb("LG", [P, NR])
        NM = sb("NM", [P, 1])
        EL = sb("EL", [P, NR])
        SE = sb("SE", [P, 1])
        RE = sb("RE", [P, 1])
        PR = sb("PR", [P, NR])
        P8 = sb("P8", [P, 8])
        PQ = sb("PQ", [P, NR])
        PW = sb("PW", [P, NE, NR])
        WE = sb("WE", [P, NE])
        HW = sb("HW", [P, P])
        bO = banks[0:2]
        bR = banks[2]
        bK = banks[3]
        bT = banks[4]
        bX, bY, bZ = banks[5], banks[6], banks[7]
        FC0 = 4 * CS + 16

        NCONV, NDT, NSM = 2 * (TAPS - 1), 18, 9
        per = dict(cls_in=(1, 16), xswap=2, xt=1, xtc=1, wr=1, wi=2, wsum=1, v1=1, v2=1, vsum=1,
                   km=2, hev=4, st1=4, rs1=1, sd1=1, nm1=1, xh1=1, tt=2, tr1=2, xte=2, down=1, gelu=1,
                   pin=3, xms=1, conv0=4, conv=NCONV, cbm=TAPS - 1, cbc=TAPS - 1, dtc=NDT, asp=2, edt=1, th=2, xs=3, thz=1, sz=1, trx=1, gram=1, xse=1,
                   rf=2, rb=2, seg=1, ex=1, g4=4, dd=1, nf=1, nb=1, ns=1, mm=2, xd=1, yy=1, y1=1, yz=1, sq=2,
                   ms=1, rs=1, yn=2, tyn=1, yte=1, outp=1, u2=1, gt=1, gth=1, gtl=1,
                   fetched=(2, 16), up=2, h1=2, st2=4, rs2=1, nm2=1, hb=1, xh2=1, tr2=2, xhi=2, xlo=2,
                   rt=1, sm=NSM, se=1, hw=1, trh=1, hwe=1, hwl=1, o=2, fin=2)
        S = {}
        for n, c in per.items():
            c, unit = c if isinstance(c, tuple) else (c, 1)
            S[n] = Step(sem(n), c, unit)

        x_in = [sem("x_in_even"), sem("x_in_odd")]
        stored = [sem("stored_even"), sem("stored_odd")]
        carry = [sem("carry_even"), sem("carry_odd")]

        def wait_x(eng, i, p):
            eng.wait_ge(x_in[p], (i - p) * 24 + 48)

        def wait_carry(eng, t, p):
            if not (isinstance(t, int) and t < 0):
                eng.wait_ge(carry[p], (t - p) * 16 + 32)

        def wait_stored(eng, t, p):
            if not (isinstance(t, int) and t < 0):
                eng.wait_ge(stored[p], (t - p) * 16 + 32)

        def inc(ins, name):
            ins.then_inc(S[name].sem, S[name].unit)

        def wait(eng, n, **at):
            for name, j in at.items():
                S[name].after(eng, n, j)

        def apart(eng):
            eng.nop(nofuse=True)

        def active(i, lag, count):
            return (not isinstance(i, int)) or 0 <= i - lag < count

        def v3(ap, b):
            return ap.rearrange("p (a b) -> p a b", b=b)

        def decays(d, part):
            return AS[:, part, d, :, :].bitcast(F32).rearrange("p a h -> p (a h)").unsqueeze(2) \
                .broadcast_to([P, 2 * NH, CS])

        LOOP_FROM, LOOP_TO, LAST = 8, CLS - 2, TILES + 5
        assert CLS % 2 == 0 and LOOP_TO > LOOP_FROM

        def iterations(eng, body):
            for i in range(LOOP_FROM):
                body(i, i % 2)
            with eng.Fori(LOOP_FROM, LOOP_TO, 2) as m:
                for u in range(2):
                    body(m + u, u)
            for i in range(LOOP_TO, LAST):
                body(i, i % 2)

        with nc.Block() as block:

            @block.sync
            def _(sp):
                def body(i, p):
                    if isinstance(i, int) and i == 0:
                        load_x(0, 0)
                    if active(i, -1, CLS + 1) and not (isinstance(i, int) and i + 1 >= CLS):
                        load_x(i + 1, 1 - p)
                    if isinstance(i, int) and i == CLS:
                        wait(sp, i - 1, tr1=2, tt=2)
                        sp.dma_start(H0[:, :], cls_tok[0].broadcast_to([P, HID])).then_inc(S["cls_in"].sem, 16)
                    if active(i, 5, TILES):
                        store(i - 5, 1 - p)
                    if active(i, 3, TILES):
                        src = at(carried, i - 3)
                        wait_carry(sp, i - 3, 1 - p)
                        wait(sp, i - 4, tr2=2)
                        apart(sp)
                        wait(sp, i - 4, hb=1, gt=1)
                        apart(sp)
                        inc(sp.dma_start(T2[:, :], src[:, 0:HID]), "fetched")
                        inc(sp.dma_start(XM[:, :], src[:, HID:HID + P]), "fetched")
                    if active(i, 0, TILES):
                        dst = at(carried, i)
                        wait(sp, i, gelu=1)
                        apart(sp)
                        sp.dma_start(dst[:, HID:HID + P], U[:, p, 0, :]).then_inc(carry[p], 16)
                        wait(sp, i, tt=2)
                        apart(sp)
                        sp.dma_start(dst[:, 0:HID], T[:, p, :]).then_inc(carry[p], 16)

                def at(dram, t):
                    return dram[t] if isinstance(t, int) else dram[bass.ds(t, 1)].rearrange("a f k -> (a f) k")

                def load_x(t, p):
                    wait(sp, t - 2, xt=1, xswap=2, v1=1, wr=1, v2=1, wi=2)
                    apart(sp)
                    tb = tables[t] if isinstance(t, int) else tables[bass.ds(t, 1)].rearrange("a f b k -> (a f) b k")
                    sp.dma_start(TB[:, p, :, :], tb).then_inc(x_in[p], 16)
                    for b in range(2):
                        h = t * 2 + b
                        src = x[:, h, :, :].rearrange("c n r -> c (n r)") if isinstance(t, int) \
                            else x[:, bass.ds(h, 1), :, :].rearrange("c a n r -> c (a n r)")
                        sp.dma_start(XI[CS * b:CS * (b + 1), p, :], src).then_inc(x_in[p], 16)

                def store(t, p):
                    wait(sp, t, fin=2)
                    apart(sp)
                    if isinstance(t, int) and t == CLS:
                        sp.dma_start(out[:, 0, :], HB[0:CS, p, :]).then_inc(stored[p], 16)
                        return
                    for b in range(2):
                        row = t * 2 + b + 1
                        dst = out[:, row, :] if isinstance(t, int) else out[:, bass.ds(row, 1), :].rearrange("c a d -> c (a d)")
                        sp.dma_start(dst, HB[CS * b:CS * (b + 1), p, :]).then_inc(stored[p], 16)

                iterations(sp, body)
                sp.wait_ge(stored[0], 16 * (CLS + 1))
                sp.wait_ge(stored[1], 16 * CLS)

            @block.gpsimd
            def _(pool):
                def body(i, p):
                    A, A1, D = active(i, 0, CLS), active(i, 0, TILES), active(i, 4, TILES)
                    H, G = active(i, 1, TILES + 2), active(i, 2, TILES + 2)
                    q, r, td = i - 1, i - 2, i - 4

                    def swap(k):
                        if A:
                            wait_x(pool, i, p)
                            wait(pool, i - 1, xt=1)
                            apart(pool)
                            xi = XI[:, p, :].rearrange("p (n r) -> p n r", r=2)
                            inc(pool.tensor_copy(XSW[:, :, k], xi[:, :, 1 - k]), "xswap")

                    def kernel_q():
                        if A:
                            wait_x(pool, i, p)
                            wait(pool, i - 1, vsum=1)
                            inc(pool.tensor_tensor(V2[:, :, :, :], TB[:, p, :, TQ].unsqueeze(2).broadcast_to([P, 2, 16, 16]),
                                                   TB[:, p, :, TJI].unsqueeze(3).broadcast_to([P, 2, 16, 16]), ALU.mult), "v2")

                    def shift_imag():
                        if A:
                            wait(pool, i, xtc=1)
                            wait(pool, i - 1, wsum=1)
                            inc(pool.tensor_tensor(WI[:, :, :, :], XTC[:, 1, :, :].unsqueeze(2).broadcast_to([P, 2, 3, CS]),
                                                   TB[:, p, :, TSI].unsqueeze(3).broadcast_to([P, 2, 3, CS]), ALU.mult), "wi")

                    def shift_none():
                        if A:
                            wait(pool, i, xtc=1)
                            wait(pool, i - 1, km=2)
                            apart(pool)
                            inc(pool.tensor_copy(W[:, :, 0, :], XTC[:, 0, :, :]), "wi")

                    def gram_back():
                        if G:
                            wait(pool, r, g4=4)
                            wait(pool, r - 1, ns=1)
                            dtB = SP16["dt"][:, 1, :, :].unsqueeze(3).broadcast_to([P, 2, NH, CS])
                            inc(pool.tensor_tensor(NB[:, :, :].rearrange("p (a h) t -> p a h t", a=2),
                                                   GB[:, :, :].unsqueeze(2).broadcast_to([P, 2, NH, CS]), dtB, ALU.mult), "nb")

                    def skip():
                        if G:
                            wait(pool, r, xse=1, dd=1)
                            wait(pool, r - 1, yn=2, tyn=1)
                            inc(pool.tensor_tensor(XD[:, :, :], v3(XS[:, :], HD),
                                                   DD[:, :].unsqueeze(2).broadcast_to([P, 2 * NH, HD]), ALU.mult), "xd")

                    def root_y():
                        if G:
                            wait(pool, r, ms=1)
                            wait(pool, r - 1, yn=2)
                            inc(pool.tensor_tensor(RS[:, :], MS[:, :], half_neg[:, :], ALU.pow), "rs")

                    def root_1():
                        if A1:
                            wait(pool, i, st1=4)
                            wait(pool, i - 1, xh1=1, sd1=1)
                            inc(pool.tensor_tensor(RS1[:, :], VE1[:, :], half_neg[:, 0:1], ALU.pow), "rs1")

                    def root_2():
                        if D:
                            wait(pool, td, st2=4)
                            wait(pool, td - 1, xh2=1)
                            inc(pool.tensor_tensor(RS2[:, :], VE2[:, :], half_neg[:, 0:1], ALU.pow), "rs2")

                    def start_out():
                        if D:
                            wait(pool, td, h1=2)
                            wait_stored(pool, td - 2, p)
                            inc(pool.tensor_tensor(HB[:, p, :], T2[:, :], bbase[:, :], ALU.add), "hb")

                    def decays_back(part):
                        if H:
                            wait(pool, q, asp=2)
                            wait(pool, r, seg=1)
                            inc(pool.tensor_tensor(RB[:, part, :, :], m_gt[:, :].unsqueeze(1).broadcast_to([P, 2 * NH, CS]),
                                                   decays(1, part), ALU.mult), "rb")

                    def add_bc(s):
                        if H:
                            wait(pool, q, cbm=s)
                            if s > 1:
                                wait(pool, q, cbc=s - 1)
                            inc(pool.tensor_tensor(CB[:, :, s:CS], CB[:, :, s:CS], CM[:, s % 3, :, 0:CS - s], ALU.add), "cbc")

                    def carry_h():
                        if A1:
                            wait(pool, i, sd1=1, xh1=1)
                            wait_carry(pool, i - 2, p)
                            apart(pool)
                            inc(pool.tensor_scalar(T[:, p, :], H0[:, :], SD1[:, 0:1], MV1[:, 0:1], ALU.mult, ALU.add), "tt")

                    def carry_bias():
                        if A1:
                            wait(pool, i, tt=1)
                            inc(pool.tensor_tensor(T[:, p, :], T[:, p, :], bup[:, :], ALU.add), "tt")

                    swap(0)
                    swap(1)
                    gram_back()
                    kernel_q()
                    skip()
                    shift_imag()
                    shift_none()
                    root_y()
                    root_1()
                    add_bc(1)
                    add_bc(2)
                    add_bc(3)
                    start_out()
                    root_2()
                    add_bc(4)
                    carry_h()
                    add_bc(5)
                    add_bc(6)
                    decays_back(0)
                    decays_back(1)
                    carry_bias()

                iterations(pool, body)

            @block.scalar
            def _(act):
                def copy(dst, src, name, scale=1.0):
                    inc(act.activation(dst, src, ACT.Copy, scale=scale), name)

                def body(i, p):
                    A, A1 = active(i, 0, CLS), active(i, 0, TILES)
                    D, E = active(i, 4, TILES), active(i, 5, TILES)
                    H, G = active(i, 1, TILES + 2), active(i, 2, TILES + 2)
                    q, r, td, te = i - 1, i - 2, i - 4, i - 5

                    def conv_first(c):
                        if H:
                            wait(act, q, pin=1 if c < 2 else 2)
                            wait(act, q - 1, trx=1, gram=1)
                            if c < 2:
                                src = bX[:, :].rearrange("p (c g t) -> p c g t", c=2, g=4)[:, c]
                                inc(act.activation(CX[:, c], src, ACT.Identity, bias=cb[:, c:c + 1],
                                                   scale=cw[:, c, TAPS - 1:TAPS]), "conv0")
                            else:
                                src = bY[0:BCP, 0:256].rearrange("p (g t) -> p g t", g=4)
                                inc(act.activation(CB[:, :, :], src, ACT.Identity, bias=cbb[:, 0:1],
                                                   scale=cwb[:, TAPS - 1:TAPS]), "conv0")

                    def keep_bc():
                        if H:
                            wait(act, q, pin=2)
                            wait(act, q - 1, cbm=TAPS - 1)
                            copy(CR[:, :, :], bY[0:BCP, 0:256].rearrange("p (g t) -> p g t", g=4), "conv0")

                    def scale_bc(s):
                        if H:
                            wait(act, q, conv0=4)
                            if s > 3:
                                wait(act, q, cbc=s - 3)
                            else:
                                wait(act, q - 1, cbc=TAPS - 1)
                            k = TAPS - 1 - s
                            copy(CM[:, s % 3, :, 0:CS], CR[:, :, :], "cbm", scale=cwb[:, k:k + 1])

                    def norm_y(a):
                        if G:
                            wait(act, r, rs=1)
                            ya = v3(XD[:, :, :].rearrange("p a b -> p (a b)"), 256)[:, a, :]
                            inc(act.activation(ya, ya, ACT.Copy, scale=RS[:, a:a + 1]), "yn")

                    def norm_1():
                        if A1:
                            wait(act, i, nm1=1, rs1=1)
                            inc(act.activation(H0[:, :], H0[:, :], ACT.Identity, bias=NM1[:, 0:1], scale=RS1[:, 0:1]), "xh1")

                    def norm_2():
                        if D:
                            wait(act, td, nm2=1, rs2=1, hb=1)
                            inc(act.activation(T2[:, :], T2[:, :], ACT.Identity, bias=NM2[:, 0:1], scale=RS2[:, 0:1]), "xh2")

                    def gated_hi():
                        if D:
                            wait(act, td, gt=1)
                            wait(act, td - 1, up=2)
                            copy(GTS[:, 0, :], GT[:, :], "gth")

                    def keep_x():
                        if A:
                            wait(act, i, xt=1)
                            wait(act, i - 1, wr=1, wi=2)
                            copy(XTC[:, :, :, :].rearrange("p a b c -> p (a b c)"), bK[:, 0:256], "xtc")

                    def keep_xs():
                        if G:
                            wait(act, r, trx=1, xs=3)
                            wait(act, r - 1, xd=1)
                            copy(XS[:, :], bX[:, :], "xse")

                    def exp_decays():
                        if G:
                            wait(act, r, seg=1)
                            inc(act.activation(EX[:, :, :].rearrange("p a b -> p (a b)"), bZ[:, :], ACT.Exp), "ex")

                    def keep_h(b, h):
                        if A:
                            wait(act, i, km=b + 1)
                            wait(act, i - 1, tr1=2, tt=2)
                            copy(H0[CS * b:CS * (b + 1), HALF * h:HALF * (h + 1)], bK[CS * h:CS * (h + 1), :], "hev")

                    def exp_router():
                        if E:
                            wait(act, te, sm=2)
                            wait(act, te - 1, sm=NSM)
                            inc(act.activation(EL[:, :], LG[:, :], ACT.Exp, bias=NM[:, 0:1], accum_out=SE[:, 0:1]), "se")

                    def squares(a):
                        if G:
                            wait(act, r, yz=1)
                            wait(act, r - 1, ms=1)
                            if a:
                                wait(act, r, sq=1)
                            inc(act.activation(SQ[:, :], v3(XD[:, :, :].rearrange("p a b -> p (a b)"), 256)[:, a, :],
                                               ACT.Square, accum_out=SSQ[:, a:a + 1]), "sq")

                    def keep_y():
                        if G:
                            wait(act, r, tyn=1, mm=2)
                            wait(act, r - 1, outp=1)
                            copy(YT[:, :, :].rearrange("p a b -> p (a b)"), bZ[:, :], "yte")

                    def keep_w():
                        if E:
                            wait(act, te, trh=1)
                            wait(act, te - 1, o=2)
                            copy(HWS[:, 0, :], bR[:, 256:384], "hwe", scale=2.0)

                    def exp_dt():
                        if H:
                            wait(act, q, dtc=2)
                            inc(act.activation(SP16["u"][:, :, :, :], SP16["a"][:, :, :, :], ACT.Exp), "edt")

                    def tanh_z():
                        if H:
                            wait(act, q, pin=3)
                            wait(act, r, yz=1)
                            inc(act.activation(SZ[:, :], bZ[:, :], ACT.Tanh), "thz")

                    def keep_turned(g):
                        if A1:
                            wait(act, i, tr1=g + 1)
                            wait(act, i - 1, down=1)
                            copy(XHT[:, 4 * g:4 * g + 4, :], v3(bT[:, :], P), "xte")

                    def tanh_x():
                        if H:
                            wait(act, q, conv=NCONV)
                            wait(act, r, yy=1, xd=1)
                            inc(act.activation(TH[:, :], CX[:, :, :, :].rearrange("p a b c -> p (a b c)"), ACT.Tanh), "th")

                    def tanh_bc():
                        if H:
                            wait(act, q, cbc=TAPS - 1)
                            wait(act, r, xs=3)
                            inc(act.activation(THB[:, :], CB[:, :, :].rearrange("p b c -> p (b c)"), ACT.Tanh), "th")

                    def split_hi(g):
                        if D:
                            wait(act, td, tr2=g + 1)
                            wait(act, td - 2, o=2)
                            copy(XHI[:, p, 4 * g:4 * g + 4, :], v3(bT[:, :], P), "xhi")

                    def gelu():
                        if A1:
                            wait(act, i, down=1)
                            wait(act, i - 2, pin=3)
                            wait_carry(act, i - 2, p)
                            inc(act.activation(U[:, p, 0, :], bK[:, 0:P], ACT.Gelu, bias=bdn[:, 0:1]), "gelu")

                    exp_decays()
                    keep_x()
                    keep_xs()
                    keep_h(0, 0)
                    squares(0)
                    squares(1)
                    keep_h(0, 1)
                    conv_first(0)
                    conv_first(1)
                    norm_y(0)
                    norm_y(1)
                    keep_h(1, 0)
                    keep_h(1, 1)
                    keep_y()
                    gated_hi()
                    exp_router()
                    conv_first(2)
                    keep_bc()
                    scale_bc(1)
                    scale_bc(2)
                    exp_dt()
                    scale_bc(3)
                    norm_1()
                    scale_bc(4)
                    keep_turned(0)
                    scale_bc(5)
                    tanh_z()
                    scale_bc(6)
                    keep_w()
                    keep_turned(1)
                    norm_2()
                    tanh_x()
                    split_hi(0)
                    tanh_bc()
                    gelu()
                    split_hi(1)

                iterations(act, body)

            @block.vector
            def _(dve):
                TT, TS, STT = dve.tensor_tensor, dve.tensor_scalar, dve.scalar_tensor_tensor

                def body(i, p):
                    A, A1 = active(i, 0, CLS), active(i, 0, TILES)
                    D, E = active(i, 4, TILES), active(i, 5, TILES)
                    H, G = active(i, 1, TILES + 2), active(i, 2, TILES + 2)
                    q, r, td, te = i - 1, i - 2, i - 4, i - 5
                    xd = XD[:, :, :].rearrange("p a b -> p (a b)")

                    def conv(s, c):
                        if H:
                            if s == 1:
                                wait(dve, q, conv0=2)
                            else:
                                wait(dve, q, conv=2 * (s - 2) + c + 1)
                            src = bX[:, :].rearrange("p (c g t) -> p c g t", c=2, g=4)[:, c]
                            k = TAPS - 1 - s
                            inc(STT(CX[:, c, :, s:CS], src[:, :, 0:CS - s], cw[:, c, k:k + 1], CX[:, c, :, s:CS],
                                    ALU.mult, ALU.add), "conv")

                    def softplus(j):
                        if not H:
                            return
                        f = {n: t[:, :, :, :] for n, t in SP16.items()}
                        if j > 0:
                            wait(dve, q, dtc=j)
                        if j == 0:
                            wait(dve, q, conv0=4)
                            wait(dve, q - 1, nb=1)
                            ins = TT(f["x"], bY[:, 256:272].rearrange("p (a d h) -> p d a h", a=2, d=2),
                                     dtb[:, :].unsqueeze(1).unsqueeze(1).broadcast_to([P, 2, 2, NH]), ALU.add)
                        elif j == 1:
                            wait(dve, q - 1, edt=1)
                            ins = STT(f["a"], f["x"], -1.0, f["x"], ALU.mult, ALU.min)
                        elif j == 2:
                            wait(dve, q, edt=1)
                            ins = TS(f["z"], f["u"], 2.0, None, ALU.add)
                        elif j == 3:
                            ins = dve.reciprocal(f["w"], f["z"])
                        elif j == 4:
                            ins = TT(f["z"], f["u"], f["w"], ALU.mult)
                        elif j == 5:
                            ins = TT(f["w"], f["z"], f["z"], ALU.mult)
                        elif j == 6:
                            ins = TS(f["p"], f["w"], 1.0 / 17, None, ALU.mult)
                        elif j < 14:
                            ins = STT(f["p"], f["p"], 1.0 / (29 - 2 * j), f["w"], ALU.add, ALU.mult)
                        elif j == 14:
                            ins = STT(f["p"], f["p"], 1.0, f["z"], ALU.add, ALU.mult)
                        elif j == 15:
                            ins = TS(f["x"], f["x"], 0.0, None, ALU.max)
                        elif j == 16:
                            wait(dve, q - 1, nb=1)
                            ins = STT(f["dt"], f["p"], 2.0, f["x"], ALU.mult, ALU.add)
                        elif j == 17:
                            ins = TT(f["aa"], f["dt"],
                                     negA[:, :].unsqueeze(1).unsqueeze(1).broadcast_to([P, 2, 2, NH]), ALU.mult)
                        inc(ins, "dtc")

                    def kernel_p():
                        if A:
                            wait_x(dve, i, p)
                            wait(dve, i - 1, km=2)
                            inc(TT(VB[:, :, :, :], TB[:, p, :, TP].unsqueeze(2).broadcast_to([P, 2, 16, 16]),
                                   TB[:, p, :, TJR].unsqueeze(3).broadcast_to([P, 2, 16, 16]), ALU.mult), "v1")

                    def kernel_sum():
                        if A:
                            wait(dve, i, v2=1, v1=1)
                            inc(TT(VB[:, :, :, :], VB[:, :, :, :], V2[:, :, :, :], ALU.add), "vsum")

                    def shift_real():
                        if A:
                            wait(dve, i, xtc=1)
                            wait(dve, i - 1, km=2)
                            inc(TT(W[:, :, 1:4, :], XTC[:, 0, :, :].unsqueeze(2).broadcast_to([P, 2, 3, CS]),
                                   TB[:, p, :, TSR].unsqueeze(3).broadcast_to([P, 2, 3, CS]), ALU.mult), "wr")

                    def shift_sum():
                        if A:
                            wait(dve, i, wi=1, wr=1)
                            inc(TT(W[:, :, 1:4, :], W[:, :, 1:4, :], WI[:, :, :, :], ALU.add), "wsum")

                    def gram(b, d):
                        if G:
                            wait(dve, r, gram=1)
                            wait(dve, r - 1, nb=1, nf=1)
                            rows = slice(CS * b, CS * (b + 1))
                            gr = bY[rows, 0:256].rearrange("p (a c) -> p a c", a=2)
                            if d == 0:
                                ins = TT(GF[rows, :, 1:CS], gr[:, :, CS * b:CS * b + CS - 1],
                                         m_lt[rows, 1:CS].unsqueeze(1).broadcast_to([CS, 2, CS - 1]), ALU.mult)
                            else:
                                ins = TT(GB[rows, :, 0:CS - 1], gr[:, :, CS * b + 1:CS * b + CS],
                                         m_gt[rows, 0:CS - 1].unsqueeze(1).broadcast_to([CS, 2, CS - 1]), ALU.mult)
                            inc(ins, "g4")

                    def skip_scale():
                        if G:
                            wait(dve, r, gram=1)
                            wait(dve, r - 1, xd=1)
                            inc(TT(DD[:, :].rearrange("p (a h) -> p a h", a=2), v3(bY[:, FC0:FC0 + 2 * NH], NH),
                                   Dbc[:, :].unsqueeze(1).broadcast_to([P, 2, NH]), ALU.add), "dd")

                    def gram_forth():
                        if G:
                            wait(dve, r, g4=4)
                            wait(dve, r - 1, outp=1, mm=2)
                            dtF = SP16["dt"][:, 0, :, :].unsqueeze(3).broadcast_to([P, 2, NH, CS])
                            inc(TT(NF[:, :, :].rearrange("p (a h) t -> p a h t", a=2),
                                   GF[:, :, :].unsqueeze(2).broadcast_to([P, 2, NH, CS]), dtF, ALU.mult), "nf")

                    def gram_sum():
                        if G:
                            wait(dve, r, nf=1, nb=1)
                            inc(TT(NF[:, :, :], NF[:, :, :], NB[:, :, :], ALU.add), "ns")

                    def mix_matrix(b):
                        if G:
                            wait(dve, r, ns=1, ex=1)
                            wait(dve, r - 1, yy=1)
                            rows = slice(CS * b, CS * (b + 1))
                            inc(TT(Mt[rows, :, :, rows].rearrange("p a h t -> p (a h) t"), NF[rows, :, :], EX[rows, :, :],
                                   ALU.mult), "mm")

                    def add_skip():
                        if G:
                            wait(dve, r, yy=1, xd=1)
                            inc(TT(xd, bX[:, :], xd, ALU.add), "y1")

                    def times_z():
                        if G:
                            wait(dve, r, y1=1, sz=1)
                            inc(TT(xd, xd, SZ[:, :], ALU.mult), "yz")

                    def mean_square():
                        if G:
                            wait(dve, r, sq=2)
                            wait(dve, r - 1, rs=1)
                            inc(TS(MS[:, :], SSQ[:, :], 1.0 / DIN, EPS, ALU.mult, ALU.add), "ms")

                    def gated_lo():
                        if D:
                            wait(dve, td, gth=1)
                            inc(TT(GTS[:, 1, :], GT[:, :], GTS[:, 0, :].bitcast(F32), ALU.subtract), "gtl")

                    def weighted_lo():
                        if E:
                            wait(dve, te, hwe=1)
                            inc(STT(HWS[:, 1, :], bR[:, 256:384], 2.0, HWS[:, 0, :].bitcast(F32), ALU.mult, ALU.subtract), "hwl")

                    def layer_out():
                        if G:
                            wait(dve, r, outp=1)
                            wait(dve, r - 1, pin=3)
                            inc(dve.tensor_copy(U[:, p, 1, :], bY[:, 0:P]), "u2")

                    def router(j):
                        if not E:
                            return
                        if j:
                            wait(dve, te, sm=j)
                        if j == 0:
                            wait(dve, te, rt=1)
                            wait(dve, te - 1, se=1)
                            inc(TT(LG[:, :], bR[:, P:P + NR], rbias[:, :], ALU.add), "sm")
                        elif j == 1:
                            wait(dve, te - 1, se=1)
                            inc(dve.tensor_reduce(NM[:, :], LG[:, :], AX.X, ALU.max, negate=True), "sm")
                        elif j == 2:
                            wait(dve, te, se=1)
                            inc(dve.reciprocal(RE[:, :], SE[:, :]), "sm")
                        elif j == 3:
                            inc(TS(PR[:, :], EL[:, :], RE[:, 0:1], None, ALU.mult), "sm")
                        elif j == 4:
                            apart(dve)
                            inc(dve.max(P8[:, :], PR[:, :]), "sm")
                        elif j == 5:
                            apart(dve)
                            inc(dve.match_replace(PQ[:, :], P8[:, :], PR[:, :], 0.0), "sm")
                        elif j == 6:
                            inc(TT(PQ[:, :], PR[:, :], PQ[:, :], ALU.subtract), "sm")
                        elif j == 7:
                            inc(TT(PW[:, :, :], onehot[:, :, :], PQ[:, :].unsqueeze(1).broadcast_to([P, NE, NR]),
                                   ALU.mult), "sm")
                        elif j == 8:
                            inc(dve.tensor_reduce(WE[:, :], PW[:, :, :], AX.X, ALU.add), "sm")
                        elif j == 9:
                            wait(dve, te - 1, trh=1)
                            inc(TT(HW[:, :].rearrange("p (e r) -> p e r", e=NE), bR[:, 0:P].rearrange("p (e r) -> p e r", e=NE),
                                   WE[:, :].unsqueeze(2).broadcast_to([P, NE, RK]), ALU.mult), "hw")

                    def stats_1(j):
                        if not A1:
                            return
                        if j < 2:
                            if isinstance(i, int) and i == CLS:
                                dve.wait_ge(S["cls_in"].sem, 16)
                            else:
                                wait(dve, i, hev=4)
                            inc(dve.bn_stats(ST1[:, j, :], H0[:, HALF * j:HALF * (j + 1)]), "st1")
                        elif j == 2:
                            wait(dve, i, st1=2)
                            wait(dve, i - 1, tt=2)
                            apart(dve)
                            inc(dve.bn_aggr(MV1[:, :], ST1[:, :, :].rearrange("p a b -> p (a b)")), "st1")
                        else:
                            wait(dve, i, st1=3)
                            inc(TS(VE1[:, :], MV1[:, 1:2], EPS, None, ALU.add), "st1")

                    def shift_1():
                        if A1:
                            wait(dve, i, rs1=1)
                            wait(dve, i - 1, xh1=1)
                            inc(STT(NM1[:, :], MV1[:, 0:1], -1.0, RS1[:, 0:1], ALU.mult, ALU.mult), "nm1")

                    def deviation_1():
                        if A1:
                            wait(dve, i, rs1=1)
                            wait(dve, i - 1, tt=1)
                            inc(TS(SD1[:, :], VE1[:, :], RS1[:, 0:1], 1.0, ALU.mult, ALU.add), "sd1")

                    def gated_a():
                        if D:
                            wait(dve, td, fetched=2)
                            inc(TS(XM[:, :], XM[:, :], al1[:, 0:1], None, ALU.mult), "xms")

                    def gated_b():
                        if D:
                            wait(dve, td, xms=1)
                            wait(dve, r, outp=1)
                            wait(dve, td - 1, gth=1, gtl=1)
                            inc(STT(GT[:, :], bY[:, P:2 * P], be1[:, 0:1], XM[:, :], ALU.mult, ALU.add), "gt")

                    def residual(h):
                        if D:
                            wait(dve, td, up=h + 1, fetched=2)
                            c = slice(HALF * h, HALF * (h + 1))
                            inc(TT(T2[:, c], bT[:, :], T2[:, c], ALU.add), "h1")

                    def stats_2(j):
                        if not D:
                            return
                        if j < 2:
                            wait(dve, td, h1=j + 1)
                            inc(dve.bn_stats(ST2[:, j, :], T2[:, HALF * j:HALF * (j + 1)]), "st2")
                        elif j == 2:
                            wait(dve, td, st2=2)
                            apart(dve)
                            inc(dve.bn_aggr(MV2[:, :], ST2[:, :, :].rearrange("p a b -> p (a b)")), "st2")
                        else:
                            wait(dve, td, st2=3)
                            inc(TS(VE2[:, :], MV2[:, 1:2], EPS, None, ALU.add), "st2")

                    def shift_2():
                        if D:
                            wait(dve, td, rs2=1)
                            wait(dve, td - 1, xh2=1)
                            inc(STT(NM2[:, :], MV2[:, 0:1], -1.0, RS2[:, 0:1], ALU.mult, ALU.mult), "nm2")

                    def split_lo(g):
                        if D:
                            wait(dve, td, xhi=g + 1)
                            wait(dve, td - 2, o=2)
                            ks = slice(4 * g, 4 * g + 4)
                            inc(TT(XLO[:, p, ks, :], v3(bT[:, :], P), XHI[:, p, ks, :].bitcast(F32), ALU.subtract), "xlo")

                    def silu_z():
                        if H:
                            wait(dve, q, thz=1, pin=3)
                            inc(STT(SZ[:, :], SZ[:, :], 1.0, bZ[:, :], ALU.add, ALU.mult), "sz")

                    def decays_forth(part):
                        if H:
                            wait(dve, q, asp=part + 1)
                            wait(dve, r, seg=1)
                            inc(TT(RF[:, part, :, :], m_lt[:, :].unsqueeze(1).broadcast_to([P, 2 * NH, CS]),
                                   decays(0, part), ALU.mult), "rf")

                    def split_decays(part):
                        if H:
                            if part == 0:
                                wait(dve, q, dtc=NDT)
                                wait(dve, r, rb=2, rf=2)
                                inc(dve.tensor_copy(AS[:, 0], SP16["aa"][:, :, :, :]), "asp")
                            else:
                                wait(dve, q, asp=1)
                                inc(TT(AS[:, 1], SP16["aa"][:, :, :, :], AS[:, 0].bitcast(F32), ALU.subtract), "asp")

                    def silu_x():
                        if H:
                            wait(dve, q, th=1)
                            wait(dve, r, trx=1, gram=1)
                            cx = CX[:, :, :, :].rearrange("p a b c -> p (a b c)")
                            inc(STT(cx, TH[:, :], 1.0, cx, ALU.add, ALU.mult), "xs")

                    def silu_bc(k):
                        if H:
                            wait(dve, q, th=2)
                            wait(dve, r, gram=1)
                            cbf = CB[:, :, :].rearrange("p b c -> p (b c)")
                            n = slice(32 * k, 32 * k + DST)
                            inc(STT((BT, CT)[k][:, :], THB[n, :], 1.0, cbf[n, :], ALU.add, ALU.mult), "xs")

                    def final(h):
                        if E:
                            wait(dve, te, o=h + 1, hb=1)
                            c = slice(HALF * h, HALF * (h + 1))
                            inc(TT(HB[:, 1 - p, c], bO[h][:, :], HB[:, 1 - p, c], ALU.add), "fin")

                    gram(0, 0)
                    gram(0, 1)
                    gram(1, 0)
                    gram(1, 1)
                    skip_scale()
                    kernel_p()
                    gram_forth()
                    gram_sum()
                    mix_matrix(0)
                    mix_matrix(1)
                    shift_real()
                    gated_a()
                    kernel_sum()
                    shift_sum()
                    add_skip()
                    times_z()
                    mean_square()
                    conv(1, 0)
                    conv(1, 1)
                    conv(2, 0)
                    conv(2, 1)
                    conv(3, 0)
                    stats_1(0)
                    stats_1(1)
                    gated_b()
                    layer_out()
                    router(0)
                    conv(3, 1)
                    gated_lo()
                    stats_1(2)
                    router(1)
                    stats_1(3)
                    conv(4, 0)
                    conv(4, 1)
                    router(2)
                    shift_1()
                    residual(0)
                    softplus(0)
                    router(3)
                    softplus(1)
                    stats_2(0)
                    softplus(2)
                    router(4)
                    softplus(3)
                    residual(1)
                    softplus(4)
                    router(5)
                    softplus(5)
                    stats_2(1)
                    softplus(6)
                    router(6)
                    softplus(7)
                    router(7)
                    softplus(8)
                    deviation_1()
                    softplus(9)
                    router(8)
                    softplus(10)
                    stats_2(2)
                    softplus(11)
                    router(9)
                    softplus(12)
                    stats_2(3)
                    conv(5, 0)
                    softplus(13)
                    conv(5, 1)
                    softplus(14)
                    conv(6, 0)
                    softplus(15)
                    shift_2()
                    softplus(16)
                    weighted_lo()
                    softplus(17)
                    conv(6, 1)
                    split_decays(0)
                    silu_z()
                    split_decays(1)
                    decays_forth(0)
                    silu_x()
                    final(0)
                    split_lo(0)
                    silu_bc(0)
                    silu_bc(1)
                    final(1)
                    decays_forth(1)
                    split_lo(1)

                iterations(dve, body)

            @block.tensor
            def _(pe):
                mm, tr = pe.matmul, pe.transpose

                def body(i, p):
                    A, A1 = active(i, 0, CLS), active(i, 0, TILES)
                    D, E = active(i, 4, TILES), active(i, 5, TILES)
                    H, G = active(i, 1, TILES + 2), active(i, 2, TILES + 2)
                    q, r, td, te = i - 1, i - 2, i - 4, i - 5
                    u = U[:, 1 - p, :, :].rearrange("p a t -> p (a t)")

                    def ffn(c0, c1, bank, ks, last=None):
                        for k in ks:
                            for n, (xs_, ws) in enumerate(((XHI, w_hi), (XHI, w_lo), (XLO, w_hi))):
                                ins = mm(bank[:, 0:c1 - c0], xs_[:, 1 - p, k, :], ws[:, k, c0:c1],
                                         start=(k == 0 and n == 0), stop=(last == k and n == 2))
                        return ins

                    def route(a, b):
                        if E:
                            if a == 0:
                                wait(pe, te, xlo=2)
                                wait(pe, te - 1, hwl=1)
                            ins = ffn(HID, FW, bR, range(a, b), last=KC - 1)
                            if b == KC:
                                inc(ins, "rt")

                    def bases(h, a, b):
                        if E:
                            if a == 0:
                                wait(pe, te, xlo=2)
                                wait(pe, te - 1, fin=h + 1)
                            ffn(HALF * h, HALF * (h + 1), bO[h], range(a, b))

                    def turn_h():
                        if E:
                            wait(pe, te, hw=1)
                            inc(tr(bR[:, 256:256 + P], HW[:, :], ident[:, :]), "trh")

                    def lora(h):
                        if E:
                            wait(pe, te, hwl=1)
                            c = slice(HALF * h, HALF * (h + 1))
                            mm(bO[h][:, :], HWS[:, 0, :], lb_hi[:, c], start=False, stop=False)
                            mm(bO[h][:, :], HWS[:, 1, :], lb_hi[:, c], start=False, stop=False)
                            inc(mm(bO[h][:, :], HWS[:, 0, :], lb_lo[:, c], start=False, stop=True), "o")

                    def up(h):
                        if D:
                            if h == 0:
                                wait(pe, td, gtl=1)
                                bT_free(UP)
                            else:
                                wait(pe, td, h1=1)
                            c = slice(HALF * h, HALF * (h + 1))
                            mm(bT[:, :], GTS[:, 0, :], wu_hi[:, c], start=True, stop=False)
                            mm(bT[:, :], GTS[:, 1, :], wu_hi[:, c], start=False, stop=False)
                            inc(mm(bT[:, :], GTS[:, 0, :], wu_lo[:, c], start=False, stop=True), "up")

                    def turn_d(g):
                        if D:
                            if g == 0:
                                wait(pe, td, xh2=1)
                                bT_free(TURN_D)
                            else:
                                wait(pe, td, xlo=1)
                            for k in range(4):
                                ins = tr(bT[:, P * k:P * (k + 1)], T2[:, (4 * g + k) * P:(4 * g + k + 1) * P], ident[:, :])
                            inc(ins, "tr2")

                    def turn_a(g):
                        if A1:
                            if g == 0:
                                wait(pe, i, xh1=1)
                                bT_free(TURN_A)
                            else:
                                wait(pe, i, xte=1)
                            for k in range(4):
                                ins = tr(bT[:, P * k:P * (k + 1)], H0[:, (4 * g + k) * P:(4 * g + k + 1) * P], ident[:, :])
                            inc(ins, "tr1")

                    def bT_free(user):
                        if user == TURN_D:
                            wait(pe, min(i, CLS) if isinstance(i, int) else i, xte=2)
                            wait(pe, td, h1=2)
                        elif user == TURN_A:
                            if D:
                                wait(pe, td, h1=2)
                            wait(pe, td - 1, xlo=2)
                        else:
                            wait(pe, td - 1, xlo=2)
                            wait(pe, min(i - 1, CLS) if isinstance(i, int) else i - 1, xte=2)

                    def s4d(b):
                        if A:
                            if b == 0:
                                wait(pe, i, xtc=1, wsum=1, wi=2, vsum=1)
                            else:
                                wait(pe, i, hev=2)
                            for s in range(2):
                                ins = mm(bK[:, 256 * s:256 * (s + 1)], W[:, b, 2 * s:2 * s + 2, :].rearrange("p a c -> p (a c)"),
                                         VB[:, b, :, :].rearrange("p a c -> p (a c)"), start=True, stop=True)
                            inc(ins, "km")

                    def down():
                        if A1:
                            wait(pe, i, xte=2)
                            if A:
                                wait(pe, i, hev=4)
                            for k in range(KC):
                                ins = mm(bK[:, 0:P], wdT[:, k, :], XHT[:, k, :], start=(k == 0), stop=(k == KC - 1))
                            inc(ins, "down")

                    def turn_x():
                        if A:
                            wait_x(pe, i, p)
                            wait(pe, i, xswap=2)
                            wait(pe, i - 1, gelu=1)
                            tr(bK[:, 0:P], XI[:, p, :], ident[:, :])
                            inc(tr(bK[:, P:2 * P], XSW[:, :, :].rearrange("p n r -> p (n r)"), ident[:, :]), "xt")

                    def project_x():
                        if H:
                            u_ready()
                            wait(pe, r, y1=1)
                            for c in range(2):
                                ins = mm(bX[:, 256 * c:256 * (c + 1)], wx[:, P * c:P * (c + 1)], u, start=True, stop=True)
                            inc(ins, "pin")

                    def project_bc():
                        if H:
                            wait(pe, min(q, TILES - 1) if isinstance(i, int) else q, gelu=1)
                            wait(pe, r, u2=1)
                            wait(pe, td, gt=1)
                            for a in range(2):
                                mm(bY[:, 256 + 8 * a:264 + 8 * a], U[:, 1 - p, a, :], wbc[:, BCP:BCP + 2 * NH],
                                   start=True, stop=True)
                            inc(mm(bY[0:BCP, 0:256], wbc[:, 0:BCP], u, start=True, stop=True), "pin")

                    def project_z():
                        if H:
                            u_ready()
                            wait(pe, r, yte=1)
                            for a in range(2):
                                ins = mm(bZ[:, 256 * a:256 * (a + 1)], U[:, 1 - p, a, :], wz[:, :], start=True, stop=True)
                            inc(ins, "pin")

                    def u_ready():
                        wait(pe, min(q, TILES - 1) if isinstance(i, int) else q, gelu=1)
                        wait(pe, r - 1, u2=1)

                    def turn_xs():
                        if G:
                            wait(pe, r, xs=1, conv=NCONV)
                            for a in range(2):
                                for c in range(2):
                                    ins = tr(bX[:, (2 * a + c) * P:(2 * a + c + 1) * P],
                                             CX[:, c, 2 * a:2 * a + 2, :].rearrange("p g t -> p (g t)"), ident[:, :])
                            inc(ins, "trx")

                    def grams():
                        if G:
                            wait(pe, r, dtc=1, xs=3, conv=NCONV)
                            for a in range(2):
                                for c in range(2):
                                    mm(bY[:, FC0 + NH * a:FC0 + NH * (a + 1)],
                                       CX[:, c, 2 * a:2 * a + 2, :].rearrange("p g t -> p (g t)"),
                                       fcT[:, c, :], start=(c == 0), stop=(c == 1))
                            for a in range(2):
                                ins = mm(bY[:, P * a:P * (a + 1)], BT[:, P * a:P * (a + 1)], CT[:, P * a:P * (a + 1)],
                                         start=True, stop=True)
                            inc(ins, "gram")

                    def decay_sums():
                        if G:
                            wait(pe, r, rf=2, rb=2, sz=1)
                            for a in range(2):
                                for n, (m, dec) in enumerate(((earlier, RF), (earlier, RF), (later, RB), (later, RB))):
                                    ins = mm(bZ[:, 256 * a:256 * (a + 1)], m[:, :],
                                             dec[:, n % 2, NH * a:NH * (a + 1), :].rearrange("p h t -> p (h t)"),
                                             start=(n == 0), stop=(n == 3))
                            inc(ins, "seg")

                    def mix():
                        if G:
                            wait(pe, r, mm=2, xse=1)
                            for a in range(2):
                                for h in range(NH):
                                    ins = mm(bX[:, 256 * a + HD * h:256 * a + HD * (h + 1)], Mt[:, a, h, :],
                                             XS[:, 256 * a + HD * h:256 * a + HD * (h + 1)], start=True, stop=True)
                            inc(ins, "yy")

                    def turn_y():
                        if G:
                            wait(pe, r, yn=2, ex=1)
                            for c in range(2):
                                for a in range(2):
                                    ins = tr(bZ[:, (2 * c + a) * P:(2 * c + a + 1) * P],
                                             XD[:, NH * a + 2 * c:NH * a + 2 * c + 2, :].rearrange("p a b -> p (a b)"),
                                             ident[:, :])
                            inc(ins, "tyn")

                    def project_out():
                        if G:
                            wait(pe, r, yte=1, g4=4, dd=1)
                            yt = YT[:, :, :].rearrange("p a b -> p (a b)")
                            for c in range(2):
                                ins = mm(bY[:, 0:256], owT[:, c, :], yt[:, 256 * c:256 * (c + 1)], start=(c == 0), stop=(c == 1))
                            inc(ins, "outp")

                    grams()
                    decay_sums()
                    route(0, 1)
                    bases(0, 0, 1)
                    turn_x()
                    turn_xs()
                    route(1, 2)
                    route(2, 3)
                    bases(1, 0, 1)
                    route(3, 4)
                    bases(0, 1, 2)
                    mix()
                    route(4, 5)
                    s4d(0)
                    route(5, 6)
                    bases(1, 1, 2)
                    project_x()
                    bases(0, 2, 3)
                    s4d(1)
                    bases(1, 2, 3)
                    turn_y()
                    bases(0, 3, 4)
                    route(6, 7)
                    project_out()
                    route(7, 8)
                    bases(0, 4, 5)
                    project_bc()
                    up(0)
                    bases(0, 5, 6)
                    bases(0, 6, 7)
                    up(1)
                    bases(1, 3, 4)
                    project_z()
                    turn_a(0)
                    bases(1, 4, 5)
                    bases(1, 5, 6)
                    turn_a(1)
                    turn_h()
                    bases(0, 7, 8)
                    bases(1, 6, 7)
                    bases(1, 7, 8)
                    lora(0)
                    turn_d(0)
                    lora(1)
                    down()
                    turn_d(1)

                UP, TURN_A, TURN_D = range(3)
                iterations(pe, body)


_INS = ["x", "cls_tok", "L0_tok_log_dt", "L0_tok_B", "L0_tok_inv_A_real", "L0_tok_A_imag", "L0_attn_w_down",
        "L0_attn_b_down", "L0_attn_w_up", "L0_attn_b_up", "L0_attn_gate1", "L0_attn_hy_in_w", "L0_attn_hy_conv_w",
        "L0_attn_hy_conv_b", "L0_attn_hy_dt_bias", "L0_attn_hy_A_log", "L0_attn_hy_D", "L0_attn_hy_fcD_w",
        "L0_attn_hy_norm_w", "L0_attn_hy_out_w", "L0_ffn_base_W", "L0_ffn_base_b", "L0_ffn_router_W",
        "L0_ffn_router_b", "L0_ffn_A", "L0_ffn_B", "L0_ffn_expert_map"]


def kernel(**inputs):
    import concourse.bacc as bacc
    from concourse.bass_utils import run_bass_kernel_spmd

    nc = bacc.Bacc("TRN2", target_bir_lowering=False, num_devices=1)
    arrays, args = {}, []
    for name in _INS:
        a = np.ascontiguousarray(inputs[name])
        if a.ndim == 0:
            a = a.reshape(1, 1)
        arrays[f"in_{name}"] = a
        args.append(nc.dram_tensor(f"in_{name}", a.shape, mybir.dt.from_np(a.dtype), kind="ExternalInput").ap())
    steps, rows, states, _ = inputs["x"].shape
    shape = (steps, rows + 1, inputs["cls_tok"].shape[-1])
    args.append(nc.dram_tensor("out_0", shape, F32, kind="ExternalOutput").ap())
    build(nc, *args, pairs=rows // 2)
    r = run_bass_kernel_spmd(nc, [arrays], core_ids=[0])
    return r.results[0]["out_0"]
```
